# Optimizing a Trainium2 kernel written in Bass

```python
import numpy as np
import jax
import jax.numpy as jnp

def _softmax(x, axis=-1):
    return jax.nn.softmax(x, axis=axis)

def _gelu(x):
    return jax.nn.gelu(x, approximate=True)

def _silu(x):
    return jax.nn.silu(x)

def _sigmoid(x):
    return jax.nn.sigmoid(x)

def _layernorm(x, axis=-1, eps=1e-05):
    m = jnp.mean(x, axis=axis, keepdims=True)
    v = jnp.var(x, axis=axis, keepdims=True)
    return (x - m) / jnp.sqrt(v + eps)

def _scatter_add(tgt, idx, src, axis=0):
    return tgt.at[idx].add(src)

def _segment_sum(src, seg, n):
    return jax.ops.segment_sum(src, seg, n)
kernel_name = 'mk_lm_tower_d2_tok_ids768_r4_55d991'

def setup_inputs(seed: int=0):
    np.random.seed(seed)
    _w = jnp.asarray

    def _rec_inputs():
        import jax
        import jax.numpy as jnp
        _rk = jax.random.key(seed)
        x = jax.random.randint(jax.random.fold_in(_rk, 1), (32, 128), 0, 30522, jnp.int32)
        mask_BS_i1_0 = jnp.where(jnp.ones((32, 128), dtype=bool), 1, 0).astype(jnp.int32)
        return (x, mask_BS_i1_0)
    x, mask_BS_i1_0 = _rec_inputs()

    def _L0_tok_setup():
        import jax, jax.numpy as jnp
        import numpy as np
        VOCAB = 30522
        HIDDEN = 192
        MAX_POS = 128
        TYPE_VOCAB = 2
        EPS = 1e-05
        key = jax.random.key(seed)
        k1, k2, k3, k4, k5 = jax.random.split(key, 5)
        B, S = (32, 128)
        return {'input_ids': jax.random.randint(k1, (B, S), 0, VOCAB, dtype=jnp.int64 if jax.config.jax_enable_x64 else jnp.int32), 'token_type_ids': jax.random.randint(k2, (B, S), 0, TYPE_VOCAB, dtype=jnp.int32), 'tok_w': jax.random.normal(k3, (VOCAB, HIDDEN), dtype=jnp.float32), 'pos_w': jax.random.normal(k4, (MAX_POS, HIDDEN), dtype=jnp.float32), 'type_w': jax.random.normal(k5, (TYPE_VOCAB, HIDDEN), dtype=jnp.float32), 'gamma': jnp.ones((HIDDEN,), dtype=jnp.float32), 'beta': jnp.zeros((HIDDEN,), dtype=jnp.float32)}
    _L0_tok_all = _L0_tok_setup()
    _L0_tok_in = {k: v for k, v in _L0_tok_all.items() if k in ('tok_w', 'pos_w', 'type_w', 'gamma', 'beta')}
    del _L0_tok_all

    def _L0_attn_setup():
        import jax, jax.numpy as jnp
        import numpy as np
        B, S, D, H = (8, 512, 192, 192)
        key = jax.random.key(seed)
        kx, kq, kk, kv = jax.random.split(key, 4)
        scale = 1.0 / np.sqrt(D)
        return {'x': jax.random.normal(kx, (B, S, D), dtype=jnp.float32), 'Wq': jax.random.normal(kq, (D, H), dtype=jnp.float32) * scale, 'Wk': jax.random.normal(kk, (D, H), dtype=jnp.float32) * scale, 'Wv': jax.random.normal(kv, (D, H), dtype=jnp.float32) * scale}
    _L0_attn_all = _L0_attn_setup()
    _L0_attn_in = {k: v for k, v in _L0_attn_all.items() if k in ('Wq', 'Wk', 'Wv')}
    del _L0_attn_all

    def _L0_ffn_setup():
        import jax, jax.numpy as jnp
        import numpy as np
        EPS_NORM = 1e-06
        EPS_LN = 1e-05

        def _layernorm(x, g, b):
            mu = jnp.mean(x, axis=-1, keepdims=True)
            var = jnp.mean(jnp.square(x - mu), axis=-1, keepdims=True)
            return (x - mu) * jax.lax.rsqrt(var + EPS_LN) * g + b
        key = jax.random.key(seed)
        ks = jax.random.split(key, 6)
        b, m, d = (8, 256, 192)
        n, p = (64, 16)
        h = 2 * d
        x = jax.random.normal(ks[0], (b, m, d), dtype=jnp.float32)
        phi = jax.random.normal(ks[1], (n, p, d), dtype=jnp.float32)
        ln_g = jnp.ones((n, d), dtype=jnp.float32)
        ln_b = jnp.zeros((n, d), dtype=jnp.float32)
        w1 = jax.random.normal(ks[2], (n, d, h), dtype=jnp.float32) * (1.0 / np.sqrt(d))
        b1 = jax.random.normal(ks[3], (n, h), dtype=jnp.float32) * 0.01
        w2 = jax.random.normal(ks[4], (n, h, d), dtype=jnp.float32) * (1.0 / np.sqrt(h))
        b2 = jax.random.normal(ks[5], (n, d), dtype=jnp.float32) * 0.01
        return {'x': x, 'phi': phi, 'ln_g': ln_g, 'ln_b': ln_b, 'w1': w1, 'b1': b1, 'w2': w2, 'b2': b2}
    _L0_ffn_all = _L0_ffn_setup()
    _L0_ffn_in = {k: v for k, v in _L0_ffn_all.items() if k in ('phi', 'ln_g', 'ln_b', 'w1', 'b1', 'w2', 'b2')}
    del _L0_ffn_all

    def _L1_attn_setup():
        import jax, jax.numpy as jnp
        import numpy as np
        HEADS = 12
        ROPE_THETA = 10000.0

        def _rope(t):
            B, H, N, D = t.shape
            inv_freq = 1.0 / ROPE_THETA ** (jnp.arange(0, D, 2, dtype=jnp.float32) / D)
            freqs = jnp.arange(N, dtype=jnp.float32)[:, None] * inv_freq[None, :]
            freqs = jnp.repeat(freqs, 2, axis=-1)
            cos, sin = (jnp.cos(freqs), jnp.sin(freqs))
            tp = t.reshape(B, H, N, D // 2, 2)
            rot = jnp.stack([-tp[..., 1], tp[..., 0]], axis=-1).reshape(B, H, N, D)
            return t * cos + rot * sin
        key = jax.random.key(seed)
        k1, k2, k3 = jax.random.split(key, 3)
        dim = 192
        x = jax.random.normal(k1, (2, 512, dim), dtype=jnp.float32)
        w_qkv = jax.random.normal(k2, (3 * dim, dim), dtype=jnp.float32) * dim ** (-0.5)
        w_proj = jax.random.normal(k3, (dim, dim), dtype=jnp.float32) * dim ** (-0.5)
        b_proj = jnp.zeros((dim,), dtype=jnp.float32)
        return {'x': x, 'w_qkv': w_qkv, 'w_proj': w_proj, 'b_proj': b_proj}
    _L1_attn_all = _L1_attn_setup()
    _L1_attn_in = {k: v for k, v in _L1_attn_all.items() if k in ('w_qkv', 'w_proj', 'b_proj')}
    del _L1_attn_all

    def _L1_ffn_setup():
        import jax, jax.numpy as jnp
        import numpy as np
        import math
        SQRT_2_OVER_PI = math.sqrt(2.0 / math.pi)

        def gelu(x):
            return x * 0.5 * (1.0 + jnp.tanh(SQRT_2_OVER_PI * (x + 0.044715 * x * x * x)))
        key = jax.random.key(seed)
        ks = jax.random.split(key, 6)
        B, S, D, M, E = (8, 128, 192, 768, 8)
        return {'x': jax.random.normal(ks[0], (B, S, D), dtype=jnp.float32), 'router_w': jax.random.normal(ks[1], (D, E), dtype=jnp.float32) * (1.0 / np.sqrt(D)), 'w1': jax.random.normal(ks[2], (E, D, M), dtype=jnp.float32) * (1.0 / np.sqrt(D)), 'b1': jax.random.normal(ks[3], (E, M), dtype=jnp.float32) * 1e-06, 'w2': jax.random.normal(ks[4], (E, M, D), dtype=jnp.float32) * (1.0 / np.sqrt(M)), 'b2': jax.random.normal(ks[5], (E, D), dtype=jnp.float32) * 1e-06}
    _L1_ffn_all = _L1_ffn_setup()
    _L1_ffn_in = {k: v for k, v in _L1_ffn_all.items() if k in ('router_w', 'w1', 'b1', 'w2', 'b2')}
    del _L1_ffn_all
    return {'x': x, 'mask_BS_i1_0': mask_BS_i1_0, 'L0_tok_tok_w': _L0_tok_in['tok_w'], 'L0_tok_pos_w': _L0_tok_in['pos_w'], 'L0_tok_type_w': _L0_tok_in['type_w'], 'L0_tok_gamma': _L0_tok_in['gamma'], 'L0_tok_beta': _L0_tok_in['beta'], 'L0_attn_Wq': _L0_attn_in['Wq'], 'L0_attn_Wk': _L0_attn_in['Wk'], 'L0_attn_Wv': _L0_attn_in['Wv'], 'L0_ffn_phi': _L0_ffn_in['phi'], 'L0_ffn_ln_g': _L0_ffn_in['ln_g'], 'L0_ffn_ln_b': _L0_ffn_in['ln_b'], 'L0_ffn_w1': _L0_ffn_in['w1'], 'L0_ffn_b1': _L0_ffn_in['b1'], 'L0_ffn_w2': _L0_ffn_in['w2'], 'L0_ffn_b2': _L0_ffn_in['b2'], 'L1_attn_w_qkv': _L1_attn_in['w_qkv'], 'L1_attn_w_proj': _L1_attn_in['w_proj'], 'L1_attn_b_proj': _L1_attn_in['b_proj'], 'L1_ffn_router_w': _L1_ffn_in['router_w'], 'L1_ffn_w1': _L1_ffn_in['w1'], 'L1_ffn_b1': _L1_ffn_in['b1'], 'L1_ffn_w2': _L1_ffn_in['w2'], 'L1_ffn_b2': _L1_ffn_in['b2']}

def reference(x, mask_BS_i1_0, L0_tok_tok_w, L0_tok_pos_w, L0_tok_type_w, L0_tok_gamma, L0_tok_beta, L0_attn_Wq, L0_attn_Wk, L0_attn_Wv, L0_ffn_phi, L0_ffn_ln_g, L0_ffn_ln_b, L0_ffn_w1, L0_ffn_b1, L0_ffn_w2, L0_ffn_b2, L1_attn_w_qkv, L1_attn_w_proj, L1_attn_b_proj, L1_ffn_router_w, L1_ffn_w1, L1_ffn_b1, L1_ffn_w2, L1_ffn_b2):
    import jax
    import jax.numpy as jnp

    def _L0_tok_ref(input_ids, token_type_ids, tok_w, pos_w, type_w, gamma, beta):
        import jax, jax.numpy as jnp
        import numpy as np
        VOCAB = 30522
        HIDDEN = 192
        MAX_POS = 128
        TYPE_VOCAB = 2
        EPS = 1e-05
        S = input_ids.shape[-1]
        emb = tok_w[input_ids] + pos_w[jnp.arange(S)] + type_w[token_type_ids]
        mean = jnp.mean(emb, axis=-1, keepdims=True)
        var = jnp.mean(jnp.square(emb - mean), axis=-1, keepdims=True)
        out = (emb - mean) * gamma * jax.lax.rsqrt(var + EPS) + beta
        return out

    def _L0_attn_ref(x, Wq, Wk, Wv):
        import jax, jax.numpy as jnp
        import numpy as np
        B, S, D, H = (8, 512, 192, 192)
        q = jnp.einsum('bsd,dh->bsh', x, Wq)
        k = jnp.einsum('bsd,dh->bsh', x, Wk)
        v = jnp.einsum('bsd,dh->bsh', x, Wv)
        S_len = x.shape[-2]
        scores = jnp.einsum('bqh,bkh->bqk', q, k)
        tril = jnp.tril(jnp.ones((S_len, S_len), dtype=jnp.float32))
        scores = jnp.where(tril == 0, -jnp.inf, scores)
        attn = jax.nn.softmax(scores, axis=-1)
        return jnp.einsum('bqk,bkh->bqh', attn, v)

    def _L0_ffn_ref(x, phi, ln_g, ln_b, w1, b1, w2, b2):
        import jax, jax.numpy as jnp
        import numpy as np
        EPS_NORM = 1e-06
        EPS_LN = 1e-05

        def _layernorm(x, g, b):
            mu = jnp.mean(x, axis=-1, keepdims=True)
            var = jnp.mean(jnp.square(x - mu), axis=-1, keepdims=True)
            return (x - mu) * jax.lax.rsqrt(var + EPS_LN) * g + b
        phi_n = phi * jax.lax.rsqrt(jnp.sum(jnp.square(phi), axis=0, keepdims=True) + EPS_NORM)
        bsz, m, d = x.shape
        n, p, _ = phi_n.shape
        logits = jnp.einsum('bmd,npd->bmnp', x, phi_n)
        D = jax.nn.softmax(logits, axis=1)
        C = jax.nn.softmax(logits.reshape(bsz, m, n * p), axis=-1)
        Xs = jnp.einsum('bmd,bmnp->bnpd', x, D)
        hdn = _layernorm(Xs, ln_g[:, None, :], ln_b[:, None, :])
        hdn = jnp.einsum('bnpd,ndh->bnph', hdn, w1) + b1[:, None, :]
        hdn = jax.nn.gelu(hdn, approximate=False)
        Ys = jnp.einsum('bnph,nhd->bnpd', hdn, w2) + b2[:, None, :]
        Ys = Ys.reshape(bsz, n * p, d)
        Y = jnp.einsum('bsd,bms->bmd', Ys, C)
        return Y

    def _L1_attn_ref(x, w_qkv, w_proj, b_proj):
        import jax, jax.numpy as jnp
        import numpy as np
        HEADS = 12
        ROPE_THETA = 10000.0

        def _rope(t):
            B, H, N, D = t.shape
            inv_freq = 1.0 / ROPE_THETA ** (jnp.arange(0, D, 2, dtype=jnp.float32) / D)
            freqs = jnp.arange(N, dtype=jnp.float32)[:, None] * inv_freq[None, :]
            freqs = jnp.repeat(freqs, 2, axis=-1)
            cos, sin = (jnp.cos(freqs), jnp.sin(freqs))
            tp = t.reshape(B, H, N, D // 2, 2)
            rot = jnp.stack([-tp[..., 1], tp[..., 0]], axis=-1).reshape(B, H, N, D)
            return t * cos + rot * sin
        B, N, C = x.shape
        H = HEADS
        d = C // H
        scale = d ** (-0.5)
        qkv = x @ w_qkv.T
        q, k, v = jnp.split(qkv, 3, axis=-1)

        def to_heads(t):
            return t.reshape(B, N, H, d).transpose(0, 2, 1, 3)
        q, k, v = map(to_heads, (q, k, v))
        q = _rope(q * scale)
        k = _rope(k)
        attn = jnp.einsum('bhid,bhjd->bhij', q, k)
        attn = jax.nn.softmax(attn, axis=-1)
        out = jnp.einsum('bhij,bhjd->bhid', attn, v)
        out = out.transpose(0, 2, 1, 3).reshape(B, N, C)
        return out @ w_proj.T + b_proj

    def _L1_ffn_ref(x, router_w, w1, b1, w2, b2):
        import jax, jax.numpy as jnp
        import numpy as np
        import math
        SQRT_2_OVER_PI = math.sqrt(2.0 / math.pi)

        def gelu(x):
            return x * 0.5 * (1.0 + jnp.tanh(SQRT_2_OVER_PI * (x + 0.044715 * x * x * x)))
        B, S, D = x.shape
        E = router_w.shape[1]
        T = B * S
        C = T // E
        xf = x.reshape(T, D)
        router_logits = xf @ router_w
        router_probs = jax.nn.softmax(router_logits, axis=-1)
        expert_gate = jnp.max(router_probs, axis=-1)
        expert_index = jnp.argmax(router_probs, axis=-1)
        expert_mask = jax.nn.one_hot(expert_index, E, dtype=xf.dtype)
        position_in_expert = (jnp.cumsum(expert_mask, axis=0) * expert_mask).astype(jnp.int32)
        expert_mask = expert_mask * (position_in_expert < C).astype(xf.dtype)
        expert_mask_flat = jnp.sum(expert_mask, axis=-1)
        expert_gate = expert_gate * expert_mask_flat
        combine = (expert_gate * expert_mask_flat)[:, None, None] * jax.nn.one_hot(expert_index, E, dtype=xf.dtype)[:, :, None] * jax.nn.one_hot(position_in_expert, C, dtype=xf.dtype)
        dispatch = (combine != 0).astype(xf.dtype)
        expert_inputs = jnp.einsum('td,tec->ecd', xf, dispatch)
        h = gelu(jnp.einsum('ecd,edm->ecm', expert_inputs, w1) + b1[:, None, :])
        expert_outputs = gelu(jnp.einsum('ecm,emd->ecd', h, w2) + b2[:, None, :])
        out = jnp.einsum('ecd,tec->td', expert_outputs, combine)
        return out.reshape(B, S, D)
    h = _L0_tok_ref(x, mask_BS_i1_0, L0_tok_tok_w, L0_tok_pos_w, L0_tok_type_w, L0_tok_gamma, L0_tok_beta)
    h = h + _L0_attn_ref(_layernorm(h, axis=-1), L0_attn_Wq, L0_attn_Wk, L0_attn_Wv)
    h = h + _L0_ffn_ref(_layernorm(h, axis=-1), L0_ffn_phi, L0_ffn_ln_g, L0_ffn_ln_b, L0_ffn_w1, L0_ffn_b1, L0_ffn_w2, L0_ffn_b2)
    h = h + _L1_attn_ref(_layernorm(h, axis=-1), L1_attn_w_qkv, L1_attn_w_proj, L1_attn_b_proj)
    h = h + _L1_ffn_ref(_layernorm(h, axis=-1), L1_ffn_router_w, L1_ffn_w1, L1_ffn_b1, L1_ffn_w2, L1_ffn_b2)
    return h

_drawn_inputs = setup_inputs


def setup_inputs(seed=0):
    import zlib

    import numpy as np

    out = dict(_drawn_inputs(seed))
    spreads = {'L0_tok_gamma': (1.0, 0.2),
     'L0_tok_beta': (0.0, 0.1),
     'L0_ffn_ln_g': (1.0, 0.6),
     'L0_ffn_ln_b': (0.0, 0.777),
     'L1_attn_b_proj': (0.0, 0.1)}
    factors = {'L0_ffn_b1': 42.037, 'L0_ffn_b2': 33.677, 'L1_ffn_b1': 64.0, 'L1_ffn_b2': 64.0}
    for name, (base, spread) in spreads.items():
        noise = np.random.default_rng([zlib.crc32(name.encode()), seed]).standard_normal(out[name].shape)
        drawn = base * np.exp(spread * noise) if base else spread * noise
        out[name] = jnp.asarray(drawn.astype(out[name].dtype))
    for name, factor in factors.items():
        out[name] = (out[name] * factor).astype(out[name].dtype)
    return out
```

```python
from contextlib import ExitStack

import concourse.bass as bass
from concourse import mybir
import numpy as np

F32 = mybir.dt.float32
F32R = mybir.dt.float32r
I32 = mybir.dt.int32
ALU = mybir.AluOpType
ACT = mybir.ActivationFunctionType
AX_X = mybir.AxisListType.X
ds = bass.ds

P = 128
NB = 32
D = 192
DR = D - P
GB = 4
NG = NB // GB
NE0 = 64
SP_E = 16
NS = NE0 * SP_E
NC = NS // P
H0 = 384
NH = 12
HD = D // NH
NE1 = 8
H1 = 768
CAP = P * NB // NE1
EPS = 1e-5
EPS_PHI = 1e-6
MASKED = -1e30


def group4(ap):
    return ap.rearrange("p (j n) -> p j n", j=GB)


def matmuls(pe, out, pairs, **kw):
    for n, (w, m) in enumerate(pairs):
        last = pe.matmul(out, w, m, start=n == 0, stop=n == len(pairs) - 1, **kw)
    return last


def wait_apart(eng, sem, value):
    eng.wait_ge(sem, value)
    eng.nop(nofuse=True)


class Steps:

    def __init__(self, eng, sem, turn=0, per_turn=0, start=0):
        self.eng, self.sem, self.base, self.n, self.per_turn = eng, sem, turn * per_turn + start, 0, per_turn

    def did(self, ins):
        ins.then_inc(self.sem, 1)
        self.n += 1
        return ins

    def wait(self):
        self.eng.wait_ge(self.sem, self.base + self.n)

    def wait_apart(self):
        wait_apart(self.eng, self.sem, self.base + self.n)

    def link(self, ins):
        self.did(ins)
        self.wait()

    def end(self):
        assert self.n == self.per_turn, (self.n, self.per_turn)


class Alloc:
    def __init__(self, nc, ctx):
        self.nc, self.ctx = nc, ctx

    def sb(self, name, shape, dt=F32):
        return self.ctx.enter_context(self.nc.sbuf_tensor(name, shape, dt))

    def sem(self, name):
        return self.ctx.enter_context(self.nc.semaphore(name))


def tower_program(nc, ins, out):
    with ExitStack() as ctx:
        al = Alloc(nc, ctx)
        T = {}
        T["ident"] = al.sb("ident", [P, P])
        T["h"] = al.sb("h_all", [P, NB, D])
        T["xT0"] = al.sb("xT0_all", [P, NB * P])
        T["xT1"] = al.sb("xT1_all", [DR, NB * P])
        T["phiT0"] = al.sb("phiT0", [P, NS])
        T["phiT1"] = al.sb("phiT1", [DR, NS])
        T["half"] = al.sb("minus_half", [P, GB])
        T["gate"] = al.sb("gate", [P, NB])
        T["from_i"] = al.sb("from_i", [P, NB], I32)
        T["minus_upper"] = al.sb("minus_upper", [P, 1])
        T["bank"] = ctx.enter_context(nc.psum_tensor("bank", [P, 8, 512], F32))
        T["xs"] = nc.dram_tensor("slot_inputs", [NS, NB, D], F32, kind="Internal").ap()
        T["ys"] = nc.dram_tensor("slot_outputs", [NS, NB, D], F32, kind="Internal").ap()
        T["xm"] = nc.dram_tensor("routed_inputs", [NE1 * CAP, D], F32, kind="Internal").ap()
        T["ym"] = nc.dram_tensor("routed_outputs", [NE1 * CAP, D], F32, kind="Internal").ap()
        with ExitStack() as c2:
            a2 = Alloc(nc, c2)
            for n, shape in (("M0", [P, D]), ("M1", [DR, D]), ("Wv0", [P, D]), ("Wv1", [DR, D]),
                             ("causal", [P, P]), ("pos0", [P, D]), ("dtype", [P, D]),
                             ("maskf", [P, NB]), ("gamma", [P, D]), ("beta", [P, D])):
                T[n] = a2.sb(n, shape)
            setup_phase(nc, ins, T)
            tower_phase(nc, T)
        expert_phase(nc, T, "e0", NE0, H0, T["xs"].rearrange("s b d -> (s b) d"),
                     T["ys"].rearrange("s b d -> (s b) d"), ins["w1_0"], ins["b1_0"], ins["w2_0"],
                     ins["b2_0"], ACT.Gelu, ln=(ins["ln_g"], ins["ln_b"]))
        combine_phase(nc, ins, T)
        routing_phase(nc, ins, T)
        expert_phase(nc, T, "e1", NE1, H1, T["xm"], T["ym"], ins["w1_1"], ins["b1_1"], ins["w2_1"],
                     ins["b2_1"], ACT.Gelu_apprx_tanh, gelu_out=True)
        gather_phase(nc, T, out)


def setup_phase(nc, ins, T):
    with ExitStack() as ctx:
        al = Alloc(nc, ctx)
        ids = al.sb("ids", [P, NB], I32)
        maski = al.sb("maski", [P, NB], I32)
        type0 = al.sb("type0", [P, D])
        type1 = al.sb("type1", [P, D])
        WqT0, WqT1 = al.sb("WqT0", [P, D]), al.sb("WqT1", [DR, D])
        WkT0, WkT1 = al.sb("WkT0", [P, D]), al.sb("WkT1", [DR, D])
        sq = al.sb("phi_sq", [P, NS])
        nrm = al.sb("phi_norm", [P, 2, SP_E])
        half16 = al.sb("minus_half16", [P, SP_E])
        loads = {n: al.sem(f"{n}_loaded") for n in ("ids", "qk", "phi", "emb", "rest")}
        gathered = al.sem("rows_gathered")
        qk_product = al.sem("qk_product")
        consts = al.sem("pool_constants")
        squares = al.sem("phi_sums")
        powed = al.sem("phi_rsqrt")
        vsteps = al.sem("setup_vector_steps")
        zero = al.sb("zero", [P, 4, D])
        zeroed = al.sem("zeroed")
        bank = T["bank"]
        with nc.Block() as block:

            @block.sync
            def _(sp):
                sp.dma_start(ids[:], ins["ids"]).then_inc(loads["ids"], 16)
                for t, n in ((WqT0, "WqT"), (WkT0, "WkT")):
                    sp.dma_start(t[:], ins[n][0:P]).then_inc(loads["qk"], 16)
                for t, n in ((WqT1, "WqT"), (WkT1, "WkT")):
                    sp.dma_start(t[:], ins[n][P:D]).then_inc(loads["qk"], 16)
                sp.dma_start(T["phiT0"][:], ins["phiT"][0:P]).then_inc(loads["phi"], 16)
                sp.dma_start(T["phiT1"][:], ins["phiT"][P:D]).then_inc(loads["phi"], 16)
                sp.dma_start(T["pos0"][:], ins["pos"]).then_inc(loads["emb"], 16)
                sp.dma_start(type0[:], ins["type"][0, :].partition_broadcast(P)).then_inc(loads["emb"], 16)
                sp.dma_start(type1[:], ins["type"][1, :].partition_broadcast(P)).then_inc(loads["emb"], 16)
                sp.dma_start(maski[:], ins["mask"]).then_inc(loads["emb"], 16)
                sp.dma_start(T["gamma"][:], ins["gamma"].partition_broadcast(P)).then_inc(loads["rest"], 16)
                sp.dma_start(T["beta"][:], ins["beta"].partition_broadcast(P)).then_inc(loads["rest"], 16)
                sp.dma_start(T["Wv0"][:], ins["Wv"][0:P]).then_inc(loads["rest"], 16)
                sp.dma_start(T["Wv1"][:], ins["Wv"][P:D]).then_inc(loads["rest"], 16)
                sp.wait_ge(zeroed, 1)
                xm = T["xm"].rearrange("(r p j) d -> r p j d", p=P, j=4)
                for r in range(NE1 * CAP // (4 * P)):
                    sp.dma_start(xm[r], zero[:]).then_inc(loads["rest"], 16)
                sp.wait_ge(loads["rest"], 16 * (4 + NE1 * CAP // (4 * P)))

            @block.gpsimd
            def _(pool):
                pool.memset(T["half"][:], -0.5).then_inc(consts, 1)
                pool.memset(half16[:], -0.5).then_inc(consts, 1)
                pool.wait_ge(loads["ids"], 16)
                for b in range(NB):
                    pool.indirect_dma_start(
                        out=T["h"][:, b, :], out_offset=None, in_=ins["tok"],
                        in_offset=bass.IndirectOffsetOnAxis(ap=ids[:, b:b + 1], axis=0),
                    ).then_inc(gathered, 16)
                pool.memset(T["ident"][:], 0.0).then_inc(consts, 1)
                pool.memset(T["causal"][:], 0.0).then_inc(consts, 1)
                pool.wait_ge(consts, 4)
                pool.affine_select(out=T["ident"][:], in_=T["ident"][:], compare_op=ALU.not_equal,
                                   fill=1.0, base=0, pattern=[[-1, P]],
                                   channel_multiplier=1).then_inc(consts, 1)
                pool.affine_select(out=T["causal"][:], in_=T["causal"][:], compare_op=ALU.is_ge,
                                   fill=MASKED, base=0, pattern=[[-1, P]],
                                   channel_multiplier=1).then_inc(consts, 1)
                for k, rows in ((0, P), (1, DR)):
                    pool.wait_ge(squares, k + 1)
                    pool.tensor_tensor(nrm[0:rows, k, :], nrm[0:rows, k, :], half16[0:rows, :],
                                       ALU.pow).then_inc(powed, 1)
                pool.wait_ge(gathered, 16 * NB)

            @block.vector
            def _(dve):
                st = Steps(dve, vsteps)
                dve.memset(zero[:], 0.0).then_inc(zeroed, 1)
                dve.memset(T["minus_upper"][0:DR, :], 0.0)
                dve.memset(T["minus_upper"][DR:P, :], -1.0)
                dve.wait_ge(loads["phi"], 32)
                for k, (t, rows) in enumerate(((T["phiT0"], P), (T["phiT1"], DR))):
                    st.link(dve.tensor_tensor(sq[0:rows, :], t[:], t[:], ALU.mult))
                    by_slot = sq[0:rows, :].rearrange("d (n p) -> d p n", p=SP_E)
                    st.link(dve.tensor_reduce(nrm[0:rows, k, :], by_slot, AX_X, ALU.add))
                    dve.tensor_scalar(nrm[0:rows, k, :], nrm[0:rows, k, :], EPS_PHI, None,
                                      ALU.add).then_inc(squares, 1)
                for k, (t, rows) in enumerate(((T["phiT0"], P), (T["phiT1"], DR))):
                    dve.wait_ge(powed, k + 1)
                    v = t[:].rearrange("d (n p) -> d n p", p=SP_E)
                    dve.tensor_tensor(v, v, nrm[0:rows, k:k + 1, :].broadcast_to([rows, NE0, SP_E]),
                                      ALU.mult)
                dve.wait_ge(loads["emb"], 64)
                dve.tensor_tensor(T["pos0"][:], T["pos0"][:], type0[:], ALU.add)
                dve.tensor_tensor(T["dtype"][:], type1[:], type0[:], ALU.subtract)
                dve.tensor_copy(T["maskf"][:], maski[:])

            @block.tensor
            def _(pe):
                pe.wait_ge(loads["qk"], 64)
                matmuls(pe, bank[:, 0, 0:D], [(WqT0[:, 0:P], WkT0[:]), (WqT1[:, 0:P], WkT1[:])])
                matmuls(pe, bank[0:DR, 1, 0:D], [(WqT0[:, P:D], WkT0[:]), (WqT1[:, P:D], WkT1[:])]
                        ).then_inc(qk_product, 1)

            @block.scalar
            def _(act):
                act.wait_ge(qk_product, 1)
                act.activation(T["M0"][:], bank[:, 0, 0:D], ACT.Copy)
                act.activation(T["M1"][:], bank[0:DR, 1, 0:D], ACT.Copy)


def tower_phase(nc, T):
    with ExitStack() as ctx:
        al = Alloc(nc, ctx)
        sb, sem = al.sb, al.sem
        bank, ident, h = T["bank"], T["ident"], T["h"]
        half = T["half"]
        typed = sb("typed", [P, GB, D])
        st6, mv = sb("ln_stats", [P, GB, 6]), sb("ln_mean_var", [P, GB, 2])
        ve, rs = sb("ln_var_eps", [P, GB]), sb("ln_rstd", [P, GB])
        xn = sb("xn", [P, GB, D])
        xT0, xT1 = sb("xT0", [P, GB * P]), sb("xT1", [DR, GB * P])
        qT0, qT1 = sb("qT0", [P, GB * P]), sb("qT1", [DR, GB * P])
        v = sb("v", [P, GB, D])
        sm, ex = sb("masked_scores", [P, GB, P]), sb("exp_scores", [P, GB, P])
        nmx, ssum, rinv = sb("neg_max", [P, GB]), sb("exp_sum", [P, GB]), sb("inv_sum", [P, GB])
        pT = sb("probsT", [P, GB * P])
        emb_added, emb_normed, h0_ready = sem("emb_added"), sem("emb_normed"), sem("h0_ready")
        var_ready, rstd_ready = sem("var_ready"), sem("rstd_ready")
        pool_steps, vec_steps = sem("attn_pool_steps"), sem("attn_vector_steps")
        xn_ready = sem("xn_ready")
        product = sem("attn_product")
        act_took, dve_took = sem("attn_act_took"), sem("attn_vector_took")
        score_max, exp_done = sem("score_max_ready"), sem("exp_done")
        PRIME = 2
        x3 = sb("x3", [P, GB, D + 2])
        ls = sb("logits_less_max", [P, 2, 512])
        mxc = sb("column_max", [P, 2, GB])
        disp = sb("dispatch_weights", [P, 2, 512])
        usum = sb("slot_sums", [P, 2, GB, 2])
        uss = sb("slot_square_sums", [P, 2, GB])
        usq = sb("slot_squares", [P, D])
        q1, q2, uve = sb("eps_s2", [P, GB]), sb("minus_mean2", [P, GB]), sb("slot_var", [P, GB])
        umean, urs = sb("slot_mean", [P, 2, GB]), sb("slot_rstd", [P, 2, GB])
        stage = sb("slot_stage", [P, 2, GB, D])
        x3_ready, x3T_product, x3T_act, x3T_dve = (sem("x3_ready"), sem("x3T_product"), sem("x3T_act"),
                                                   sem("x3T_vector"))
        logits, less_max, exped = sem("logits"), sem("less_max"), sem("exped")
        turned, disp_ready, slots_sum = sem("weights_turned"), sem("dispatch_ready"), sem("slots_summed")
        stats_ready, stage_ready, stored = sem("slot_stats_ready"), sem("stage_ready"), [sem("stored0"), sem("stored1")]
        svar_ready, srstd_ready = sem("slot_var_ready"), sem("slot_rstd_ready")
        x3_steps, slot_steps, act_steps = sem("x3_vector_steps"), sem("slot_vector_steps"), sem("slot_act_steps")
        U = [bank[:, 2:4, 0:2 * (D + 2)].rearrange("p k (j d) -> p k j d", j=2),
             bank[:, 4:6, 0:2 * (D + 2)].rearrange("p k (j d) -> p k j d", j=2)]

        def hg(g):
            return h[:, ds(g * GB, GB), :]

        def norm_stats(dve, steps, x, ready):
            for j in range(GB):
                steps.did(dve.bn_stats(st6[:, j, :], x[:, j, :]))
            steps.wait_apart()
            for j in range(GB):
                steps.did(dve.bn_aggr(mv[:, j, :], st6[:, j, :]))
            steps.wait()
            dve.tensor_scalar(ve[:], mv[:, :, 1], EPS, None, ALU.add).then_inc(ready, 1)

        with nc.Block() as block:

            @block.gpsimd
            def _(pool):
                pool.wait_ge(vec_steps, 1)

                def embed(g):
                    st = Steps(pool, pool_steps, g, 3)
                    st.link(pool.tensor_tensor(typed[:], T["dtype"][:].unsqueeze(1).broadcast_to([P, GB, D]),
                                               T["maskf"][:, ds(g * GB, GB)].unsqueeze(2)
                                               .broadcast_to([P, GB, D]), ALU.mult))
                    st.did(pool.tensor_tensor(typed[:], typed[:],
                                              T["pos0"][:].unsqueeze(1).broadcast_to([P, GB, D]), ALU.add))
                    st.wait_apart()
                    pool.tensor_tensor(hg(g), hg(g), typed[:], ALU.add).then_inc(emb_added, 1)
                    rsqrt(g, 0)
                    wait_apart(pool, emb_normed, g + 1)
                    st.did(pool.tensor_tensor(hg(g), hg(g),
                                              T["gamma"][:].unsqueeze(1).broadcast_to([P, GB, D]), ALU.mult))
                    st.wait_apart()
                    pool.tensor_tensor(hg(g), hg(g), T["beta"][:].unsqueeze(1).broadcast_to([P, GB, D]),
                                       ALU.add).then_inc(h0_ready, 1)
                    rsqrt(g, 1)
                    st.end()

                def rsqrt(g, k):
                    pool.wait_ge(var_ready, g * 3 + k + 1)
                    pool.tensor_tensor(rs[:], ve[:], half[:], ALU.pow).then_inc(rstd_ready, 1)

                with pool.Fori(0, NG) as g:
                    embed(g)
                    rsqrt(g, 2)
                    for c in range(NC):
                        pool.wait_ge(svar_ready, g * NC + c + 1)
                        pool.tensor_tensor(urs[:, c % 2, :], uve[:], half[:], ALU.pow).then_inc(srstd_ready, 1)

            @block.vector
            def _(dve):
                dve.memset(x3[:, :, D:D + 1], 1.0).then_inc(vec_steps, 1)
                dve.sem_inc(dve_took, PRIME)

                def attn(g):
                    st = Steps(dve, vec_steps, g, 4 * GB + 1, start=1)
                    wait_apart(dve, emb_added, g + 1)
                    norm_stats(dve, st, hg(g), var_ready)
                    dve.wait_ge(rstd_ready, g * 3 + 1)
                    for j in range(GB):
                        x = h[:, ds(g * GB + j, 1), :]
                        last = dve.tensor_scalar(x, x, mv[:, j, 0:1], rs[:, j:j + 1], ALU.subtract, ALU.mult)
                    last.then_inc(emb_normed, 1)
                    wait_apart(dve, h0_ready, g + 1)
                    norm_stats(dve, st, hg(g), var_ready)
                    dve.wait_ge(rstd_ready, g * 3 + 2)
                    for j in range(GB):
                        last = dve.tensor_scalar(xn[:, j, :], h[:, ds(g * GB + j, 1), :], mv[:, j, 0:1],
                                                 rs[:, j:j + 1], ALU.subtract, ALU.mult)
                    last.then_inc(xn_ready, 1)
                    dve.wait_ge(product, g * 10 + 2)
                    dve.tensor_copy(xT1[:], bank[0:DR, 7, :]).then_inc(dve_took, 1)
                    dve.wait_ge(product, g * 10 + 4)
                    dve.tensor_copy(qT1[:], bank[0:DR, 7, :]).then_inc(dve_took, 1)
                    dve.wait_ge(product, g * 10 + 7)
                    dve.tensor_tensor(sm[:], group4(bank[:, 6, :]),
                                      T["causal"][:].unsqueeze(1).broadcast_to([P, GB, P]),
                                      ALU.add).then_inc(dve_took, 1)
                    dve.wait_ge(dve_took, g * 5 + 3 + PRIME)
                    dve.tensor_reduce(nmx[:], sm[:], AX_X, ALU.max, negate=True).then_inc(score_max, 1)
                    dve.wait_ge(exp_done, g + 1)
                    st.link(dve.reciprocal(rinv[:], ssum[:]))
                    for k in range(2):
                        dve.wait_ge(product, g * 10 + 9 + k)
                        for j in (2 * k, 2 * k + 1):
                            x = h[:, ds(g * GB + j, 1), :].rearrange("p a d -> p (a d)")
                            o = bank[:, 6 + k, (j % 2) * D:(j % 2) * D + D]
                            last = dve.scalar_tensor_tensor(x, o, rinv[:, j:j + 1], x, ALU.mult, ALU.add)
                        last.then_inc(dve_took, 1)
                    st.end()

                def dispatch(g):
                    st = Steps(dve, x3_steps, g, 2 * GB + 1)
                    wait_apart(dve, dve_took, g * 5 + 5 + PRIME)
                    norm_stats(dve, st, hg(g), var_ready)
                    dve.wait_ge(rstd_ready, g * 3 + 3)
                    for j in range(GB):
                        last = dve.tensor_scalar(x3[:, j, 0:D], h[:, ds(g * GB + j, 1), :], mv[:, j, 0:1],
                                                 rs[:, j:j + 1], ALU.subtract, ALU.mult)
                    st.link(last)
                    dve.tensor_reduce(x3[:, :, D + 1:D + 2], x3[:, :, 0:D], AX_X, ALU.add).then_inc(x3_ready, 1)
                    dve.wait_ge(x3T_product, g * 2 + 2)
                    dve.tensor_copy(T["xT1"][:, ds(g * GB * P, GB * P)], bank[0:DR, 1, :]).then_inc(x3T_dve, 1)
                    st.end()

                    def less_max_of(c):
                        dve.wait_ge(logits, g * NC + c + 1)
                        sl.link(dve.tensor_reduce(mxc[:, c % 2, :], group4(bank[:, 0, :]), AX_X, ALU.max))
                        dve.wait_ge(turned, g * NC + c - 1 + PRIME)
                        dve.tensor_tensor(group4(ls[:, c % 2, :]), group4(bank[:, 0, :]),
                                          mxc[:, c % 2, :].unsqueeze(2).broadcast_to([P, GB, P]),
                                          ALU.subtract).then_inc(less_max, 1)

                    def slot_norm(c):
                        u = U[c % 2]
                        dve.wait_ge(stats_ready, g * NC + c + 1)
                        s, m = usum[:, c % 2, :, 0], usum[:, c % 2, :, 1]
                        sl.did(dve.scalar_tensor_tensor(q1[:], s, EPS, s, ALU.mult, ALU.mult))
                        sl.did(dve.scalar_tensor_tensor(q2[:], m, -1.0 / (D * D), m, ALU.mult, ALU.mult))
                        sl.did(dve.tensor_scalar(umean[:, c % 2, :], m, 1.0 / D, None, ALU.mult))
                        sl.wait()
                        sl.link(dve.tensor_tensor(q1[:], q1[:], q2[:], ALU.add))
                        dve.tensor_tensor(uve[:], q1[:], uss[:, c % 2, :], ALU.add).then_inc(svar_ready, 1)
                        dve.wait_ge(srstd_ready, g * NC + c + 1)
                        dve.wait_ge(stored[c % 2], 16 * (g * (NC // 2) + c // 2) + 1)
                        for j in range(GB):
                            last = dve.tensor_scalar(stage[:, c % 2, j, :], u[:, j // 2, j % 2, 0:D],
                                                     umean[:, c % 2, j:j + 1], urs[:, c % 2, j:j + 1],
                                                     ALU.subtract, ALU.mult)
                        last.then_inc(stage_ready, 1)

                    sl = Steps(dve, slot_steps, g, 5 * NC)
                    for s in range(NC + 3):
                        if s >= 3:
                            slot_norm(s - 3)
                        if s < NC:
                            less_max_of(s)
                    sl.end()

                with dve.Fori(0, NG) as g:
                    attn(g)
                    dispatch(g)

            @block.scalar
            def _(act):
                def attn(g):
                    def take(n, dst, src):
                        act.wait_ge(product, g * 10 + n)
                        act.activation(dst, src, ACT.Copy).then_inc(act_took, 1)

                    take(1, xT0[:], bank[:, 6, :])
                    take(3, qT0[:], bank[:, 6, :])
                    for k in range(2):
                        take(5 + k, v[:, 2 * k:2 * k + 2, :],
                             bank[:, 6 + k, 0:2 * D].rearrange("p (j d) -> p j d", j=2))
                    act.wait_ge(score_max, g + 1)
                    for j in range(GB):
                        last = act.activation(ex[:, j, :], sm[:, j, :], ACT.Exp, bias=nmx[:, j:j + 1],
                                              accum_out=ssum[:, j:j + 1])
                    last.then_inc(exp_done, 1)
                    take(8, pT[:], bank[:, 7, :])

                def dispatch(g):
                    act.wait_ge(x3T_product, g * 2 + 1)
                    act.activation(T["xT0"][:, ds(g * GB * P, GB * P)], bank[:, 0, :],
                                   ACT.Copy).then_inc(x3T_act, 1)
                    st = Steps(act, act_steps, g, GB * NC)

                    def exps(c):
                        act.wait_ge(less_max, g * NC + c + 1)
                        act.activation(ls[:, c % 2, :], ls[:, c % 2, :], ACT.Exp).then_inc(exped, 1)

                    def take_turned(c):
                        act.wait_ge(turned, g * NC + c + 1 + PRIME)
                        act.wait_ge(slots_sum, g * NC + c - 1 + PRIME)
                        act.activation(disp[:, c % 2, :], bank[:, 1, :], ACT.Copy).then_inc(disp_ready, 1)

                    def stats(c):
                        u = U[c % 2]
                        act.wait_ge(slots_sum, g * NC + c + 1 + PRIME)
                        for j in range(GB):
                            st.link(act.activation(usq[:], u[:, j // 2, j % 2, 0:D], ACT.Square,
                                                   scale=float(D) ** -0.5,
                                                   accum_out=uss[:, c % 2, j:j + 1]))
                        act.activation(usum[:, c % 2, :, :].rearrange("p (k j) s -> p k j s", k=2),
                                       u[:, :, :, D:D + 2], ACT.Copy).then_inc(stats_ready, 1)

                    for s in range(NC + 2):
                        if 1 <= s <= NC:
                            take_turned(s - 1)
                        if s < NC:
                            exps(s)
                        if s >= 2:
                            stats(s - 2)
                    st.end()

                with act.Fori(0, NG) as g:
                    attn(g)
                    dispatch(g)

            @block.tensor
            def _(pe):
                pe.sem_inc(turned, PRIME)
                pe.sem_inc(slots_sum, PRIME)

                def attn(g):
                    b6, b7 = bank[:, 6, :], bank[:, 7, :]

                    def done(ins):
                        ins.then_inc(product, 1)

                    pe.wait_ge(xn_ready, g + 1)
                    pe.wait_ge(dve_took, g * 5 + PRIME - 1)
                    for j in range(GB):
                        last = pe.transpose(b6[:, j * P:(j + 1) * P], xn[:, j, 0:P], ident[:])
                    done(last)
                    wait_apart(pe, dve_took, g * 5 + PRIME)
                    for j in range(GB):
                        last = pe.transpose(b7[0:DR, j * P:(j + 1) * P], xn[:, j, P:D], ident[:])
                    done(last)
                    pe.wait_ge(act_took, g * 5 + 1)
                    pe.wait_ge(dve_took, g * 5 + 1 + PRIME)
                    done(matmuls(pe, b6, [(T["M0"][:, 0:P], xT0[:]), (T["M1"][:, 0:P], xT1[:])]))
                    done(matmuls(pe, b7[0:DR, :], [(T["M0"][:, P:D], xT0[:]), (T["M1"][:, P:D], xT1[:])]))
                    for k in range(2):
                        if k == 0:
                            pe.wait_ge(act_took, g * 5 + 2)
                        else:
                            pe.wait_ge(dve_took, g * 5 + 2 + PRIME)
                        for j in (2 * k, 2 * k + 1):
                            last = matmuls(pe, bank[:, 6 + k, (j % 2) * D:(j % 2) * D + D],
                                           [(xT0[:, j * P:(j + 1) * P], T["Wv0"][:]),
                                            (xT1[:, j * P:(j + 1) * P], T["Wv1"][:])])
                        done(last)
                    pe.wait_ge(act_took, g * 5 + 3)
                    for j in range(GB):
                        c = slice(j * P, (j + 1) * P)
                        last = matmuls(pe, b6[:, c], [(qT0[:, c], xT0[:, c]), (qT1[:, c], xT1[:, c])])
                    done(last)
                    pe.wait_ge(act_took, g * 5 + 4)
                    pe.wait_ge(exp_done, g + 1)
                    for j in range(GB):
                        last = pe.transpose(b7[:, j * P:(j + 1) * P], ex[:, j, :], ident[:])
                    done(last)
                    for k in range(2):
                        pe.wait_ge(act_took, g * 5 + 5)
                        for j in (2 * k, 2 * k + 1):
                            last = pe.matmul(bank[:, 6 + k, (j % 2) * D:(j % 2) * D + D],
                                             pT[:, j * P:(j + 1) * P], v[:, j, :], start=True, stop=True)
                        done(last)

                def dispatch(g):
                    pe.wait_ge(x3_ready, g + 1)
                    for j in range(GB):
                        last = pe.transpose(bank[:, 0, j * P:(j + 1) * P], x3[:, j, 0:P], ident[:])
                    last.then_inc(x3T_product, 1)
                    for j in range(GB):
                        last = pe.transpose(bank[0:DR, 1, j * P:(j + 1) * P], x3[:, j, P:D], ident[:])
                    last.then_inc(x3T_product, 1)
                    pe.wait_ge(x3T_act, g + 1)
                    pe.wait_ge(x3T_dve, g + 1)

                    def logits_of(c):
                        if c >= 1:
                            pe.wait_ge(less_max, g * NC + c)
                        cs = slice(c * P, (c + 1) * P)
                        matmuls(pe, bank[:, 0, :], [
                            (T["phiT0"][:, cs], T["xT0"][:, ds(g * GB * P, GB * P)]),
                            (T["phiT1"][:, cs], T["xT1"][:, ds(g * GB * P, GB * P)])]).then_inc(logits, 1)

                    def turn(c):
                        pe.wait_ge(exped, g * NC + c + 1)
                        if c >= 1:
                            pe.wait_ge(disp_ready, g * NC + c)
                        for j in range(GB):
                            last = pe.transpose(bank[:, 1, j * P:(j + 1) * P],
                                                ls[:, c % 2, j * P:(j + 1) * P], ident[:])
                        last.then_inc(turned, 1)

                    def slot_sums(c):
                        pe.wait_ge(disp_ready, g * NC + c + 1)
                        if c >= 2:
                            pe.wait_ge(stage_ready, g * NC + c - 1)
                        for j in range(GB):
                            last = pe.matmul(U[c % 2][:, j // 2, j % 2, :], disp[:, c % 2, j * P:(j + 1) * P],
                                             x3[:, j, :], start=True, stop=True)
                        last.then_inc(slots_sum, 1)

                    for s in range(NC + 2):
                        if s < NC:
                            logits_of(s)
                        if 1 <= s <= NC:
                            turn(s - 1)
                        if s >= 2:
                            slot_sums(s - 2)

                with pe.Fori(0, NG) as g:
                    attn(g)
                    dispatch(g)

            @block.sync
            def _(sp):
                for k in range(2):
                    sp.sem_inc(stored[k], 1)
                with sp.Fori(0, NG) as g:
                    for c in range(NC):
                        sp.wait_ge(stage_ready, g * NC + c + 1)
                        sp.dma_start(T["xs"][c * P:(c + 1) * P, ds(g * GB, GB), :],
                                     stage[:, c % 2, :, :]).then_inc(stored[c % 2], 16)
                for k in range(2):
                    sp.wait_ge(stored[k], 16 * NG * NC // 2 + 1)


def past(eng, sem, value, wait=None):
    if not isinstance(value, int) or value > 0:
        if wait:
            wait(eng, sem, value)
        else:
            eng.wait_ge(sem, value)


def expert_phase(nc, T, name, n_exp, hid, src, dst, w1, b1T, w2, b2, act_fn, ln=None, gelu_out=False):
    MT = hid // P
    turns = n_exp // 2
    with ExitStack() as ctx:
        al = Alloc(nc, ctx)
        sb = lambda n, *a: al.sb(f"{name}_{n}", *a)
        sem = lambda n: al.sem(f"{name}_{n}")
        bank, ident = T["bank"], T["ident"]
        rows = [sb(f"rows{u}", [P, 4, D + DR]) for u in range(2)]
        w1raw = [sb(f"w1raw{u}", [P, 2, hid]) for u in range(2)]
        w1hi = [sb(f"w1hi{u}", [P, 2, hid], F32R) for u in range(2)]
        w1lo = [sb(f"w1lo{u}", [P, 2, hid], F32R) for u in range(2)]
        w2raw = [sb(f"w2raw{u}", [P, MT, D]) for u in range(2)]
        w2hi = [sb(f"w2hi{u}", [P, MT, D], F32R) for u in range(2)]
        w2lo = [sb(f"w2lo{u}", [P, MT, D], F32R) for u in range(2)]
        b1s = sb("b1", [P, MT, n_exp])
        b2s = [sb(f"b2_{u}", [P, D]) for u in range(2)]
        stage = [sb(f"stage{u}", [P, 4, D]) for u in range(2)]
        ysum = [sb(f"ysum{u}", [P, 4, D]) for u in range(2)] if gelu_out else stage
        xf = sb("x_full", [P, 2, 512])
        xhi = sb("x_hi", [P, 2, 512], F32R)
        xlo = sb("x_lo", [P, 512], F32R)
        xst = sb("x_hi_over_lo", [P, 512], F32R)
        hf = sb("h_full", [P, MT, 512])
        hhi = sb("h_hi", [P, MT, 512], F32R)
        hlo = sb("h_lo", [P, MT, 512], F32R)
        if ln is not None:
            lng, lnb = sb("ln_gain", [P, 2, n_exp]), sb("ln_shift", [P, 2, n_exp])
        rows_in, w_in = [sem(f"rows_in{u}") for u in range(2)], [sem(f"weights_in{u}") for u in range(2)]
        b2_in, stored = [sem(f"b2_in{u}") for u in range(2)], [sem(f"stored{u}") for u in range(2)]
        small_in = sem("small_in")
        doubled, w1_split, w2_split = sem("rows_doubled"), sem("w1_split"), sem("w2_split")
        pool_steps, act_steps, vec_steps = sem("pool_steps"), sem("act_steps"), sem("vector_steps")
        turned, w1_done, w2_done = sem("turned"), sem("w1_product"), sem("w2_product")
        x_taken, x_hi_ready, x_split = sem("x_taken"), sem("x_hi_ready"), sem("x_split")
        acted, h_split, y_added = sem("acted"), sem("h_split"), sem("y_added")
        lo_sign = T["minus_upper"]

        def f32(ap):
            return ap.bitcast(F32)

        def hbank(u, m):
            return bank[:, 2 + (u * MT + m) % 2, :]

        def each_pair(eng, turn):
            turn(0)
            with eng.Fori(1, turns - 1) as i:
                turn(i)
            turn(turns - 1)

        with nc.Block() as block:

            @block.sync
            def _(sp):
                sp.dma_start(b1s[:], b1T).then_inc(small_in, 16)
                if ln is not None:
                    for t, g in ((lng, ln[0]), (lnb, ln[1])):
                        sp.dma_start(t[:, 0, :], g[0:P]).then_inc(small_in, 16)
                        sp.dma_start(t[0:DR, 1, :], g[P:D]).then_inc(small_in, 16)
                        sp.dma_start(t[DR:P, 1, :], g[P:D]).then_inc(small_in, 16)

                def turn(i):
                    for u in range(2):
                        n = i * 2 + u
                        past(sp, turned, 2 * (n - 1))
                        sp.dma_start(rows[u][:, :, 0:D],
                                     src[ds(n * 512, 512), :].rearrange("(p j) d -> p j d", j=4)
                                     ).then_inc(rows_in[u], 16)
                        past(sp, w2_split, n - 1)
                        w = w1[ds(n, 1), :, :].rearrange("a d h -> (a d) h")
                        sp.dma_start(w1raw[u][:, 0, :], w[0:P]).then_inc(w_in[u], 16)
                        sp.dma_start(w1raw[u][0:DR, 1, :], w[P:D]).then_inc(w_in[u], 16)
                        sp.dma_start(w1raw[u][DR:P, 1, :], w[P:D]).then_inc(w_in[u], 16)
                        sp.dma_start(w2raw[u][:], w2[ds(n, 1), :, :].rearrange("a (k p) d -> p (a k) d", p=P)
                                     ).then_inc(w_in[u], 16)

                each_pair(sp, turn)

            @block.gpsimd
            def _(pool):
                def turn(i):
                    st = Steps(pool, pool_steps, i, 4)
                    for u in range(2):
                        n = i * 2 + u
                        wait_apart(pool, rows_in[u], 16 * (i + 1))
                        pool.tensor_copy(rows[u][:, :, D:D + DR], rows[u][:, :, P:D]).then_inc(doubled, 1)
                        pool.wait_ge(w_in[u], 64 * (i + 1))
                        past(pool, w1_done, (n - 1) * MT, wait_apart)
                        st.link(pool.tensor_copy(w1hi[u][:], w1raw[u][:]))
                        pool.tensor_tensor(w1lo[u][:], w1raw[u][:], f32(w1hi[u][:]),
                                           ALU.subtract).then_inc(w1_split, 1)
                        past(pool, w2_done, n - 1, wait_apart)
                        st.link(pool.tensor_copy(w2hi[u][:], w2raw[u][:]))
                        pool.tensor_tensor(w2lo[u][:], w2raw[u][:], f32(w2hi[u][:]),
                                           ALU.subtract).then_inc(w2_split, 1)
                    st.end()

                each_pair(pool, turn)

            @block.tensor
            def _(pe):
                def turn_rows(n, u):
                    pe.wait_ge(doubled, n + 1)
                    past(pe, x_taken, 2 * n)
                    for k in range(2):
                        for j in range(4):
                            last = pe.transpose(bank[:, k, j * P:(j + 1) * P],
                                                rows[u][:, j, k * P:(k + 1) * P], ident[:])
                        last.then_inc(turned, 1)

                def turn(i):
                    for u in range(2):
                        n = i * 2 + u
                        pe.wait_ge(x_split, n + 1)
                        pe.wait_ge(w1_split, n + 1)
                        for m in range(MT):
                            past(pe, acted, n * MT + m - 1)
                            ms = slice(m * P, (m + 1) * P)
                            matmuls(pe, hbank(u, m), [
                                (w1hi[u][:, 0, ms], xhi[:, 0, :]), (w1lo[u][:, 0, ms], xhi[:, 0, :]),
                                (w1hi[u][:, 0, ms], xlo[:]), (w1hi[u][:, 1, ms], xst[:]),
                                (w1lo[u][:, 1, ms], xst[:])]).then_inc(w1_done, 1)
                        if not isinstance(n, int) or n + 1 < n_exp:
                            turn_rows(n + 1, 1 - u)
                        pe.wait_ge(w2_split, n + 1)
                        past(pe, y_added, n)
                        for k in range(MT):
                            pe.wait_ge(h_split, n * MT + k + 1)
                            for j in range(4):
                                js = slice(j * P, (j + 1) * P)
                                for q, (a, b) in enumerate(((hhi, w2hi), (hhi, w2lo), (hlo, w2hi))):
                                    last = pe.matmul(bank[:, 4 + j, 0:D], a[:, k, js], b[u][:, k, :],
                                                     start=k == 0 and q == 0, stop=k == MT - 1 and q == 2)
                        last.then_inc(w2_done, 1)

                turn_rows(0, 0)
                each_pair(pe, turn)

            @block.scalar
            def _(act):
                def load_b2(n, u):
                    act.dma_start(b2s[u][:], b2[ds(n, 1), :].rearrange("a d -> (a d)").partition_broadcast(P)
                                  ).then_inc(b2_in[u], 16)

                def take_x(n, u):
                    for k in range(2):
                        act.wait_ge(turned, 2 * n + k + 1)
                        past(act, x_split, n)
                        if ln is None:
                            last = act.activation(xf[:, k, :], bank[:, k, :], ACT.Copy)
                        else:
                            last = act.activation(xf[:, k, :], bank[:, k, :], ACT.Identity,
                                                  bias=lnb[:, k, ds(n, 1)], scale=lng[:, k, ds(n, 1)])
                        last.then_inc(x_taken, 1)
                    act.wait_ge(x_taken, 2 * n + 2)
                    past(act, w1_done, n * MT)
                    for k in range(2):
                        act.activation(xhi[:, k, :], xf[:, k, :], ACT.Copy).then_inc(x_hi_ready, 1)

                def send(n, u):
                    act.wait_ge(y_added, n + 1)
                    if gelu_out:
                        i = n // 2 if isinstance(n, int) else None
                        past(act, stored[u], 16 * i if i is not None else (n - u) * 8)
                        act.activation(stage[u][:], ysum[u][:], act_fn).then_inc(act_steps, 1)
                        act.wait_ge(act_steps, n + 1)
                    act.dma_start(dst[ds(n * 512, 512), :].rearrange("(p j) d -> p j d", j=4),
                                  stage[u][:]).then_inc(stored[u], 16)

                def turn(i):
                    for u in range(2):
                        n = i * 2 + u
                        for m in range(MT):
                            act.wait_ge(w1_done, n * MT + m + 1)
                            past(act, h_split, (n - 1) * MT + m + 1)
                            act.activation(hf[:, m, :], hbank(u, m), act_fn,
                                           bias=b1s[:, m, ds(n, 1)]).then_inc(acted, 1)
                        if not isinstance(n, int) or n > 0:
                            send(n - 1, 1 - u)
                        if not isinstance(n, int) or n + 1 < n_exp:
                            load_b2(n + 1, 1 - u)
                            take_x(n + 1, 1 - u)

                load_b2(0, 0)
                act.wait_ge(small_in, 16 * (1 if ln is None else 7))
                take_x(0, 0)
                each_pair(act, turn)
                send(n_exp - 1, 1)
                for u in range(2):
                    act.wait_ge(stored[u], 16 * turns)

            @block.vector
            def _(dve):
                def split_x(n):
                    dve.wait_ge(x_hi_ready, 2 * n + 2)
                    dve.tensor_tensor(xlo[:], xf[:, 0, :], f32(xhi[:, 0, :]), ALU.subtract)
                    dve.scalar_tensor_tensor(xst[:], f32(xhi[:, 1, :]), lo_sign[:, 0:1], xf[:, 1, :],
                                             ALU.mult, ALU.add).then_inc(x_split, 1)

                def turn(i):
                    st = Steps(dve, vec_steps, i, 2 * MT)
                    for u in range(2):
                        n = i * 2 + u
                        for m in range(MT):
                            dve.wait_ge(acted, n * MT + m + 1)
                            if m == 0:
                                past(dve, w2_done, n)
                            st.link(dve.tensor_copy(hhi[:, m, :], hf[:, m, :]))
                            dve.tensor_tensor(hlo[:, m, :], hf[:, m, :], f32(hhi[:, m, :]),
                                              ALU.subtract).then_inc(h_split, 1)
                        if not isinstance(n, int) or n + 1 < n_exp:
                            split_x(n + 1)
                        dve.wait_ge(w2_done, n + 1)
                        dve.wait_ge(b2_in[u], 16 * (i + 1))
                        if gelu_out:
                            past(dve, act_steps, n - 1)
                        else:
                            past(dve, stored[u], 16 * i)
                        for j in range(4):
                            last = dve.tensor_tensor(ysum[u][:, j, :], bank[:, 4 + j, 0:D], b2s[u][:], ALU.add)
                        last.then_inc(y_added, 1)
                    st.end()

                split_x(0)
                each_pair(dve, turn)


def combine_phase(nc, ins, T):
    with ExitStack() as ctx:
        al = Alloc(nc, ctx)
        sb, sem = al.sb, al.sem
        bank, ident, h, half = T["bank"], T["ident"], T["h"], T["half"]
        xc0, xc1 = sb("xc0", [P, P]), sb("xc1", [DR, P])
        ysb = [sb(f"slot_out{u}", [P, NC, D]) for u in range(2)]
        nm, csum, cinv = sb("row_neg_max", [P, 1]), sb("row_sum", [P, 1]), sb("row_inv", [P, 1])
        comb, combT = sb("combine_exp", [P, NS]), sb("combineT", [P, NC, P])
        st6, mv = sb("ln4_stats", [P, 6]), sb("ln4_mean_var", [P, 2])
        ve, rs = sb("ln4_var_eps", [P, 1]), sb("ln4_rstd", [P, 1])
        x4 = sb("x4", [P, D])
        x4T0, x4T1 = sb("x4T0", [P, P]), sb("x4T1", [DR, P])
        W0, W1 = sb("Wqkv0", [P, 3 * D]), sb("Wqkv1", [DR, 3 * D])
        Wp0, Wp1 = sb("Wproj0", [P, D]), sb("Wproj1", [DR, D])
        bproj = sb("bproj", [P, D])
        cos, sin = sb("rope_cos", [P, 2 * D]), sb("rope_sin", [P, 2 * D])
        straight, crossed = sb("rope_straight", [P, 2 * D]), sb("rope_crossed", [P, 2 * D])
        qk = sb("qk_padded", [P, 2 * NH, 2 * HD])
        vs = sb("v_and_one", [P, NH, HD + 1])
        qT, kT = sb("headsT_q", [P, 3 * P]), sb("headsT_k", [P, 3 * P])
        nmx = sb("head_neg_max", [P, 4, 3])
        pr = sb("probs", [P, 4, 3, P])
        pT = sb("probsT1", [P, 4, 3, P])
        oinv, o = sb("head_inv", [P, NH]), sb("attn_out", [P, D])
        oT0, oT1 = sb("oT0", [P, P]), sb("oT1", [DR, P])
        hb = sb("h_and_bias", [P, D])
        loaded = sem("attn1_weights_in")
        ys_in = [sem(f"slot_out_in{u}") for u in range(2)]
        S = {n: sem(n) for n in (
            "xc_ready", "L_done", "L_max", "L_exp", "T_done", "T_act", "T_dve", "Y_done", "h2_ready",
            "ln_var", "ln_rstd", "x4_ready", "a_done", "a_took", "qk_done", "v_done", "rope_took", "rope_ready",
            "v_took", "c_done", "q_took", "k_took", "S_done", "S_took", "S_exp", "f_done", "f_act", "f_dve",
            "g_done", "o_ready", "h1_done", "oT_took", "p_done", "h3_ready", "hb_ready", "dve_c", "dve_a",
            "dve_o", "padded", "ones_set")}

        def at(b, n=1, k=0):
            return b * n + (k or n)

        def stages(t):
            if not isinstance(t, int):
                return t, t - 1, t - 2
            return tuple(b if 0 <= b < NB else None for b in (t, t - 1, t - 2))

        def each_turn(eng, turn):
            for t in range(4):
                turn(t, t % 2)
            with eng.Fori(2, NB // 2) as i:
                for u in range(2):
                    turn(i * 2 + u, u)
            for t in range(NB, NB + 2):
                turn(t, t % 2)

        def pT_flat(n):
            return pT[:].rearrange("p s g n -> p (s g n)")[:, n * 512:(n + 1) * 512]

        hb_of = lambda b: h[:, ds(b, 1), :].rearrange("p a d -> p (a d)")

        with nc.Block() as block:

            @block.sync
            def _(sp):
                for t, s in ((W0, ins["Wqkv"][0:P]), (W1, ins["Wqkv"][P:D]), (Wp0, ins["Wproj"][0:P]),
                             (Wp1, ins["Wproj"][P:D]), (bproj, ins["bproj"].partition_broadcast(P)),
                             (cos, ins["cos"]), (sin, ins["sin"])):
                    sp.dma_start(t[:], s).then_inc(loaded, 16)

                def turn(t, u):
                    b1, _, _ = stages(t)
                    if b1 is None:
                        return
                    past(sp, S["Y_done"], b1 - 1)
                    sp.dma_start(ysb[u][:], T["ys"][:, ds(b1, 1), :].rearrange("(c p) a d -> p c (a d)", p=P)
                                 ).then_inc(ys_in[u], 16)

                each_turn(sp, turn)

            @block.gpsimd
            def _(pool):
                pool.memset(qk[:], 0.0).then_inc(S["padded"], 1)
                pool.memset(vs[:], 1.0).then_inc(S["ones_set"], 1)
                pool.wait_ge(loaded, 7 * 16)

                def turn(t, u):
                    b1, b2, b3 = stages(t)
                    if b1 is not None:
                        past(pool, S["L_done"], 2 * b1)
                        pool.tensor_copy(xc0[:], T["xT0"][:, ds(b1 * P, P)]).then_inc(S["xc_ready"], 1)
                        pool.tensor_copy(xc1[:], T["xT1"][:, ds(b1 * P, P)]).then_inc(S["xc_ready"], 1)
                    if b2 is not None:
                        pool.wait_ge(S["ln_var"], at(b2))
                        pool.tensor_tensor(rs[:], ve[:], half[:, 0:1], ALU.pow).then_inc(S["ln_rstd"], 1)
                    if b3 is not None:
                        past(pool, S["h3_ready"], b3)
                        pool.tensor_tensor(hb[:], hb_of(b3), bproj[:], ALU.add).then_inc(S["hb_ready"], 1)

                each_turn(pool, turn)

            @block.tensor
            def _(pe):
                pe.wait_ge(loaded, 7 * 16)

                def turn(t, u):
                    b1, b2, b3 = stages(t)

                    def logits_half(k):
                        if k == 0:
                            pe.wait_ge(S["xc_ready"], at(b1, 2))
                            past(pe, S["h2_ready"], b1)
                        ks = slice(k * 512, (k + 1) * 512)
                        matmuls(pe, bank[:, k, :], [(xc0[:], T["phiT0"][:, ks]), (xc1[:], T["phiT1"][:, ks])]
                                ).then_inc(S["L_done"], 1)

                    def turn_probs():
                        pe.wait_ge(S["S_exp"], at(b3))
                        for n in range(3):
                            for m in range(4):
                                s, g = divmod(n * 4 + m, 3)
                                last = pe.transpose(bank[:, 4 + n, m * P:(m + 1) * P], pr[:, s, g, :], ident[:])
                            last.then_inc(S["f_done"], 1)

                    def heads_out():
                        pe.wait_ge(S["f_act"], at(b3, 2))
                        pe.wait_ge(S["f_dve"], at(b3))
                        for hd in range(NH):
                            last = pe.matmul(bank[:, 7, hd * (HD + 1):(hd + 1) * (HD + 1)], pT[:, hd % 4, hd // 4, :],
                                             vs[:, hd, :], start=True, stop=True)
                        last.then_inc(S["g_done"], 1)

                    def two_pieces(src, n, done):
                        pe.transpose(bank[:, n, 0:P], src[:, 0:P], ident[:])
                        pe.transpose(bank[0:DR, n, P:2 * P], src[:, P:D], ident[:]).then_inc(done, 1)

                    if b1 is not None:
                        logits_half(0)
                    if b3 is not None:
                        turn_probs()
                    if b1 is not None:
                        logits_half(1)
                    if b3 is not None:
                        heads_out()
                    if b2 is not None:
                        pe.wait_ge(S["x4_ready"], at(b2))
                        two_pieces(x4, 4, S["a_done"])
                    if b3 is not None:
                        pe.wait_ge(S["o_ready"], at(b3))
                        two_pieces(o, 5, S["h1_done"])
                    if b2 is not None:
                        pe.wait_ge(S["a_took"], at(b2, 2))
                        matmuls(pe, bank[:, 6, 0:2 * D], [(x4T0[:], W0[:, 0:2 * D]), (x4T1[:], W1[:, 0:2 * D])]
                                ).then_inc(S["qk_done"], 1)
                        matmuls(pe, bank[:, 7, 0:D], [(x4T0[:], W0[:, 2 * D:]), (x4T1[:], W1[:, 2 * D:])]
                                ).then_inc(S["v_done"], 1)
                    if b3 is not None:
                        pe.wait_ge(S["oT_took"], at(b3, 2))
                        if b2 is None:
                            past(pe, S["a_took"], 2 * NB)
                        matmuls(pe, bank[:, 4, 0:D], [(oT0[:], Wp0[:]), (oT1[:], Wp1[:])]
                                ).then_inc(S["p_done"], 1)
                    if b1 is not None:
                        pe.wait_ge(S["L_exp"], at(b1))
                        for k in range(2):
                            for m in range(4):
                                c = 4 * k + m
                                last = pe.transpose(bank[:, 2 + k, m * P:(m + 1) * P],
                                                    comb[:, c * P:(c + 1) * P], ident[:])
                            last.then_inc(S["T_done"], 1)
                    if b2 is not None:
                        pe.wait_ge(S["rope_ready"], at(b2))
                        for k in range(2):
                            for g in range(3):
                                last = pe.transpose(
                                    bank[:, 5 + k, g * P:(g + 1) * P],
                                    qk[:, k * NH + 4 * g:k * NH + 4 * g + 4, :].rearrange("p a d -> p (a d)"),
                                    ident[:])
                            last.then_inc(S["c_done"], 1)
                    if b1 is not None:
                        pe.wait_ge(S["T_act"], at(b1))
                        pe.wait_ge(S["T_dve"], at(b1))
                        pe.wait_ge(ys_in[u], ys_value(t))
                        matmuls(pe, bank[:, 0, 0:D], [(combT[:, c, :], ysb[u][:, c, :]) for c in range(NC)]
                                ).then_inc(S["Y_done"], 1)
                    if b2 is not None:
                        pe.wait_ge(S["q_took"], at(b2))
                        pe.wait_ge(S["k_took"], at(b2))
                        pe.wait_ge(S["v_took"], at(b2))
                        past(pe, S["h3_ready"], b2)
                        for g in range(3):
                            gs = slice(g * P, (g + 1) * P)
                            for s in range(4):
                                rows = slice(32 * s, 32 * s + HD)
                                last = pe.matmul(bank[:, 4 + s, gs], qT[rows, gs], kT[rows, gs],
                                                 start=True, stop=True)
                        last.then_inc(S["S_done"], 1)

                def ys_value(t):
                    return 16 * (t // 2 + 1) if isinstance(t, int) else (t - t_par[0]) * 8 + 16

                t_par = [0]

                def turn_with_parity(t, u):
                    t_par[0] = u
                    turn(t, u)

                each_turn(pe, turn_with_parity)

            @block.scalar
            def _(act):
                act.wait_ge(S["ones_set"], 1)

                def turn(t, u):
                    b1, b2, b3 = stages(t)

                    def pieces(n, d0, d1, done, took):
                        act.wait_ge(done, at(b_of))
                        act.activation(d0[:], bank[:, n, 0:P], ACT.Copy).then_inc(took, 1)
                        act.activation(d1[:], bank[0:DR, n, P:2 * P], ACT.Copy).then_inc(took, 1)

                    if b3 is not None:
                        for k, n in enumerate((0, 2)):
                            act.wait_ge(S["f_done"], at(b3, 3, n + 1))
                            past(act, S["g_done"], b3)
                            act.activation(pT_flat(n), bank[:, 4 + n, :], ACT.Copy).then_inc(S["f_act"], 1)
                    if b2 is not None:
                        b_of = b2
                        pieces(4, x4T0, x4T1, S["a_done"], S["a_took"])
                    if b3 is not None:
                        b_of = b3
                        pieces(5, oT0, oT1, S["h1_done"], S["oT_took"])
                    if b1 is not None:
                        act.wait_ge(S["L_max"], at(b1))
                        past(act, S["T_done"], 2 * b1)
                        act.activation(comb[:].rearrange("p (k n) -> p k n", k=2), bank[:, 0:2, :], ACT.Exp,
                                       bias=nm[:], accum_out=csum[:]).then_inc(S["L_exp"], 1)
                    if b2 is not None:
                        act.wait_ge(S["v_done"], at(b2))
                        past(act, S["g_done"], b2)
                        act.activation(vs[:, :, 0:HD], bank[:, 7, 0:D].rearrange("p (a d) -> p a d", d=HD),
                                       ACT.Copy).then_inc(S["v_took"], 1)
                    if b1 is not None:
                        act.wait_ge(S["T_done"], at(b1, 2, 1))
                        past(act, S["Y_done"], b1)
                        act.activation(combT[:, 0:4, :], group4(bank[:, 2, :]), ACT.Copy).then_inc(S["T_act"], 1)
                    if b2 is not None:
                        act.wait_ge(S["c_done"], at(b2, 2, 1))
                        past(act, S["S_done"], b2)
                        act.activation(qT[:], bank[:, 5, 0:3 * P], ACT.Copy).then_inc(S["q_took"], 1)
                        act.wait_ge(S["S_took"], at(b2))
                        act.activation(pr[:], pr[:], ACT.Exp).then_inc(S["S_exp"], 1)

                each_turn(act, turn)

            @block.vector
            def _(dve):
                dve.wait_ge(loaded, 7 * 16)
                dve.wait_ge(S["padded"], 1)

                def turn(t, u):
                    b1, b2, b3 = stages(t)
                    if b2 is not None:
                        x = hb_of(b2)
                        wait_apart(dve, S["h2_ready"], at(b2))
                        dve.bn_stats(st6[:], x).then_inc(S["dve_a"], 1)
                        wait_apart(dve, S["dve_a"], at(b2, 5, 1))
                        dve.bn_aggr(mv[:], st6[:]).then_inc(S["dve_a"], 1)
                        dve.wait_ge(S["dve_a"], at(b2, 5, 2))
                        dve.tensor_scalar(ve[:], mv[:, 1:2], EPS, None, ALU.add).then_inc(S["ln_var"], 1)
                    if b3 is not None:
                        dve.wait_ge(S["f_done"], at(b3, 3, 2))
                        past(dve, S["g_done"], b3)
                        dve.tensor_copy(pT_flat(1), bank[:, 5, :]).then_inc(S["f_dve"], 1)
                    if b2 is not None:
                        dve.wait_ge(S["ln_rstd"], at(b2))
                        past(dve, S["a_done"], b2)
                        dve.tensor_scalar(x4[:], x, mv[:, 0:1], rs[:], ALU.subtract, ALU.mult
                                          ).then_inc(S["x4_ready"], 1)
                    if b3 is not None:
                        heads = bank[:, 7, 0:NH * (HD + 1)].rearrange("p (a d) -> p a d", d=HD + 1)
                        dve.wait_ge(S["g_done"], at(b3))
                        dve.reciprocal(oinv[:], heads[:, :, HD]).then_inc(S["dve_o"], 1)
                        dve.wait_ge(S["dve_o"], at(b3))
                        past(dve, S["h1_done"], b3)
                        dve.tensor_tensor(o[:].rearrange("p (a d) -> p a d", d=HD), heads[:, :, 0:HD],
                                          oinv[:].unsqueeze(2).broadcast_to([P, NH, HD]), ALU.mult
                                          ).then_inc(S["o_ready"], 1)
                    if b1 is not None:
                        dve.wait_ge(S["L_done"], at(b1, 2))
                        past(dve, S["L_exp"], b1)
                        dve.tensor_reduce(nm[:], bank[:, 0:2, :].rearrange("p k n -> p (k n)"), AX_X, ALU.max,
                                          negate=True).then_inc(S["L_max"], 1)
                    if b2 is not None:
                        src = bank[:, 6, 0:2 * D]
                        pairs = src.rearrange("p (m two) -> p m two", two=2)
                        cp = crossed[:].rearrange("p (m two) -> p m two", two=2)
                        sp_ = sin[:].rearrange("p (m two) -> p m two", two=2)
                        dve.wait_ge(S["qk_done"], at(b2))
                        dve.tensor_tensor(straight[:], src, cos[:], ALU.mult).then_inc(S["dve_a"], 1)
                        dve.tensor_tensor(cp[:, :, 0:1], pairs[:, :, 1:2], sp_[:, :, 0:1], ALU.mult
                                          ).then_inc(S["dve_a"], 1)
                        dve.tensor_tensor(cp[:, :, 1:2], pairs[:, :, 0:1], sp_[:, :, 1:2], ALU.mult
                                          ).then_inc(S["dve_a"], 1)
                        dve.wait_ge(S["dve_a"], at(b2, 5, 5))
                        past(dve, S["c_done"], 2 * b2)
                        dve.tensor_tensor(qk[:, :, 0:HD], straight[:].rearrange("p (a d) -> p a d", d=HD),
                                          crossed[:].rearrange("p (a d) -> p a d", d=HD), ALU.add
                                          ).then_inc(S["rope_ready"], 1)
                    if b1 is not None:
                        dve.wait_ge(S["T_done"], at(b1, 2, 2))
                        past(dve, S["Y_done"], b1)
                        dve.tensor_copy(combT[:, 4:8, :], group4(bank[:, 3, :])).then_inc(S["T_dve"], 1)
                    if b3 is not None:
                        dve.wait_ge(S["p_done"], at(b3))
                        dve.wait_ge(S["hb_ready"], at(b3))
                        dve.tensor_tensor(hb_of(b3), bank[:, 4, 0:D], hb[:], ALU.add).then_inc(S["h3_ready"], 1)
                    if b2 is not None:
                        dve.wait_ge(S["c_done"], at(b2, 2, 2))
                        past(dve, S["S_done"], b2)
                        dve.tensor_copy(kT[:], bank[:, 6, 0:3 * P]).then_inc(S["k_took"], 1)
                    if b1 is not None:
                        dve.wait_ge(S["L_exp"], at(b1))
                        dve.reciprocal(cinv[:], csum[:]).then_inc(S["dve_c"], 1)
                        dve.wait_ge(S["dve_c"], at(b1))
                        dve.wait_ge(S["Y_done"], at(b1))
                        dve.scalar_tensor_tensor(hb_of(b1), bank[:, 0, 0:D], cinv[:, 0:1], hb_of(b1),
                                                 ALU.mult, ALU.add).then_inc(S["h2_ready"], 1)
                    if b2 is not None:
                        sc = bank[:, 4:8, 0:3 * P].rearrange("p s (g n) -> p s g n", g=3)
                        dve.wait_ge(S["S_done"], at(b2))
                        dve.tensor_reduce(nmx[:], sc, AX_X, ALU.max).then_inc(S["rope_took"], 1)
                        dve.wait_ge(S["rope_took"], at(b2))
                        past(dve, S["f_done"], 3 * b2)
                        for s in range(4):
                            last = dve.tensor_tensor(pr[:, s], sc[:, s],
                                                     nmx[:, s, :].unsqueeze(2).broadcast_to([P, 3, P]), ALU.subtract)
                        last.then_inc(S["S_took"], 1)

                each_turn(dve, turn)


def routing_phase(nc, ins, T):
    with ExitStack() as ctx:
        al = Alloc(nc, ctx)
        sb, sem = al.sb, al.sem
        bank, ident, h, half = T["bank"], T["ident"], T["h"], T["half"]
        st6, mv = sb("ln5_stats", [P, GB, 6]), sb("ln5_mean_var", [P, GB, 2])
        ve, rs = sb("ln5_var_eps", [P, GB]), sb("ln5_rstd", [P, GB])
        x5 = sb("x5_all", [P, NB, D])
        x5s = sb("x5_group", [P, GB, D])
        x5T0, x5T1 = sb("x5T0", [P, GB * P]), sb("x5T1", [DR, GB * P])
        rw0, rw1 = sb("router0", [P, NE1]), sb("router1", [DR, NE1])
        lg = sb("router_logits", [P, NB, NE1])
        rank, w, onehot = sb("rank", [P, NE1]), sb("ranked", [P, NB, NE1]), sb("onehot", [P, NB, NE1])
        lmax, first = sb("router_max", [P, NB]), sb("first", [P, NB])
        upto, ones = sb("upto", [P, P]), sb("ones", [P, P])
        pre = [sb(f"before{k}", [P, NB, NE1]) for k in range(2)]
        pos, kept = sb("position", [P, NB]), sb("kept", [P, NB])
        base, to_f, from_f = sb("expert_base", [P, NB]), sb("to_f", [P, NB]), sb("from_f", [P, NB])
        to_i = sb("to_i", [P, NB], I32)
        loaded, consts = sem("router_in"), sem("router_constants")
        steps, var, rstd = sem("router_steps"), sem("ln5_var"), sem("ln5_rstd_ready")
        ready, tproduct, took, ttook = sem("x5_ready"), sem("x5T_product"), sem("x5T_act"), sem("x5T_vector")
        lproduct, ltook = sem("router_product"), sem("router_took")
        chosen, counted, placed, scattered = sem("chosen"), sem("counted"), sem("placed"), sem("scattered")
        exped = sem("router_exp")
        lx, lsum = sb("router_exp_of", [P, NB, NE1]), sb("router_sum", [P, NB])
        bc = lambda t: t[:].unsqueeze(2).broadcast_to([P, NB, NE1])
        with nc.Block() as block:

            @block.sync
            def _(sp):
                sp.dma_start(rw0[:], ins["router"][0:P]).then_inc(loaded, 16)
                sp.dma_start(rw1[:], ins["router"][P:D]).then_inc(loaded, 16)
                sp.dma_start(rank[:], ins["rank"].partition_broadcast(P)).then_inc(loaded, 16)
                sp.wait_ge(loaded, 48)

            @block.gpsimd
            def _(pool):
                pool.memset(upto[:], 1.0).then_inc(consts, 1)
                pool.memset(ones[:], 1.0).then_inc(consts, 1)
                pool.wait_ge(consts, 2)
                pool.affine_select(out=upto[:], in_=upto[:], compare_op=ALU.is_ge, fill=0.0, base=0,
                                   pattern=[[1, P]], channel_multiplier=-1).then_inc(consts, 1)
                with pool.Fori(0, NG) as g:
                    pool.wait_ge(var, g + 1)
                    pool.tensor_tensor(rs[:], ve[:], half[:], ALU.pow).then_inc(rstd, 1)
                pool.wait_ge(placed, 1)
                for b in range(NB):
                    pool.indirect_dma_start(
                        out=T["xm"], out_offset=bass.IndirectOffsetOnAxis(ap=to_i[:, b:b + 1], axis=0),
                        in_=x5[:, b, :], in_offset=None, bounds_check=NE1 * CAP - 1, oob_is_err=False,
                    ).then_inc(scattered, 16)
                pool.wait_ge(scattered, 16 * NB)

            @block.vector
            def _(dve):
                with dve.Fori(0, NG) as g:
                    st = Steps(dve, steps, g, 2 * GB)
                    for j in range(GB):
                        st.did(dve.bn_stats(st6[:, j, :], h[:, ds(g * GB + j, 1), :]))
                    st.wait_apart()
                    for j in range(GB):
                        st.did(dve.bn_aggr(mv[:, j, :], st6[:, j, :]))
                    st.wait()
                    dve.tensor_scalar(ve[:], mv[:, :, 1], EPS, None, ALU.add).then_inc(var, 1)
                    dve.wait_ge(rstd, g + 1)
                    for j in range(GB):
                        last = dve.tensor_scalar(x5s[:, j, :], h[:, ds(g * GB + j, 1), :], mv[:, j, 0:1],
                                                 rs[:, j:j + 1], ALU.subtract, ALU.mult)
                    last.then_inc(ready, 1)
                    dve.wait_ge(tproduct, g * 2 + 2)
                    dve.tensor_copy(x5T1[:], bank[0:DR, 1, :]).then_inc(ttook, 1)
                    dve.wait_ge(ltook, g * 2 + 2)
                st = Steps(dve, steps, start=2 * GB * NG)
                dve.wait_ge(loaded, 48)
                st.link(dve.tensor_reduce(lmax[:], lg[:], AX_X, ALU.max))
                st.link(dve.tensor_tensor(w[:], lg[:], bc(lmax), ALU.is_equal))
                st.link(dve.tensor_tensor(w[:], w[:], rank[:].unsqueeze(1).broadcast_to([P, NB, NE1]), ALU.mult))
                st.link(dve.tensor_reduce(first[:], w[:], AX_X, ALU.max))
                dve.tensor_tensor(onehot[:], w[:], bc(first), ALU.is_equal).then_inc(chosen, 1)
                dve.tensor_tensor(lx[:], lg[:], bc(lmax), ALU.subtract).then_inc(chosen, 1)
                dve.wait_ge(exped, 1)
                st.link(dve.tensor_reduce(lsum[:], lx[:], AX_X, ALU.add))
                st.link(dve.reciprocal(lsum[:], lsum[:]))
                dve.wait_ge(counted, 1)
                tot = bank[:, 1, 0:NB * NE1].rearrange("p (b e) -> p b e", e=NE1)
                cum = bank[:, 0, 0:NB * NE1].rearrange("p (b e) -> p b e", e=NE1)
                st.did(dve.memset(pre[0][:, 0, :], 0.0))
                st.did(dve.tensor_copy(pre[0][:, 1:NB, :], tot[:, 0:NB - 1, :]))
                st.wait()
                a, k = 0, 1
                while k < NB:
                    st.did(dve.tensor_copy(pre[1 - a][:, 0:k, :], pre[a][:, 0:k, :]))
                    st.did(dve.tensor_tensor(pre[1 - a][:, k:NB, :], pre[a][:, k:NB, :], pre[a][:, 0:NB - k, :],
                                             ALU.add))
                    st.wait()
                    a, k = 1 - a, 2 * k
                st.link(dve.tensor_tensor(pre[a][:], pre[a][:], cum, ALU.add))
                st.link(dve.tensor_tensor(pre[a][:], pre[a][:], onehot[:], ALU.mult))
                st.link(dve.tensor_reduce(pos[:], pre[a][:], AX_X, ALU.add))
                st.did(dve.tensor_scalar(kept[:], pos[:], float(CAP), None, ALU.is_lt))
                st.did(dve.tensor_scalar(base[:], first[:], float(NE1), -float(CAP), ALU.subtract, ALU.mult))
                st.wait()
                st.link(dve.tensor_tensor(from_f[:], pos[:], kept[:], ALU.mult))
                st.link(dve.tensor_tensor(from_f[:], from_f[:], base[:], ALU.add))
                st.did(dve.tensor_copy(T["from_i"][:], from_f[:]))
                st.did(dve.tensor_scalar(to_f[:], kept[:], -1.0, -float(NE1 * CAP), ALU.add, ALU.mult))
                st.did(dve.tensor_tensor(T["gate"][:], lsum[:], kept[:], ALU.mult))
                st.wait()
                st.link(dve.tensor_tensor(to_f[:], to_f[:], from_f[:], ALU.add))
                dve.tensor_copy(to_i[:], to_f[:]).then_inc(placed, 1)

            @block.scalar
            def _(act):
                with act.Fori(0, NG) as g:
                    act.wait_ge(tproduct, g * 2 + 1)
                    act.activation(x5T0[:], bank[:, 0, :], ACT.Copy).then_inc(took, 1)
                    act.activation(x5[:, ds(g * GB, GB), :], x5s[:], ACT.Copy).then_inc(ltook, 1)
                    act.wait_ge(lproduct, g + 1)
                    act.activation(lg[:, ds(g * GB, GB), :],
                                   bank[:, 2, 0:GB * NE1].rearrange("p (j e) -> p j e", e=NE1),
                                   ACT.Copy).then_inc(ltook, 1)
                act.wait_ge(chosen, 2)
                act.activation(lx[:], lx[:], ACT.Exp).then_inc(exped, 1)

            @block.tensor
            def _(pe):
                pe.wait_ge(loaded, 48)
                with pe.Fori(0, NG) as g:
                    pe.wait_ge(ready, g + 1)
                    for k, rows in ((0, P), (1, DR)):
                        for j in range(GB):
                            last = pe.transpose(bank[0:rows, k, j * P:(j + 1) * P],
                                                x5s[:, j, k * P:k * P + rows], ident[:])
                        last.then_inc(tproduct, 1)
                    pe.wait_ge(took, g + 1)
                    pe.wait_ge(ttook, g + 1)
                    for j in range(GB):
                        js = slice(j * P, (j + 1) * P)
                        last = matmuls(pe, bank[:, 2, j * NE1:(j + 1) * NE1],
                                       [(x5T0[:, js], rw0[:]), (x5T1[:, js], rw1[:])])
                    last.then_inc(lproduct, 1)
                pe.wait_ge(consts, 3)
                pe.wait_ge(chosen, 1)
                flat = onehot[:].rearrange("p b e -> p (b e)")
                pe.matmul(bank[:, 0, 0:NB * NE1], upto[:], flat, start=True, stop=True)
                pe.matmul(bank[:, 1, 0:NB * NE1], ones[:], flat, start=True, stop=True).then_inc(counted, 1)


def gather_phase(nc, T, out):
    with ExitStack() as ctx:
        al = Alloc(nc, ctx)
        got = al.sb("gathered_rows", [P, NB, D])
        taken = [al.sem(f"row_gathered{half}") for half in range(2)]
        added, stored = al.sem("row_added"), al.sem("out_stored")
        h = T["h"]
        with nc.Block() as block:

            @block.gpsimd
            def _(pool):
                for b in range(NB):
                    pool.indirect_dma_start(
                        out=got[:, b, :], out_offset=None, in_=T["ym"],
                        in_offset=bass.IndirectOffsetOnAxis(ap=T["from_i"][:, b:b + 1], axis=0),
                    ).then_inc(taken[2 * b // NB], 16)

            @block.vector
            def _(dve):
                for b in range(NB):
                    dve.wait_ge(taken[2 * b // NB], 16 * NB // 2)
                    dve.scalar_tensor_tensor(h[:, b, :], got[:, b, :], T["gate"][:, b:b + 1], h[:, b, :],
                                             ALU.mult, ALU.add).then_inc(added, 1)

            @block.sync
            def _(sp):
                for g in range(NG):
                    sp.wait_ge(added, (g + 1) * GB)
                    sp.dma_start(out[g * GB:(g + 1) * GB].rearrange("b p d -> p b d"),
                                 h[:, g * GB:(g + 1) * GB, :]).then_inc(stored, 16)
                sp.wait_ge(stored, 16 * NG)


def hidden_bias(b):
    return np.ascontiguousarray(b.reshape(b.shape[0], -1, P).transpose(2, 1, 0))


def host_layout(inputs):
    a = {k: np.asarray(v) for k, v in inputs.items()}
    return {
        "ids": np.ascontiguousarray(a["x"].T), "mask": np.ascontiguousarray(a["mask_BS_i1_0"].T),
        "tok": a["L0_tok_tok_w"], "pos": a["L0_tok_pos_w"], "type": a["L0_tok_type_w"],
        "gamma": a["L0_tok_gamma"], "beta": a["L0_tok_beta"],
        "WqT": np.ascontiguousarray(a["L0_attn_Wq"].T), "WkT": np.ascontiguousarray(a["L0_attn_Wk"].T),
        "Wv": a["L0_attn_Wv"],
        "ln_g": np.ascontiguousarray(a["L0_ffn_ln_g"].T), "ln_b": np.ascontiguousarray(a["L0_ffn_ln_b"].T),
        "Wqkv": np.ascontiguousarray(a["L1_attn_w_qkv"].T), "Wproj": np.ascontiguousarray(a["L1_attn_w_proj"].T),
        "bproj": a["L1_attn_b_proj"], "router": a["L1_ffn_router_w"],
        "rank": np.arange(NE1, 0, -1, dtype=np.float32), **rope_tables(),
        "w1_0": a["L0_ffn_w1"], "w2_0": a["L0_ffn_w2"], "b2_0": a["L0_ffn_b2"],
        "b1_0": hidden_bias(a["L0_ffn_b1"]),
        "w1_1": a["L1_ffn_w1"], "w2_1": a["L1_ffn_w2"], "b2_1": a["L1_ffn_b2"],
        "b1_1": hidden_bias(a["L1_ffn_b1"]),
        "phiT": np.ascontiguousarray(a["L0_ffn_phi"].reshape(NS, D).T),
    }


def rope_tables():
    freq = 1.0 / np.float32(10000.0) ** (np.arange(0, HD, 2, dtype=np.float32) / np.float32(HD))
    angle = np.arange(P, dtype=np.float32)[:, None] * freq[None, :].astype(np.float32)
    cos = np.repeat(np.cos(angle), 2, axis=1)
    sin = np.stack([-np.sin(angle), np.sin(angle)], axis=-1).reshape(P, HD)
    q_and_k = lambda t: np.concatenate([np.tile(t, NH) * np.float32(HD ** -0.5), np.tile(t, NH)], axis=1)
    return {"cos": q_and_k(cos).astype(np.float32), "sin": q_and_k(sin).astype(np.float32)}


def kernel(**inputs):
    from concourse import bacc
    from concourse.bass_utils import run_bass_kernel_spmd

    nc = bacc.Bacc("TRN2", target_bir_lowering=False, num_devices=1)
    arrays = host_layout(inputs)
    ins = {n: nc.dram_tensor(f"in_{n}", v.shape, mybir.dt.from_np(v.dtype), kind="ExternalInput").ap()
           for n, v in arrays.items()}
    out = nc.dram_tensor("out", (NB, P, D), F32, kind="ExternalOutput").ap()
    tower_program(nc, ins, out)
    r = run_bass_kernel_spmd(nc, [{f"in_{n}": v for n, v in arrays.items()}], core_ids=[0])
    return r.results[0]["out"]
```

```python
from contextlib import ExitStack

import concourse.bass as bass
from concourse import mybir
import numpy as np

F32 = mybir.dt.float32
F32R = mybir.dt.float32r
I32 = mybir.dt.int32
ALU = mybir.AluOpType
ACT = mybir.ActivationFunctionType
AX_X = mybir.AxisListType.X
ds = bass.ds

P = 128
NB = 32
D = 192
DR = D - P
GB = 4
NG = NB // GB
NE0 = 64
SP_E = 16
NS = NE0 * SP_E
NC = NS // P
H0 = 384
NH = 12
HD = D // NH
NE1 = 8
H1 = 768
CAP = P * NB // NE1
EPS = 1e-5
EPS_PHI = 1e-6
MASKED = -1e30


def group4(ap):
    return ap.rearrange("p (j n) -> p j n", j=GB)


def matmuls(pe, out, pairs, **kw):
    for n, (w, m) in enumerate(pairs):
        last = pe.matmul(out, w, m, start=n == 0, stop=n == len(pairs) - 1, **kw)
    return last


def wait_apart(eng, sem, value):
    eng.wait_ge(sem, value)
    eng.nop(nofuse=True)


class Steps:

    def __init__(self, eng, sem, turn=0, per_turn=0, start=0):
        self.eng, self.sem, self.base, self.n, self.per_turn = eng, sem, turn * per_turn + start, 0, per_turn

    def did(self, ins):
        ins.then_inc(self.sem, 1)
        self.n += 1
        return ins

    def wait(self):
        self.eng.wait_ge(self.sem, self.base + self.n)

    def wait_apart(self):
        wait_apart(self.eng, self.sem, self.base + self.n)

    def link(self, ins):
        self.did(ins)
        self.wait()

    def end(self):
        assert self.n == self.per_turn, (self.n, self.per_turn)


class Alloc:
    def __init__(self, nc, ctx):
        self.nc, self.ctx, self.sems = nc, ctx, []

    def sb(self, name, shape, dt=F32):
        return self.ctx.enter_context(self.nc.sbuf_tensor(name, shape, dt))

    def sem(self, name):
        self.sems.append(self.nc.alloc_semaphore(name))
        return self.sems[-1]

    def free_sems(self):
        self.nc.clear_and_free_semaphores(self.sems)
        self.nc.all_engine_barrier()


def tower_program(nc, ins, out):
    with ExitStack() as ctx:
        al = Alloc(nc, ctx)
        T = {}
        T["ident"] = al.sb("ident", [P, P])
        T["h"] = al.sb("h_all", [P, NB, D])
        T["xT0"] = al.sb("xT0_all", [P, NB * P])
        T["xT1"] = al.sb("xT1_all", [DR, NB * P])
        T["phiT0"] = al.sb("phiT0", [P, NS])
        T["phiT1"] = al.sb("phiT1", [DR, NS])
        T["half"] = al.sb("minus_half", [P, GB])
        T["gate"] = al.sb("gate", [P, NB])
        T["from_i"] = al.sb("from_i", [P, NB], I32)
        T["minus_upper"] = al.sb("minus_upper", [P, 1])
        T["bank"] = ctx.enter_context(nc.psum_tensor("bank", [P, 8, 512], F32))
        T["xs"] = nc.dram_tensor("slot_inputs", [NS, NB, D], F32, kind="Internal").ap()
        T["ys"] = nc.dram_tensor("slot_outputs", [NS, NB, D], F32, kind="Internal").ap()
        T["xm"] = nc.dram_tensor("routed_inputs", [NE1 * CAP, D], F32, kind="Internal").ap()
        T["ym"] = nc.dram_tensor("routed_outputs", [NE1 * CAP, D], F32, kind="Internal").ap()
        with ExitStack() as c2:
            a2 = Alloc(nc, c2)
            for n, shape in (("M0", [P, D]), ("M1", [DR, D]), ("Wv0", [P, D]), ("Wv1", [DR, D]),
                             ("causal", [P, P]), ("pos0", [P, D]), ("dtype", [P, D]),
                             ("maskf", [P, NB]), ("gamma", [P, D]), ("beta", [P, D])):
                T[n] = a2.sb(n, shape)
            T["tok"], T["ids"] = ins["tok"], a2.sb("ids", [P, NB], I32)
            T["gathered"] = [a2.sem(f"rows_gathered{k}") for k in range(3)]
            setup_phase(nc, ins, T)
            tower_phase(nc, T)
        expert_phase(nc, T, "e0", NE0, H0, T["xs"].rearrange("s b d -> (s b) d"),
                     T["ys"].rearrange("s b d -> (s b) d"), ins["w1_0"], ins["b1_0"], ins["w2_0"],
                     ins["b2_0"], ACT.Gelu, ln=(ins["ln_g"], ins["ln_b"]))
        combine_phase(nc, ins, T)
        routing_phase(nc, ins, T)
        expert_phase(nc, T, "e1", NE1, H1, T["xm"], T["ym"], ins["w1_1"], ins["b1_1"], ins["w2_1"],
                     ins["b2_1"], ACT.Gelu_apprx_tanh, gelu_out=True)
        gather_phase(nc, T, out)


def setup_phase(nc, ins, T):
    with ExitStack() as ctx:
        al = Alloc(nc, ctx)
        ids, gathered = T["ids"], T["gathered"]
        maski = al.sb("maski", [P, NB], I32)
        type0 = al.sb("type0", [P, D])
        type1 = al.sb("type1", [P, D])
        WqT0, WqT1 = al.sb("WqT0", [P, D]), al.sb("WqT1", [DR, D])
        WkT0, WkT1 = al.sb("WkT0", [P, D]), al.sb("WkT1", [DR, D])
        sq = al.sb("phi_sq", [P, NS])
        nrm = al.sb("phi_norm", [P, 2, SP_E])
        half16 = al.sb("minus_half16", [P, SP_E])
        loads = {n: al.sem(f"{n}_loaded") for n in ("ids", "qk", "phi", "emb", "rest")}
        qk_product = al.sem("qk_product")
        consts = al.sem("pool_constants")
        squares = al.sem("phi_sums")
        powed = al.sem("phi_rsqrt")
        vsteps = al.sem("setup_vector_steps")
        zero = al.sb("zero", [P, 4, D])
        zeroed = al.sem("zeroed")
        bank = T["bank"]
        with nc.Block() as block:

            @block.sync
            def _(sp):
                sp.dma_start(ids[:], ins["ids"]).then_inc(loads["ids"], 16)
                for t, n in ((WqT0, "WqT"), (WkT0, "WkT")):
                    sp.dma_start(t[:], ins[n][0:P]).then_inc(loads["qk"], 16)
                for t, n in ((WqT1, "WqT"), (WkT1, "WkT")):
                    sp.dma_start(t[:], ins[n][P:D]).then_inc(loads["qk"], 16)
                sp.dma_start(T["phiT0"][:], ins["phiT"][0:P]).then_inc(loads["phi"], 16)
                sp.dma_start(T["phiT1"][:], ins["phiT"][P:D]).then_inc(loads["phi"], 16)
                sp.dma_start(T["pos0"][:], ins["pos"]).then_inc(loads["emb"], 16)
                sp.dma_start(type0[:], ins["type"][0, :].partition_broadcast(P)).then_inc(loads["emb"], 16)
                sp.dma_start(type1[:], ins["type"][1, :].partition_broadcast(P)).then_inc(loads["emb"], 16)
                sp.dma_start(maski[:], ins["mask"]).then_inc(loads["emb"], 16)
                sp.dma_start(T["gamma"][:], ins["gamma"].partition_broadcast(P)).then_inc(loads["rest"], 16)
                sp.dma_start(T["beta"][:], ins["beta"].partition_broadcast(P)).then_inc(loads["rest"], 16)
                sp.dma_start(T["Wv0"][:], ins["Wv"][0:P]).then_inc(loads["rest"], 16)
                sp.dma_start(T["Wv1"][:], ins["Wv"][P:D]).then_inc(loads["rest"], 16)
                sp.wait_ge(zeroed, 1)
                xm = T["xm"].rearrange("(r p j) d -> r p j d", p=P, j=4)
                for r in range(NE1 * CAP // (4 * P)):
                    sp.dma_start(xm[r], zero[:]).then_inc(loads["rest"], 16)
                sp.wait_ge(loads["rest"], 16 * (4 + NE1 * CAP // (4 * P)))

            @block.gpsimd
            def _(pool):
                pool.memset(T["half"][:], -0.5).then_inc(consts, 1)
                pool.memset(half16[:], -0.5).then_inc(consts, 1)
                pool.wait_ge(loads["ids"], 16)
                for b in range(2 * GB):
                    pool.indirect_dma_start(
                        out=T["h"][:, b, :], out_offset=None, in_=ins["tok"],
                        in_offset=bass.IndirectOffsetOnAxis(ap=ids[:, b:b + 1], axis=0),
                    ).then_inc(gathered[b // GB], 16)
                pool.memset(T["ident"][:], 0.0).then_inc(consts, 1)
                pool.memset(T["causal"][:], 0.0).then_inc(consts, 1)
                pool.wait_ge(consts, 4)
                pool.affine_select(out=T["ident"][:], in_=T["ident"][:], compare_op=ALU.not_equal,
                                   fill=1.0, base=0, pattern=[[-1, P]],
                                   channel_multiplier=1).then_inc(consts, 1)
                pool.affine_select(out=T["causal"][:], in_=T["causal"][:], compare_op=ALU.is_ge,
                                   fill=MASKED, base=0, pattern=[[-1, P]],
                                   channel_multiplier=1).then_inc(consts, 1)
                for k, rows in ((0, P), (1, DR)):
                    pool.wait_ge(squares, k + 1)
                    pool.tensor_tensor(nrm[0:rows, k, :], nrm[0:rows, k, :], half16[0:rows, :],
                                       ALU.pow).then_inc(powed, 1)

            @block.vector
            def _(dve):
                st = Steps(dve, vsteps)
                dve.memset(zero[:], 0.0).then_inc(zeroed, 1)
                dve.memset(T["minus_upper"][0:DR, :], 0.0)
                dve.memset(T["minus_upper"][DR:P, :], -1.0)
                dve.wait_ge(loads["phi"], 32)
                for k, (t, rows) in enumerate(((T["phiT0"], P), (T["phiT1"], DR))):
                    st.link(dve.tensor_tensor(sq[0:rows, :], t[:], t[:], ALU.mult))
                    by_slot = sq[0:rows, :].rearrange("d (n p) -> d p n", p=SP_E)
                    st.link(dve.tensor_reduce(nrm[0:rows, k, :], by_slot, AX_X, ALU.add))
                    dve.tensor_scalar(nrm[0:rows, k, :], nrm[0:rows, k, :], EPS_PHI, None,
                                      ALU.add).then_inc(squares, 1)
                for k, (t, rows) in enumerate(((T["phiT0"], P), (T["phiT1"], DR))):
                    dve.wait_ge(powed, k + 1)
                    v = t[:].rearrange("d (n p) -> d n p", p=SP_E)
                    dve.tensor_tensor(v, v, nrm[0:rows, k:k + 1, :].broadcast_to([rows, NE0, SP_E]),
                                      ALU.mult)
                dve.wait_ge(loads["emb"], 64)
                dve.tensor_tensor(T["pos0"][:], T["pos0"][:], type0[:], ALU.add)
                dve.tensor_tensor(T["dtype"][:], type1[:], type0[:], ALU.subtract)
                dve.tensor_copy(T["maskf"][:], maski[:])

            @block.tensor
            def _(pe):
                pe.wait_ge(loads["qk"], 64)
                matmuls(pe, bank[:, 0, 0:D], [(WqT0[:, 0:P], WkT0[:]), (WqT1[:, 0:P], WkT1[:])])
                matmuls(pe, bank[0:DR, 1, 0:D], [(WqT0[:, P:D], WkT0[:]), (WqT1[:, P:D], WkT1[:])]
                        ).then_inc(qk_product, 1)

            @block.scalar
            def _(act):
                act.wait_ge(qk_product, 1)
                act.activation(T["M0"][:], bank[:, 0, 0:D], ACT.Copy)
                act.activation(T["M1"][:], bank[0:DR, 1, 0:D], ACT.Copy)


def tower_phase(nc, T):
    with ExitStack() as ctx:
        al = Alloc(nc, ctx)
        sb, sem = al.sb, al.sem
        bank, ident, h = T["bank"], T["ident"], T["h"]
        half = T["half"]
        typed = sb("typed", [P, GB, D])
        st6, mv = sb("ln_stats", [P, GB, 6]), sb("ln_mean_var", [P, GB, 2])
        ve, rs = sb("ln_var_eps", [P, GB]), sb("ln_rstd", [P, GB])
        xn = sb("xn", [P, GB, D])
        emb_added, h0_ready = sem("emb_added"), sem("h0_ready")
        evar, erstd = sem("emb_var_ready"), sem("emb_rstd_ready")
        pool_steps, emb_steps = sem("emb_pool_steps"), sem("emb_vector_steps")
        xn_ready = sem("xn_ready")
        xT0, xT1 = sb("xT0", [P, GB * P]), sb("xT1", [DR, GB * P])
        qT0, qT1 = sb("qT0", [P, GB * P]), sb("qT1", [DR, GB * P])
        v = sb("v", [P, GB, D])
        sm, ex = sb("masked_scores", [P, GB, P]), sb("exp_scores", [P, GB, P])
        nmx, ssum, rinv = sb("neg_max", [P, GB]), sb("exp_sum", [P, GB]), sb("inv_sum", [P, GB])
        pT = sb("probsT", [P, GB * P])
        product = sem("attn_product")
        act_took, dve_took = sem("attn_act_took"), sem("attn_vector_took")
        score_max, exp_done, attn_steps = sem("score_max_ready"), sem("exp_done"), sem("attn_vector_steps")
        PRIME = 2
        xst6, xmv = sb("x3_stats", [P, GB, 6]), sb("x3_mean_var", [P, GB, 2])
        xve, xrs = sb("x3_var_eps", [P, GB]), sb("x3_rstd", [P, GB])
        xvar, xrstd = sem("x3_var_ready"), sem("x3_rstd_ready")
        x3 = sb("x3", [P, GB, D + 2])
        ls = sb("slot_exp", [P, 2, 512])
        nmc = sb("column_neg_max", [P, 2, GB])
        disp = sb("dispatch_weights", [P, 2, 512])
        usum = sb("slot_sums", [P, 2, GB, 2])
        uss = sb("slot_square_sums", [P, 2, GB])
        usq = sb("slot_squares", [P, D])
        q1, q2, uve = sb("eps_s2", [P, 2, GB]), sb("minus_mean2", [P, 2, GB]), sb("slot_var", [P, 2, GB])
        umean, urs = sb("slot_mean", [P, 2, GB]), sb("slot_rstd", [P, 2, GB])
        stage = sb("slot_stage", [P, 2, GB, D])
        x3_ready, x3T_product, x3T_act = sem("x3_ready"), sem("x3T_product"), sem("x3T_act")
        logits, col_max, exped = sem("logits"), sem("col_max"), sem("exped")
        turned, disp_ready, slots_sum = sem("weights_turned"), sem("dispatch_ready"), sem("slots_summed")
        stats_ready, stage_ready, stored = sem("slot_stats_ready"), sem("stage_ready"), [sem("stored0"), sem("stored1")]
        svar_ready, srstd_ready = sem("slot_var_ready"), sem("slot_rstd_ready")
        x3_steps, slot_steps, act_steps = sem("x3_vector_steps"), sem("slot_vector_steps"), sem("slot_act_steps")
        U = [bank[:, 2:4, 0:2 * (D + 2)].rearrange("p k (j d) -> p k j d", j=2),
             bank[:, 4:6, 0:2 * (D + 2)].rearrange("p k (j d) -> p k j d", j=2)]

        def hg(g):
            return h[:, ds(g * GB, GB), :]

        def turns(eng, turn):
            turn(0, None, None)
            turn(1, 0, None)
            with eng.Fori(1, NG - 1) as t:
                turn(t + 1, t, t - 1)
            turn(None, NG - 1, NG - 2)
            turn(None, None, NG - 1)

        def norm_stats(dve, steps, x, st6, mv, ve, ready):
            for j in range(GB):
                steps.did(dve.bn_stats(st6[:, j, :], x[:, j, :]))
            steps.wait_apart()
            for j in range(GB):
                steps.did(dve.bn_aggr(mv[:, j, :], st6[:, j, :]))
            steps.wait()
            dve.tensor_scalar(ve[:], mv[:, :, 1], EPS, None, ALU.add).then_inc(ready, 1)

        with nc.Block() as block:

            @block.gpsimd
            def _(pool):
                tiles = lambda t: t.unsqueeze(2).broadcast_to([P, GB, D])
                columns = lambda t: t[:].unsqueeze(1).broadcast_to([P, GB, D])

                def embed(e, s):
                    if s == 0:
                        if isinstance(e, int):
                            pool.wait_ge(T["gathered"][e], 16 * GB)
                        past(pool, emb_added, e)
                        st = Steps(pool, pool_steps, e, 5)
                        st.link(pool.tensor_tensor(typed[:], T["dtype"][:].unsqueeze(1).broadcast_to([P, GB, D]),
                                                   T["maskf"][:, ds(e * GB, GB)].unsqueeze(2)
                                                   .broadcast_to([P, GB, D]), ALU.mult))
                        st.did(pool.tensor_tensor(typed[:], typed[:],
                                                  T["pos0"][:].unsqueeze(1).broadcast_to([P, GB, D]), ALU.add))
                        st.wait_apart()
                        pool.tensor_tensor(hg(e), hg(e), typed[:], ALU.add).then_inc(emb_added, 1)
                    if s == 1:
                        rsqrt(evar, e * 2 + 1, rs[:], ve[:], erstd)
                    if s == 2:
                        wait_apart(pool, erstd, e * 2 + 1)
                        st = Steps(pool, pool_steps, e, 5, start=2)
                        st.did(pool.tensor_tensor(hg(e), hg(e), tiles(mv[:, :, 0]), ALU.subtract))
                    if 3 <= s <= 5:
                        st = Steps(pool, pool_steps, e, 5, start=s)
                        st.wait_apart()
                        b, op = {3: (tiles(rs[:]), ALU.mult), 4: (columns(T["gamma"]), ALU.mult),
                                 5: (columns(T["beta"]), ALU.add)}[s]
                        last = pool.tensor_tensor(hg(e), hg(e), b, op)
                        if s < 5:
                            st.did(last)
                        else:
                            last.then_inc(h0_ready, 1)
                    if s == 6:
                        rsqrt(evar, e * 2 + 2, rs[:], ve[:], erstd)

                def rsqrt(ready, value, out, of, done):
                    pool.wait_ge(ready, value)
                    pool.tensor_tensor(out, of, half[:], ALU.pow).then_inc(done, 1)

                def turn(e, a, d):
                    for s in range(NC + 3):
                        if d is not None and s >= 3:
                            c = s - 3
                            rsqrt(svar_ready, d * NC + c + 1, urs[:, c % 2, :], uve[:, c % 2, :], srstd_ready)
                        if e is not None:
                            embed(e, s)
                        if a is not None and s == 7:
                            rsqrt(xvar, a + 1, xrs[:], xve[:], xrstd)
                    if e is not None and isinstance(e, int) and e == 0:
                        for b in range(2 * GB, NB):
                            pool.indirect_dma_start(
                                out=h[:, b, :], out_offset=None, in_=T["tok"],
                                in_offset=bass.IndirectOffsetOnAxis(ap=T["ids"][:, b:b + 1], axis=0),
                            ).then_inc(T["gathered"][2], 16)
                    if isinstance(e, int) and e == 1:
                        pool.wait_ge(T["gathered"][2], 16 * (NB - 2 * GB))

                turns(pool, turn)

            @block.vector
            def _(dve):
                dve.memset(x3[:, :, D:D + 1], 1.0)
                dve.sem_inc(dve_took, PRIME)

                def embed(e, s):
                    if s == 1:
                        wait_apart(dve, emb_added, e + 1)
                        norm_stats(dve, Steps(dve, emb_steps, e, 4 * GB), hg(e), st6, mv, ve, evar)
                    if s == 6:
                        wait_apart(dve, h0_ready, e + 1)
                        norm_stats(dve, Steps(dve, emb_steps, e, 4 * GB, start=2 * GB), hg(e), st6, mv, ve, evar)
                    if s == 8:
                        dve.wait_ge(erstd, e * 2 + 2)
                        past(dve, product, (e - 1) * 10 + 2)
                        for j in range(GB):
                            last = dve.tensor_scalar(xn[:, j, :], h[:, ds(e * GB + j, 1), :], mv[:, j, 0:1],
                                                     rs[:, j:j + 1], ALU.subtract, ALU.mult)
                        last.then_inc(xn_ready, 1)

                def take_xT(a):
                    dve.wait_ge(product, a * 10 + 2)
                    dve.tensor_copy(xT1[:], bank[0:DR, 7, :]).then_inc(dve_took, 1)

                def attn(a, s):
                    if s == 2:
                        dve.wait_ge(product, a * 10 + 7)
                        dve.tensor_tensor(sm[:], group4(bank[:, 6, :]),
                                          T["causal"][:].unsqueeze(1).broadcast_to([P, GB, P]),
                                          ALU.add).then_inc(dve_took, 1)
                        dve.wait_ge(dve_took, a * 4 + 2 + PRIME)
                        dve.tensor_reduce(nmx[:], sm[:], AX_X, ALU.max, negate=True).then_inc(score_max, 1)
                    if s == 5:
                        dve.wait_ge(exp_done, a + 1)
                        Steps(dve, attn_steps, a, 1).link(dve.reciprocal(rinv[:], ssum[:]))
                        for k in range(2):
                            dve.wait_ge(product, a * 10 + 9 + k)
                            for j in (2 * k, 2 * k + 1):
                                x = h[:, ds(a * GB + j, 1), :].rearrange("p a d -> p (a d)")
                                o = bank[:, 6 + k, (j % 2) * D:(j % 2) * D + D]
                                last = dve.scalar_tensor_tensor(x, o, rinv[:, j:j + 1], x, ALU.mult, ALU.add)
                            last.then_inc(dve_took, 1)
                    if s == 7:
                        wait_apart(dve, dve_took, a * 4 + 4 + PRIME)
                        norm_stats(dve, Steps(dve, x3_steps, a, 2 * GB + 1), hg(a), xst6, xmv, xve, xvar)
                    if s == 9:
                        dve.wait_ge(xrstd, a + 1)
                        past(dve, slots_sum, a * NC + PRIME if not isinstance(a, int) or a > 0 else 0)
                        for j in range(GB):
                            last = dve.tensor_scalar(x3[:, j, 0:D], h[:, ds(a * GB + j, 1), :], xmv[:, j, 0:1],
                                                     xrs[:, j:j + 1], ALU.subtract, ALU.mult)
                        Steps(dve, x3_steps, a, 2 * GB + 1, start=2 * GB).link(last)
                        dve.tensor_reduce(x3[:, :, D + 1:D + 2], x3[:, :, 0:D], AX_X, ALU.add).then_inc(x3_ready, 1)

                def column_max(d, c):
                    dve.wait_ge(logits, d * NC + c + 1)
                    dve.tensor_reduce(nmc[:, c % 2, :], group4(bank[:, 0, :]), AX_X, ALU.max,
                                      negate=True).then_inc(col_max, 1)

                def slot_var(d, c, sl):
                    dve.wait_ge(stats_ready, d * NC + c + 1)
                    s, m = usum[:, c % 2, :, 0], usum[:, c % 2, :, 1]
                    sl.did(dve.scalar_tensor_tensor(q1[:, c % 2, :], s, EPS, s, ALU.mult, ALU.mult))
                    sl.did(dve.scalar_tensor_tensor(q2[:, c % 2, :], m, -1.0 / (D * D), m, ALU.mult, ALU.mult))
                    sl.did(dve.tensor_scalar(umean[:, c % 2, :], m, 1.0 / D, None, ALU.mult))
                    sl.wait()
                    sl.link(dve.tensor_tensor(q1[:, c % 2, :], q1[:, c % 2, :], q2[:, c % 2, :], ALU.add))
                    dve.tensor_tensor(uve[:, c % 2, :], q1[:, c % 2, :], uss[:, c % 2, :], ALU.add).then_inc(svar_ready, 1)

                def slot_norm(d, c):
                    u = U[c % 2]
                    dve.wait_ge(srstd_ready, d * NC + c + 1)
                    dve.wait_ge(stored[c % 2], 16 * (d * (NC // 2) + c // 2) + 1)
                    for j in range(GB):
                        last = dve.tensor_scalar(stage[:, c % 2, j, :], u[:, j // 2, j % 2, 0:D],
                                                 umean[:, c % 2, j:j + 1], urs[:, c % 2, j:j + 1],
                                                 ALU.subtract, ALU.mult)
                    last.then_inc(stage_ready, 1)

                def turn(e, a, d):
                    if d is not None:
                        sl = Steps(dve, slot_steps, d, 4 * NC)
                    for s in range(NC + 2):
                        if d is not None and s < NC:
                            if s >= 4:
                                slot_norm(d, s - 4)
                            column_max(d, s)
                        if s == 9:
                            if e is not None:
                                take_xT(e)
                            if d is not None:
                                slot_norm(d, s - 4)
                            if a is not None:
                                attn(a, s)
                            if d is not None:
                                slot_var(d, NC - 2, sl)
                                slot_var(d, NC - 1, sl)
                                slot_norm(d, NC - 2)
                                slot_norm(d, NC - 1)
                        if d is not None and s == NC:
                            slot_norm(d, s - 4)
                        if d is not None and 3 <= s <= NC:
                            slot_var(d, s - 3, sl)
                        if a is not None and s != 9:
                            attn(a, s)
                        if e is not None:
                            embed(e, s)
                    if d is not None:
                        sl.end()

                turns(dve, turn)

            @block.scalar
            def _(act):
                def take(a, n, dst, src):
                    act.wait_ge(product, a * 10 + n)
                    act.activation(dst, src, ACT.Copy).then_inc(act_took, 1)

                def attn(a, s):
                    if s == 0:
                        for k in range(2):
                            take(a, 5 + k, v[:, 2 * k:2 * k + 2, :],
                                 bank[:, 6 + k, 0:2 * D].rearrange("p (j d) -> p j d", j=2))
                    if s == 3:
                        act.wait_ge(score_max, a + 1)
                        for j in range(GB):
                            last = act.activation(ex[:, j, :], sm[:, j, :], ACT.Exp, bias=nmx[:, j:j + 1],
                                                  accum_out=ssum[:, j:j + 1])
                        last.then_inc(exp_done, 1)
                    if s == 4:
                        take(a, 8, pT[:], bank[:, 7, :])

                def exps(d, c):
                    act.wait_ge(col_max, d * NC + c + 1)
                    act.wait_ge(turned, d * NC + c - 1 + PRIME)
                    for j in range(GB):
                        js = slice(j * P, (j + 1) * P)
                        last = act.activation(ls[:, c % 2, js], bank[:, 0, js], ACT.Exp, bias=nmc[:, c % 2, j:j + 1])
                    last.then_inc(exped, 1)

                def take_turned(d, c):
                    act.wait_ge(turned, d * NC + c + 1 + PRIME)
                    act.wait_ge(slots_sum, d * NC + c - 1 + PRIME)
                    act.activation(disp[:, c % 2, :], bank[:, 1, :], ACT.Copy).then_inc(disp_ready, 1)

                def stats(d, c, st):
                    u = U[c % 2]
                    act.wait_ge(slots_sum, d * NC + c + 1 + PRIME)
                    for j in range(GB):
                        st.link(act.activation(usq[:], u[:, j // 2, j % 2, 0:D], ACT.Square,
                                               scale=float(D) ** -0.5,
                                               accum_out=uss[:, c % 2, j:j + 1]))
                    act.activation(usum[:, c % 2, :, :].rearrange("p (k j) s -> p k j s", k=2),
                                   u[:, :, :, D:D + 2], ACT.Copy).then_inc(stats_ready, 1)

                def turn(e, a, d):
                    if d is not None:
                        st = Steps(act, act_steps, d, GB * NC)
                        for k, rows in ((0, P), (1, DR)):
                            act.wait_ge(x3T_product, d * 2 + k + 1)
                            act.activation(T[f"xT{k}"][:, ds(d * GB * P, GB * P)], bank[0:rows, k, :],
                                           ACT.Copy).then_inc(x3T_act, 1)
                    for s in range(NC + 2):
                        if a is not None and s == 0:
                            attn(a, s)
                        if d is not None:
                            if 1 <= s <= NC:
                                take_turned(d, s - 1)
                            if s < NC:
                                exps(d, s)
                        if e is not None and s == 9:
                            take(e, 1, xT0[:], bank[:, 6, :])
                        if d is not None and s >= 2:
                            stats(d, s - 2, st)
                        if e is not None and s == 9:
                            take(e, 3, qT0[:], bank[:, 6, :])
                            take(e, 4, qT1[:], bank[0:DR, 7, :])
                        if a is not None and s > 0:
                            attn(a, s)
                    if d is not None:
                        st.end()

                turns(act, turn)

            @block.tensor
            def _(pe):
                pe.sem_inc(turned, PRIME)
                pe.sem_inc(slots_sum, PRIME)
                b6, b7 = bank[:, 6, :], bank[:, 7, :]

                def done(ins):
                    ins.then_inc(product, 1)

                def turn_x(a):
                    pe.wait_ge(xn_ready, a + 1)
                    pe.wait_ge(dve_took, a * 4 + PRIME - 1)
                    for j in range(GB):
                        last = pe.transpose(b6[:, j * P:(j + 1) * P], xn[:, j, 0:P], ident[:])
                    done(last)
                    wait_apart(pe, dve_took, a * 4 + PRIME)
                    for j in range(GB):
                        last = pe.transpose(b7[0:DR, j * P:(j + 1) * P], xn[:, j, P:D], ident[:])
                    done(last)

                def queries(a):
                    pe.wait_ge(act_took, a * 6 + 1)
                    pe.wait_ge(dve_took, a * 4 + 1 + PRIME)
                    done(matmuls(pe, b6, [(T["M0"][:, 0:P], xT0[:]), (T["M1"][:, 0:P], xT1[:])]))
                    done(matmuls(pe, b7[0:DR, :], [(T["M0"][:, P:D], xT0[:]), (T["M1"][:, P:D], xT1[:])]))

                def attn(a, s):
                    if s == 0:
                        for k in range(2):
                            pe.wait_ge(act_took, a * 6 + 2 + k)
                            for j in (2 * k, 2 * k + 1):
                                last = matmuls(pe, bank[:, 6 + k, (j % 2) * D:(j % 2) * D + D],
                                               [(xT0[:, j * P:(j + 1) * P], T["Wv0"][:]),
                                                (xT1[:, j * P:(j + 1) * P], T["Wv1"][:])])
                            done(last)
                    if s == 2:
                        pe.wait_ge(act_took, a * 6 + 4)
                        for j in range(GB):
                            c = slice(j * P, (j + 1) * P)
                            last = matmuls(pe, b6[:, c], [(qT0[:, c], xT0[:, c]), (qT1[:, c], xT1[:, c])])
                        done(last)
                    if s == 4:
                        pe.wait_ge(act_took, a * 6 + 5)
                        pe.wait_ge(exp_done, a + 1)
                        for j in range(GB):
                            last = pe.transpose(b7[:, j * P:(j + 1) * P], ex[:, j, :], ident[:])
                        done(last)
                    if s == 5:
                        for k in range(2):
                            pe.wait_ge(act_took, a * 6 + 6)
                            for j in (2 * k, 2 * k + 1):
                                last = pe.matmul(bank[:, 6 + k, (j % 2) * D:(j % 2) * D + D],
                                                 pT[:, j * P:(j + 1) * P], v[:, j, :], start=True, stop=True)
                            done(last)

                def turn_x3(d):
                    pe.wait_ge(x3_ready, d + 1)
                    for j in range(GB):
                        last = pe.transpose(bank[:, 0, j * P:(j + 1) * P], x3[:, j, 0:P], ident[:])
                    last.then_inc(x3T_product, 1)
                    for j in range(GB):
                        last = pe.transpose(bank[0:DR, 1, j * P:(j + 1) * P], x3[:, j, P:D], ident[:])
                    last.then_inc(x3T_product, 1)

                def logits_of(d, c):
                    if c == 0:
                        pe.wait_ge(x3T_act, d * 2 + 2)
                    else:
                        pe.wait_ge(exped, d * NC + c)
                    cs = slice(c * P, (c + 1) * P)
                    matmuls(pe, bank[:, 0, :], [
                        (T["phiT0"][:, cs], T["xT0"][:, ds(d * GB * P, GB * P)]),
                        (T["phiT1"][:, cs], T["xT1"][:, ds(d * GB * P, GB * P)])]).then_inc(logits, 1)

                def turn_weights(d, c):
                    pe.wait_ge(exped, d * NC + c + 1)
                    if c >= 1:
                        pe.wait_ge(disp_ready, d * NC + c)
                    for j in range(GB):
                        last = pe.transpose(bank[:, 1, j * P:(j + 1) * P],
                                            ls[:, c % 2, j * P:(j + 1) * P], ident[:])
                    last.then_inc(turned, 1)

                def slot_sums(d, c):
                    pe.wait_ge(disp_ready, d * NC + c + 1)
                    if c >= 2:
                        pe.wait_ge(stage_ready, d * NC + c - 1)
                    for j in range(GB):
                        last = pe.matmul(U[c % 2][:, j // 2, j % 2, :], disp[:, c % 2, j * P:(j + 1) * P],
                                         x3[:, j, :], start=True, stop=True)
                    last.then_inc(slots_sum, 1)

                def turn(e, a, d):
                    if d is not None:
                        turn_x3(d)
                    for s in range(NC + 2):
                        if a is not None and s == 0:
                            attn(a, s)
                        if d is not None:
                            if s < NC:
                                logits_of(d, s)
                            if 1 <= s <= NC:
                                turn_weights(d, s - 1)
                        if e is not None and s == 9:
                            turn_x(e)
                        if d is not None and s >= 2:
                            slot_sums(d, s - 2)
                        if e is not None and s == 9:
                            queries(e)
                        if a is not None and s > 0:
                            attn(a, s)

                turns(pe, turn)

            @block.sync
            def _(sp):
                for k in range(2):
                    sp.sem_inc(stored[k], 1)
                with sp.Fori(0, NG) as g:
                    for c in range(NC):
                        sp.wait_ge(stage_ready, g * NC + c + 1)
                        sp.dma_start(T["xs"][c * P:(c + 1) * P, ds(g * GB, GB), :],
                                     stage[:, c % 2, :, :]).then_inc(stored[c % 2], 16)
                for k in range(2):
                    sp.wait_ge(stored[k], 16 * NG * NC // 2 + 1)
        al.free_sems()


def past(eng, sem, value, wait=None):
    if not isinstance(value, int) or value > 0:
        if wait:
            wait(eng, sem, value)
        else:
            eng.wait_ge(sem, value)


def expert_phase(nc, T, name, n_exp, hid, src, dst, w1, b1T, w2, b2, act_fn, ln=None, gelu_out=False):
    MT = hid // P
    turns = n_exp // 2
    with ExitStack() as ctx:
        al = Alloc(nc, ctx)
        sb = lambda n, *a: al.sb(f"{name}_{n}", *a)
        sem = lambda n: al.sem(f"{name}_{n}")
        bank, ident = T["bank"], T["ident"]
        rows = [sb(f"rows{u}", [P, 4, D + DR]) for u in range(2)]
        w1raw = [sb(f"w1raw{u}", [P, 2, hid]) for u in range(2)]
        w1hi = [sb(f"w1hi{u}", [P, 2, hid], F32R) for u in range(2)]
        w1lo = [sb(f"w1lo{u}", [P, 2, hid], F32R) for u in range(2)]
        w2raw = [sb(f"w2raw{u}", [P, MT, D]) for u in range(2)]
        w2p = [sb(f"w2_hi_lo{u}", [P, MT, 2, D], F32R) for u in range(2)]
        w2hi, w2lo = [w[:, :, 0, :] for w in w2p], [w[:, :, 1, :] for w in w2p]
        b1s = sb("b1", [P, MT, n_exp])
        b2s = [sb(f"b2_{u}", [P, D]) for u in range(2)]
        stage = [sb(f"stage{u}", [P, 4, D]) for u in range(2)]
        ysum = [sb(f"ysum{u}", [P, 4, D]) for u in range(2)] if gelu_out else stage
        xf = sb("x_full", [P, 2, 512])
        xhi = [sb(f"x_hi{u}", [P, 2, 512], F32R) for u in range(2)]
        xlo = [sb(f"x_lo{u}", [P, 512], F32R) for u in range(2)]
        xst = [sb(f"x_hi_over_lo{u}", [P, 512], F32R) for u in range(2)]
        hf = sb("h_full", [P, MT, 512])
        hhi = sb("h_hi", [P, MT, 512], F32R)
        hlo = sb("h_lo", [P, MT, 512], F32R)
        if ln is not None:
            lng, lnb = sb("ln_gain", [P, 2, n_exp]), sb("ln_shift", [P, 2, n_exp])
        rows_in, w_in = [sem(f"rows_in{u}") for u in range(2)], [sem(f"weights_in{u}") for u in range(2)]
        b2_in, stored = [sem(f"b2_in{u}") for u in range(2)], [sem(f"stored{u}") for u in range(2)]
        small_in = sem("small_in")
        w1_hi_ready, w2_hi_ready = sem("w1_hi_ready"), sem("w2_hi_ready")
        w1_split, w2_split = sem("w1_split"), sem("w2_split")
        act_steps, vec_steps = sem("act_steps"), sem("vector_steps")
        turned, w1_done, w2_done = sem("turned"), sem("w1_product"), sem("w2_product")
        x_taken, x_hi_ready, x_split = sem("x_taken"), sem("x_hi_ready"), sem("x_split")
        acted, h_split, y_added = sem("acted"), sem("h_split"), sem("y_added")
        h0_hi_ready, h0_split = sem("h0_hi_ready"), sem("h0_split")
        lo_sign = T["minus_upper"]

        def f32(ap):
            return ap.bitcast(F32)

        def hbank(u, m):
            return bank[:, 2 + (u * MT + m) % 2, :]

        def each_pair(eng, turn):
            turn(0)
            with eng.Fori(1, turns - 1) as i:
                turn(i)
            turn(turns - 1)

        with nc.Block() as block:

            @block.sync
            def _(sp):
                sp.dma_start(b1s[:], b1T).then_inc(small_in, 16)
                if ln is not None:
                    for t, g in ((lng, ln[0]), (lnb, ln[1])):
                        sp.dma_start(t[:, 0, :], g[0:P]).then_inc(small_in, 16)
                        sp.dma_start(t[0:DR, 1, :], g[P:D]).then_inc(small_in, 16)
                        sp.dma_start(t[DR:P, 1, :], g[P:D]).then_inc(small_in, 16)

                def turn(i):
                    for u in range(2):
                        n = i * 2 + u
                        past(sp, turned, 2 * (n - 1))
                        x = src[ds(n * 512, 512), :].rearrange("(p j) d -> p j d", j=4)
                        sp.dma_start(rows[u][:, :, 0:D], x).then_inc(rows_in[u], 16)
                        sp.dma_start(rows[u][:, :, D:D + DR], x[:, :, P:D]).then_inc(rows_in[u], 16)
                        past(sp, w2_split, n - 1)
                        w = w1[ds(n, 1), :, :].rearrange("a d h -> (a d) h")
                        sp.dma_start(w1raw[u][:, 0, :], w[0:P]).then_inc(w_in[u], 16)
                        sp.dma_start(w1raw[u][0:DR, 1, :], w[P:D]).then_inc(w_in[u], 16)
                        sp.dma_start(w1raw[u][DR:P, 1, :], w[P:D]).then_inc(w_in[u], 16)
                        sp.dma_start(w2raw[u][:], w2[ds(n, 1), :, :].rearrange("a (k p) d -> p (a k) d", p=P)
                                     ).then_inc(w_in[u], 16)

                each_pair(sp, turn)

            @block.gpsimd
            def _(pool):
                def weights_lo(n, u):
                    pool.wait_ge(w1_hi_ready, n + 1)
                    pool.tensor_tensor(w1lo[u][:], w1raw[u][:], f32(w1hi[u][:]),
                                       ALU.subtract).then_inc(w1_split, 1)
                    pool.wait_ge(w2_hi_ready, n + 1)
                    pool.tensor_tensor(w2lo[u], w2raw[u][:], f32(w2hi[u]), ALU.subtract).then_inc(w2_split, 1)

                def turn(i):
                    for u in range(2):
                        n = i * 2 + u
                        pool.wait_ge(h0_hi_ready, n + 1)
                        pool.tensor_tensor(hlo[:, 0, :], hf[:, 0, :], f32(hhi[:, 0, :]),
                                           ALU.subtract).then_inc(h0_split, 1)
                        if not isinstance(n, int) or n + 1 < n_exp:
                            weights_lo(n + 1, 1 - u)

                weights_lo(0, 0)
                each_pair(pool, turn)

            @block.tensor
            def _(pe):
                def turn_rows(n, u):
                    pe.wait_ge(rows_in[u], 32 * (n // 2 + 1) if isinstance(n, int) else (n - u) * 16 + 32)
                    past(pe, x_taken, 2 * n)
                    for k in range(2):
                        for j in range(4):
                            last = pe.transpose(bank[:, k, j * P:(j + 1) * P],
                                                rows[u][:, j, k * P:(k + 1) * P], ident[:])
                        last.then_inc(turned, 1)

                def turn(i):
                    for u in range(2):
                        n = i * 2 + u
                        pe.wait_ge(x_split, n + 1)
                        pe.wait_ge(w1_split, n + 1)
                        for m in range(MT):
                            past(pe, acted, n * MT + m - 1)
                            ms = slice(m * P, (m + 1) * P)
                            matmuls(pe, hbank(u, m), [
                                (w1hi[u][:, 0, ms], xhi[u][:, 0, :]), (w1lo[u][:, 0, ms], xhi[u][:, 0, :]),
                                (w1hi[u][:, 0, ms], xlo[u][:]), (w1hi[u][:, 1, ms], xst[u][:]),
                                (w1lo[u][:, 1, ms], xst[u][:])]).then_inc(w1_done, 1)
                        if not isinstance(n, int) or n + 2 < n_exp:
                            turn_rows(n + 2, u)
                        pe.wait_ge(w2_split, n + 1)
                        past(pe, y_added, n)
                        for k in range(MT):
                            if k == 0:
                                pe.wait_ge(h0_split, n + 1)
                            else:
                                pe.wait_ge(h_split, n * (MT - 1) + k)
                            for j in range(4):
                                js = slice(j * P, (j + 1) * P)
                                both = w2p[u][:, k, :, :].rearrange("p q d -> p (q d)")
                                if k == 0:
                                    pe.matmul(bank[:, 4 + j, 0:2 * D], hhi[:, k, js], both, start=True, stop=False)
                                last = pe.matmul(bank[:, 4 + j, 0:D], hlo[:, k, js], w2hi[u][:, k, :],
                                                 start=False, stop=False)
                                if k > 0:
                                    last = pe.matmul(bank[:, 4 + j, 0:2 * D], hhi[:, k, js], both,
                                                     start=False, stop=k == MT - 1)
                        last.then_inc(w2_done, 1)

                turn_rows(0, 0)
                turn_rows(1, 1)
                each_pair(pe, turn)

            @block.scalar
            def _(act):
                def load_b2(n, u):
                    act.dma_start(b2s[u][:], b2[ds(n, 1), :].rearrange("a d -> (a d)").partition_broadcast(P)
                                  ).then_inc(b2_in[u], 16)

                def weights_hi(n, u, i):
                    act.wait_ge(w_in[u], 64 * (i + 1))
                    past(act, w1_done, (n - 1) * MT)
                    act.activation(w1hi[u][:], w1raw[u][:], ACT.Copy).then_inc(w1_hi_ready, 1)
                    past(act, w2_done, n - 1)
                    act.activation(w2hi[u], w2raw[u][:], ACT.Copy).then_inc(w2_hi_ready, 1)

                def take_x(n, u):
                    for k in range(2):
                        act.wait_ge(turned, 2 * n + k + 1)
                        past(act, x_split, n)
                        if ln is None:
                            last = act.activation(xf[:, k, :], bank[:, k, :], ACT.Copy)
                        else:
                            last = act.activation(xf[:, k, :], bank[:, k, :], ACT.Identity,
                                                  bias=lnb[:, k, ds(n, 1)], scale=lng[:, k, ds(n, 1)])
                        last.then_inc(x_taken, 1)
                    act.wait_ge(x_taken, 2 * n + 2)
                    past(act, w1_done, (n - 1) * MT)
                    act.activation(xhi[u][:], xf[:], ACT.Copy).then_inc(x_hi_ready, 1)

                def send(n, u):
                    act.wait_ge(y_added, n + 1)
                    if gelu_out:
                        i = n // 2 if isinstance(n, int) else None
                        past(act, stored[u], 16 * i if i is not None else (n - u) * 8)
                        act.activation(stage[u][:], ysum[u][:], act_fn).then_inc(act_steps, 1)
                        act.wait_ge(act_steps, n + 1)
                    act.dma_start(dst[ds(n * 512, 512), :].rearrange("(p j) d -> p j d", j=4),
                                  stage[u][:]).then_inc(stored[u], 16)

                def turn(i):
                    for u in range(2):
                        n = i * 2 + u
                        if not isinstance(n, int) or n + 1 < n_exp:
                            weights_hi(n + 1, 1 - u, i + u)
                        for m in range(MT):
                            act.wait_ge(w1_done, n * MT + m + 1)
                            if m == 0:
                                past(act, h0_split, n)
                            else:
                                past(act, h_split, (n - 1) * (MT - 1) + m)
                            act.activation(hf[:, m, :], hbank(u, m), act_fn,
                                           bias=b1s[:, m, ds(n, 1)]).then_inc(acted, 1)
                        if not isinstance(n, int) or n > 0:
                            send(n - 1, 1 - u)
                        if not isinstance(n, int) or n + 1 < n_exp:
                            load_b2(n + 1, 1 - u)
                        if not isinstance(n, int) or n + 2 < n_exp:
                            take_x(n + 2, u)

                load_b2(0, 0)
                weights_hi(0, 0, 0)
                act.wait_ge(small_in, 16 * (1 if ln is None else 7))
                take_x(0, 0)
                take_x(1, 1)
                each_pair(act, turn)
                send(n_exp - 1, 1)
                for u in range(2):
                    act.wait_ge(stored[u], 16 * turns)

            @block.vector
            def _(dve):
                def split_x(n, u):
                    dve.wait_ge(x_hi_ready, n + 1)
                    dve.tensor_tensor(xlo[u][:], xf[:, 0, :], f32(xhi[u][:, 0, :]), ALU.subtract)
                    dve.scalar_tensor_tensor(xst[u][:], f32(xhi[u][:, 1, :]), lo_sign[:, 0:1], xf[:, 1, :],
                                             ALU.mult, ALU.add).then_inc(x_split, 1)

                def turn(i):
                    st = Steps(dve, vec_steps, i, 2 * MT)
                    for u in range(2):
                        n = i * 2 + u
                        for m in range(MT):
                            dve.wait_ge(acted, n * MT + m + 1)
                            if m == 0:
                                past(dve, w2_done, n)
                            if m == 0:
                                dve.tensor_copy(hhi[:, m, :], hf[:, m, :]).then_inc(h0_hi_ready, 1)
                                if not isinstance(n, int) or n + 1 < n_exp:
                                    split_x(n + 1, 1 - u)
                            else:
                                st.link(dve.tensor_copy(hhi[:, m, :], hf[:, m, :]))
                                dve.tensor_tensor(hlo[:, m, :], hf[:, m, :], f32(hhi[:, m, :]),
                                                  ALU.subtract).then_inc(h_split, 1)
                        dve.wait_ge(w2_done, n + 1)
                        dve.wait_ge(b2_in[u], 16 * (i + 1))
                        if gelu_out:
                            past(dve, act_steps, n - 1)
                        else:
                            past(dve, stored[u], 16 * i)
                        st.link(dve.tensor_tensor(ysum[u][:], bank[:, 4:8, 0:D],
                                                  b2s[u][:].unsqueeze(1).broadcast_to([P, 4, D]), ALU.add))
                        dve.tensor_tensor(ysum[u][:], ysum[u][:], bank[:, 4:8, D:2 * D],
                                          ALU.add).then_inc(y_added, 1)
                    st.end()

                split_x(0, 0)
                each_pair(dve, turn)


def combine_phase(nc, ins, T):
    with ExitStack() as ctx:
        al = Alloc(nc, ctx)
        sb, sem = al.sb, al.sem
        bank, ident, h, half = T["bank"], T["ident"], T["h"], T["half"]
        xc0, xc1 = sb("xc0", [P, P]), sb("xc1", [DR, P])
        ysb = [sb(f"slot_out{u}", [P, NC, D]) for u in range(2)]
        nm2 = sb("half_row_max", [P, 2])
        nm, csum, cinv = sb("row_neg_max", [P, 1]), sb("row_sum", [P, 1]), sb("row_inv", [P, 1])
        comb, combT = sb("combine_exp", [P, NS]), sb("combineT", [P, NC, P])
        st6, mv = sb("ln4_stats", [P, 6]), sb("ln4_mean_var", [P, 2])
        ve, rs = sb("ln4_var_eps", [P, 1]), sb("ln4_rstd", [P, 1])
        x4 = sb("x4", [P, D])
        x4T0, x4T1 = sb("x4T0", [P, P]), sb("x4T1", [DR, P])
        W0, W1 = sb("Wqkv0", [P, 3 * D]), sb("Wqkv1", [DR, 3 * D])
        Wp0, Wp1 = sb("Wproj0", [P, D]), sb("Wproj1", [DR, D])
        bproj = sb("bproj", [P, D])
        cos, sin = sb("rope_cos", [P, 2 * D]), sb("rope_sin", [P, 2 * D])
        straight, crossed = sb("rope_straight", [P, 2 * D]), sb("rope_crossed", [P, 2 * D])
        qk = sb("qk_padded", [P, 2 * NH, 2 * HD])
        vs = sb("v_and_one", [P, NH, HD + 1])
        qT, kT = sb("headsT_q", [P, 3 * P]), sb("headsT_k", [P, 3 * P])
        nmx = sb("head_neg_max", [P, 4, 3])
        pr = sb("probs", [P, 4, 3, P])
        pT = sb("probsT1", [P, 4, 3, P])
        oinv, o = sb("head_inv", [P, NH]), sb("attn_out", [P, D])
        oT0, oT1 = sb("oT0", [P, P]), sb("oT1", [DR, P])
        hb = sb("h_and_bias", [P, D])
        loaded = sem("attn1_weights_in")
        ys_in = [sem(f"slot_out_in{u}") for u in range(2)]
        S = {n: sem(n) for n in (
            "xc_ready", "L_done", "L_max", "L_exp", "T_done", "T_act", "T_dve", "Y_done", "h2_ready",
            "ln_var", "ln_rstd", "x4_ready", "a_done", "a_took", "qk_done", "v_done", "head_max", "rope_ready",
            "v_took", "c_done", "q_took", "k_took", "S_done", "S_took", "S_exp", "f_done", "f_act", "f_dve",
            "g_done", "o_ready", "h1_done", "oT_took", "p_done", "h3_ready", "hb_ready", "dve_c", "dve_a",
            "dve_o", "padded", "ones_set")}

        def at(b, n=1, k=0):
            return b * n + (k or n)

        def stages(t):
            if not isinstance(t, int):
                return t, t - 1, t - 2
            return tuple(b if 0 <= b < NB else None for b in (t, t - 1, t - 2))

        def each_turn(eng, turn):
            for t in range(4):
                turn(t, t % 2)
            with eng.Fori(2, NB // 2) as i:
                for u in range(2):
                    turn(i * 2 + u, u)
            for t in range(NB, NB + 2):
                turn(t, t % 2)

        def pT_flat(n):
            return pT[:].rearrange("p s g n -> p (s g n)")[:, n * 512:(n + 1) * 512]

        hb_of = lambda b: h[:, ds(b, 1), :].rearrange("p a d -> p (a d)")

        with nc.Block() as block:

            @block.sync
            def _(sp):
                for t, s in ((W0, ins["Wqkv"][0:P]), (W1, ins["Wqkv"][P:D]), (Wp0, ins["Wproj"][0:P]),
                             (Wp1, ins["Wproj"][P:D]), (bproj, ins["bproj"].partition_broadcast(P)),
                             (cos, ins["cos"]), (sin, ins["sin"])):
                    sp.dma_start(t[:], s).then_inc(loaded, 16)

                def turn(t, u):
                    b1, _, _ = stages(t)
                    if b1 is None:
                        return
                    past(sp, S["Y_done"], b1 - 1)
                    sp.dma_start(ysb[u][:], T["ys"][:, ds(b1, 1), :].rearrange("(c p) a d -> p c (a d)", p=P)
                                 ).then_inc(ys_in[u], 16)

                each_turn(sp, turn)

            @block.gpsimd
            def _(pool):
                pool.memset(qk[:], 0.0).then_inc(S["padded"], 1)
                pool.memset(vs[:], 1.0).then_inc(S["ones_set"], 1)
                pool.wait_ge(loaded, 7 * 16)

                def turn(t, u):
                    b1, b2, b3 = stages(t)
                    if b1 is not None:
                        past(pool, S["L_done"], 2 * b1)
                        pool.tensor_copy(xc0[:], T["xT0"][:, ds(b1 * P, P)]).then_inc(S["xc_ready"], 1)
                        pool.tensor_copy(xc1[:], T["xT1"][:, ds(b1 * P, P)]).then_inc(S["xc_ready"], 1)
                    if b2 is not None:
                        pool.wait_ge(S["ln_var"], at(b2))
                        pool.tensor_tensor(rs[:], ve[:], half[:, 0:1], ALU.pow).then_inc(S["ln_rstd"], 1)
                    if b3 is not None:
                        past(pool, S["h3_ready"], b3)
                        pool.tensor_tensor(hb[:], hb_of(b3), bproj[:], ALU.add).then_inc(S["hb_ready"], 1)

                each_turn(pool, turn)

            @block.tensor
            def _(pe):
                pe.wait_ge(loaded, 7 * 16)

                def turn(t, u):
                    b1, b2, b3 = stages(t)

                    def logits_half(k):
                        if k == 0:
                            pe.wait_ge(S["xc_ready"], at(b1, 2))
                            past(pe, S["h2_ready"], b1)
                        ks = slice(k * 512, (k + 1) * 512)
                        matmuls(pe, bank[:, k, :], [(xc0[:], T["phiT0"][:, ks]), (xc1[:], T["phiT1"][:, ks])]
                                ).then_inc(S["L_done"], 1)

                    def turn_probs():
                        pe.wait_ge(S["S_exp"], at(b3, 4))
                        for n in range(3):
                            for m in range(4):
                                s, g = divmod(n * 4 + m, 3)
                                last = pe.transpose(bank[:, 4 + n, m * P:(m + 1) * P], pr[:, s, g, :], ident[:])
                            last.then_inc(S["f_done"], 1)

                    def heads_out():
                        pe.wait_ge(S["f_act"], at(b3, 2))
                        pe.wait_ge(S["f_dve"], at(b3))
                        for hd in range(NH):
                            last = pe.matmul(bank[:, 7, hd * (HD + 1):(hd + 1) * (HD + 1)], pT[:, hd % 4, hd // 4, :],
                                             vs[:, hd, :], start=True, stop=True)
                        last.then_inc(S["g_done"], 1)

                    def two_pieces(src, n, done):
                        pe.transpose(bank[:, n, 0:P], src[:, 0:P], ident[:])
                        pe.transpose(bank[0:DR, n, P:2 * P], src[:, P:D], ident[:]).then_inc(done, 1)

                    if b1 is not None:
                        logits_half(0)
                        logits_half(1)
                    if b3 is not None:
                        turn_probs()
                    if b2 is not None:
                        if b3 is not None:
                            pe.wait_ge(S["f_act"], at(b3, 2, 1))
                        pe.wait_ge(S["x4_ready"], at(b2))
                        two_pieces(x4, 4, S["a_done"])
                    if b3 is not None:
                        heads_out()
                    if b2 is not None:
                        pe.wait_ge(S["a_took"], at(b2, 2))
                        matmuls(pe, bank[:, 6, 0:2 * D], [(x4T0[:], W0[:, 0:2 * D]), (x4T1[:], W1[:, 0:2 * D])]
                                ).then_inc(S["qk_done"], 1)
                        matmuls(pe, bank[:, 4, 2 * P:2 * P + D],
                                [(x4T0[:], W0[:, 2 * D:]), (x4T1[:], W1[:, 2 * D:])]).then_inc(S["v_done"], 1)
                    if b3 is not None:
                        pe.wait_ge(S["o_ready"], at(b3))
                        two_pieces(o, 5, S["h1_done"])
                    if b1 is not None:
                        pe.wait_ge(S["L_exp"], at(b1))
                        for k in range(2):
                            for m in range(4):
                                c = 4 * k + m
                                last = pe.transpose(bank[:, 2 + k, m * P:(m + 1) * P],
                                                    comb[:, c * P:(c + 1) * P], ident[:])
                            last.then_inc(S["T_done"], 1)
                    if b3 is not None:
                        pe.wait_ge(S["oT_took"], at(b3, 2))
                        if b2 is None:
                            past(pe, S["a_took"], 2 * NB)
                        matmuls(pe, bank[:, 4, 0:D], [(oT0[:], Wp0[:]), (oT1[:], Wp1[:])]
                                ).then_inc(S["p_done"], 1)
                    if b2 is not None:
                        pe.wait_ge(S["rope_ready"], at(b2))
                        for k in range(2):
                            for g in range(3):
                                last = pe.transpose(
                                    bank[:, 5 + k, g * P:(g + 1) * P],
                                    qk[:, k * NH + 4 * g:k * NH + 4 * g + 4, :].rearrange("p a d -> p (a d)"),
                                    ident[:])
                            last.then_inc(S["c_done"], 1)
                    if b1 is not None:
                        pe.wait_ge(S["T_act"], at(b1))
                        pe.wait_ge(S["T_dve"], at(b1))
                        pe.wait_ge(ys_in[u], ys_value(t))
                        matmuls(pe, bank[:, 0, 0:D], [(combT[:, c, :], ysb[u][:, c, :]) for c in range(NC)]
                                ).then_inc(S["Y_done"], 1)
                    if b2 is not None:
                        pe.wait_ge(S["q_took"], at(b2))
                        pe.wait_ge(S["k_took"], at(b2))
                        pe.wait_ge(S["v_took"], at(b2))
                        past(pe, S["h3_ready"], b2)
                        for s in range(4):
                            rows = slice(32 * s, 32 * s + HD)
                            for g in range(3):
                                gs = slice(g * P, (g + 1) * P)
                                last = pe.matmul(bank[:, 4 + s, gs], qT[rows, gs], kT[rows, gs],
                                                 start=True, stop=True)
                            last.then_inc(S["S_done"], 1)

                def ys_value(t):
                    return 16 * (t // 2 + 1) if isinstance(t, int) else (t - t_par[0]) * 8 + 16

                t_par = [0]

                def turn_with_parity(t, u):
                    t_par[0] = u
                    turn(t, u)

                each_turn(pe, turn_with_parity)

            @block.scalar
            def _(act):
                act.wait_ge(S["ones_set"], 1)

                def turn(t, u):
                    b1, b2, b3 = stages(t)

                    def pieces(n, d0, d1, done, took):
                        act.wait_ge(done, at(b_of))
                        act.activation(d0[:], bank[:, n, 0:P], ACT.Copy).then_inc(took, 1)
                        act.activation(d1[:], bank[0:DR, n, P:2 * P], ACT.Copy).then_inc(took, 1)

                    if b3 is not None:
                        for k, n in enumerate((0, 2)):
                            act.wait_ge(S["f_done"], at(b3, 3, n + 1))
                            past(act, S["g_done"], b3)
                            act.activation(pT_flat(n), bank[:, 4 + n, :], ACT.Copy).then_inc(S["f_act"], 1)
                    if b2 is not None:
                        b_of = b2
                        pieces(4, x4T0, x4T1, S["a_done"], S["a_took"])
                    if b1 is not None:
                        act.wait_ge(S["L_max"], at(b1))
                        past(act, S["T_done"], 2 * b1)
                        act.activation(comb[:].rearrange("p (k n) -> p k n", k=2), bank[:, 0:2, :], ACT.Exp,
                                       bias=nm[:], accum_out=csum[:]).then_inc(S["L_exp"], 1)
                    if b2 is not None:
                        act.wait_ge(S["v_done"], at(b2))
                        past(act, S["g_done"], b2)
                        act.activation(vs[:, :, 0:HD], bank[:, 4, 2 * P:2 * P + D].rearrange("p (a d) -> p a d", d=HD),
                                       ACT.Copy).then_inc(S["v_took"], 1)
                    if b3 is not None:
                        b_of = b3
                        pieces(5, oT0, oT1, S["h1_done"], S["oT_took"])
                    if b1 is not None:
                        act.wait_ge(S["T_done"], at(b1, 2, 1))
                        past(act, S["Y_done"], b1)
                        act.activation(combT[:, 0:4, :], group4(bank[:, 2, :]), ACT.Copy).then_inc(S["T_act"], 1)
                    if b2 is not None:
                        act.wait_ge(S["c_done"], at(b2, 2, 1))
                        past(act, S["S_done"], 4 * b2)
                        act.activation(qT[:], bank[:, 5, 0:3 * P], ACT.Copy).then_inc(S["q_took"], 1)
                        for s in range(4):
                            act.wait_ge(S["S_took"], at(b2, 4, s + 1))
                            act.activation(pr[:, s], pr[:, s], ACT.Exp).then_inc(S["S_exp"], 1)

                each_turn(act, turn)

            @block.vector
            def _(dve):
                dve.wait_ge(loaded, 7 * 16)
                dve.wait_ge(S["padded"], 1)

                def turn(t, u):
                    b1, b2, b3 = stages(t)
                    if b2 is not None:
                        x = hb_of(b2)
                        wait_apart(dve, S["h2_ready"], at(b2))
                        dve.bn_stats(st6[:], x).then_inc(S["dve_a"], 1)
                        wait_apart(dve, S["dve_a"], at(b2, 5, 1))
                        dve.bn_aggr(mv[:], st6[:]).then_inc(S["dve_a"], 1)
                        dve.wait_ge(S["dve_a"], at(b2, 5, 2))
                        dve.tensor_scalar(ve[:], mv[:, 1:2], EPS, None, ALU.add).then_inc(S["ln_var"], 1)
                    if b2 is not None:
                        dve.wait_ge(S["ln_rstd"], at(b2))
                        past(dve, S["a_done"], b2)
                        dve.tensor_scalar(x4[:], x, mv[:, 0:1], rs[:], ALU.subtract, ALU.mult
                                          ).then_inc(S["x4_ready"], 1)
                    if b1 is not None:
                        past(dve, S["L_exp"], b1)
                        for k in range(2):
                            dve.wait_ge(S["L_done"], at(b1, 2, k + 1))
                            dve.tensor_reduce(nm2[:, k:k + 1], bank[:, k, :], AX_X, ALU.max).then_inc(S["dve_c"], 1)
                        dve.wait_ge(S["dve_c"], at(b1, 3, 2))
                        dve.tensor_reduce(nm[:], nm2[:], AX_X, ALU.max, negate=True).then_inc(S["L_max"], 1)
                    if b3 is not None:
                        dve.wait_ge(S["f_done"], at(b3, 3, 2))
                        past(dve, S["g_done"], b3)
                        dve.tensor_copy(pT_flat(1), bank[:, 5, :]).then_inc(S["f_dve"], 1)
                    if b3 is not None:
                        heads = bank[:, 7, 0:NH * (HD + 1)].rearrange("p (a d) -> p a d", d=HD + 1)
                        dve.wait_ge(S["g_done"], at(b3))
                        dve.reciprocal(oinv[:], heads[:, :, HD]).then_inc(S["dve_o"], 1)
                        dve.wait_ge(S["dve_o"], at(b3))
                        past(dve, S["h1_done"], b3)
                        dve.tensor_tensor(o[:].rearrange("p (a d) -> p a d", d=HD), heads[:, :, 0:HD],
                                          oinv[:].unsqueeze(2).broadcast_to([P, NH, HD]), ALU.mult
                                          ).then_inc(S["o_ready"], 1)
                    if b2 is not None:
                        src = bank[:, 6, 0:2 * D]
                        pairs = src.rearrange("p (m two) -> p m two", two=2)
                        cp = crossed[:].rearrange("p (m two) -> p m two", two=2)
                        sp_ = sin[:].rearrange("p (m two) -> p m two", two=2)
                        dve.wait_ge(S["qk_done"], at(b2))
                        dve.tensor_tensor(straight[:], src, cos[:], ALU.mult).then_inc(S["dve_a"], 1)
                        dve.tensor_tensor(cp[:, :, 0:1], pairs[:, :, 1:2], sp_[:, :, 0:1], ALU.mult
                                          ).then_inc(S["dve_a"], 1)
                        dve.tensor_tensor(cp[:, :, 1:2], pairs[:, :, 0:1], sp_[:, :, 1:2], ALU.mult
                                          ).then_inc(S["dve_a"], 1)
                        dve.wait_ge(S["dve_a"], at(b2, 5, 5))
                        past(dve, S["c_done"], 2 * b2)
                        dve.tensor_tensor(qk[:, :, 0:HD], straight[:].rearrange("p (a d) -> p a d", d=HD),
                                          crossed[:].rearrange("p (a d) -> p a d", d=HD), ALU.add
                                          ).then_inc(S["rope_ready"], 1)
                    if b1 is not None:
                        dve.wait_ge(S["T_done"], at(b1, 2, 2))
                        past(dve, S["Y_done"], b1)
                        dve.tensor_copy(combT[:, 4:8, :], group4(bank[:, 3, :])).then_inc(S["T_dve"], 1)
                    if b3 is not None:
                        dve.wait_ge(S["p_done"], at(b3))
                        dve.wait_ge(S["hb_ready"], at(b3))
                        dve.tensor_tensor(hb_of(b3), bank[:, 4, 0:D], hb[:], ALU.add).then_inc(S["h3_ready"], 1)
                    if b2 is not None:
                        dve.wait_ge(S["c_done"], at(b2, 2, 2))
                        past(dve, S["S_done"], 4 * b2)
                        dve.tensor_copy(kT[:], bank[:, 6, 0:3 * P]).then_inc(S["k_took"], 1)
                    if b1 is not None:
                        dve.wait_ge(S["L_exp"], at(b1))
                        dve.reciprocal(cinv[:], csum[:]).then_inc(S["dve_c"], 1)
                        dve.wait_ge(S["dve_c"], at(b1, 3))
                        dve.wait_ge(S["Y_done"], at(b1))
                        dve.scalar_tensor_tensor(hb_of(b1), bank[:, 0, 0:D], cinv[:, 0:1], hb_of(b1),
                                                 ALU.mult, ALU.add).then_inc(S["h2_ready"], 1)
                    if b2 is not None:
                        past(dve, S["f_done"], 3 * b2)
                        for s in range(4):
                            sc = group4(bank[:, 4 + s, :])[:, 0:3]
                            dve.wait_ge(S["S_done"], at(b2, 4, s + 1))
                            dve.tensor_reduce(nmx[:, s, :], sc, AX_X, ALU.max).then_inc(S["head_max"], 1)
                            dve.wait_ge(S["head_max"], at(b2, 4, s + 1))
                            dve.tensor_tensor(pr[:, s], sc, nmx[:, s, :].unsqueeze(2).broadcast_to([P, 3, P]),
                                              ALU.subtract).then_inc(S["S_took"], 1)

                each_turn(dve, turn)


def routing_phase(nc, ins, T):
    with ExitStack() as ctx:
        al = Alloc(nc, ctx)
        sb, sem = al.sb, al.sem
        bank, ident, h, half = T["bank"], T["ident"], T["h"], T["half"]
        st6, mv = sb("ln5_stats", [P, GB, 6]), sb("ln5_mean_var", [P, GB, 2])
        ve, rs = sb("ln5_var_eps", [P, GB]), sb("ln5_rstd", [P, GB])
        x5 = sb("x5_all", [P, NB, D])
        x5s = sb("x5_group", [P, GB, D])
        x5T0, x5T1 = sb("x5T0", [P, GB * P]), sb("x5T1", [DR, GB * P])
        rw0, rw1 = sb("router0", [P, NE1]), sb("router1", [DR, NE1])
        lg = sb("router_logits", [P, NB, NE1])
        rank, w, onehot = sb("rank", [P, NE1]), sb("ranked", [P, NB, NE1]), sb("onehot", [P, NB, NE1])
        lmax, first = sb("router_max", [P, NB]), sb("first", [P, NB])
        upto, ones = sb("upto", [P, P]), sb("ones", [P, P])
        pre = [sb(f"before{k}", [P, NB, NE1]) for k in range(2)]
        pos, kept = sb("position", [P, NB]), sb("kept", [P, NB])
        base, to_f, from_f = sb("expert_base", [P, NB]), sb("to_f", [P, NB]), sb("from_f", [P, NB])
        to_i = sb("to_i", [P, NB], I32)
        loaded, consts = sem("router_in"), sem("router_constants")
        steps, var, rstd = sem("router_steps"), sem("ln5_var"), sem("ln5_rstd_ready")
        ready, tproduct, took, ttook = sem("x5_ready"), sem("x5T_product"), sem("x5T_act"), sem("x5T_vector")
        lproduct, ltook = sem("router_product"), sem("router_took")
        chosen, counted, placed, scattered = sem("chosen"), sem("counted"), sem("placed"), sem("scattered")
        exped = sem("router_exp")
        lx, lsum = sb("router_exp_of", [P, NB, NE1]), sb("router_sum", [P, NB])
        bc = lambda t: t[:].unsqueeze(2).broadcast_to([P, NB, NE1])
        with nc.Block() as block:

            @block.sync
            def _(sp):
                sp.dma_start(rw0[:], ins["router"][0:P]).then_inc(loaded, 16)
                sp.dma_start(rw1[:], ins["router"][P:D]).then_inc(loaded, 16)
                sp.dma_start(rank[:], ins["rank"].partition_broadcast(P)).then_inc(loaded, 16)
                sp.wait_ge(loaded, 48)

            @block.gpsimd
            def _(pool):
                pool.memset(upto[:], 1.0).then_inc(consts, 1)
                pool.memset(ones[:], 1.0).then_inc(consts, 1)
                pool.wait_ge(consts, 2)
                pool.affine_select(out=upto[:], in_=upto[:], compare_op=ALU.is_ge, fill=0.0, base=0,
                                   pattern=[[1, P]], channel_multiplier=-1).then_inc(consts, 1)
                with pool.Fori(0, NG) as g:
                    pool.wait_ge(var, g + 1)
                    pool.tensor_tensor(rs[:], ve[:], half[:], ALU.pow).then_inc(rstd, 1)
                pool.wait_ge(placed, 1)
                for b in range(NB):
                    pool.indirect_dma_start(
                        out=T["xm"], out_offset=bass.IndirectOffsetOnAxis(ap=to_i[:, b:b + 1], axis=0),
                        in_=x5[:, b, :], in_offset=None, bounds_check=NE1 * CAP - 1, oob_is_err=False,
                    ).then_inc(scattered, 16)
                pool.wait_ge(scattered, 16 * NB)

            @block.vector
            def _(dve):
                with dve.Fori(0, NG) as g:
                    st = Steps(dve, steps, g, 2 * GB)
                    for j in range(GB):
                        st.did(dve.bn_stats(st6[:, j, :], h[:, ds(g * GB + j, 1), :]))
                    st.wait_apart()
                    for j in range(GB):
                        st.did(dve.bn_aggr(mv[:, j, :], st6[:, j, :]))
                    st.wait()
                    dve.tensor_scalar(ve[:], mv[:, :, 1], EPS, None, ALU.add).then_inc(var, 1)
                    dve.wait_ge(rstd, g + 1)
                    for j in range(GB):
                        last = dve.tensor_scalar(x5s[:, j, :], h[:, ds(g * GB + j, 1), :], mv[:, j, 0:1],
                                                 rs[:, j:j + 1], ALU.subtract, ALU.mult)
                    last.then_inc(ready, 1)
                    dve.wait_ge(tproduct, g * 2 + 2)
                    dve.tensor_copy(x5T1[:], bank[0:DR, 1, :]).then_inc(ttook, 1)
                    dve.wait_ge(ltook, g * 2 + 2)
                st = Steps(dve, steps, start=2 * GB * NG)
                dve.wait_ge(loaded, 48)
                st.link(dve.tensor_reduce(lmax[:], lg[:], AX_X, ALU.max))
                st.link(dve.tensor_tensor(w[:], lg[:], bc(lmax), ALU.is_equal))
                st.link(dve.tensor_tensor(w[:], w[:], rank[:].unsqueeze(1).broadcast_to([P, NB, NE1]), ALU.mult))
                st.link(dve.tensor_reduce(first[:], w[:], AX_X, ALU.max))
                dve.tensor_tensor(onehot[:], w[:], bc(first), ALU.is_equal).then_inc(chosen, 1)
                dve.tensor_tensor(lx[:], lg[:], bc(lmax), ALU.subtract).then_inc(chosen, 1)
                dve.wait_ge(exped, 1)
                st.link(dve.tensor_reduce(lsum[:], lx[:], AX_X, ALU.add))
                st.link(dve.reciprocal(lsum[:], lsum[:]))
                dve.wait_ge(counted, 1)
                tot = bank[:, 1, 0:NB * NE1].rearrange("p (b e) -> p b e", e=NE1)
                cum = bank[:, 0, 0:NB * NE1].rearrange("p (b e) -> p b e", e=NE1)
                st.did(dve.memset(pre[0][:, 0, :], 0.0))
                st.did(dve.tensor_copy(pre[0][:, 1:NB, :], tot[:, 0:NB - 1, :]))
                st.wait()
                a, k = 0, 1
                while k < NB:
                    st.did(dve.tensor_copy(pre[1 - a][:, 0:k, :], pre[a][:, 0:k, :]))
                    st.did(dve.tensor_tensor(pre[1 - a][:, k:NB, :], pre[a][:, k:NB, :], pre[a][:, 0:NB - k, :],
                                             ALU.add))
                    st.wait()
                    a, k = 1 - a, 2 * k
                st.link(dve.tensor_tensor(pre[a][:], pre[a][:], cum, ALU.add))
                st.link(dve.tensor_tensor(pre[a][:], pre[a][:], onehot[:], ALU.mult))
                st.link(dve.tensor_reduce(pos[:], pre[a][:], AX_X, ALU.add))
                st.did(dve.tensor_scalar(kept[:], pos[:], float(CAP), None, ALU.is_lt))
                st.did(dve.tensor_scalar(base[:], first[:], float(NE1), -float(CAP), ALU.subtract, ALU.mult))
                st.wait()
                st.link(dve.tensor_tensor(from_f[:], pos[:], kept[:], ALU.mult))
                st.link(dve.tensor_tensor(from_f[:], from_f[:], base[:], ALU.add))
                st.did(dve.tensor_copy(T["from_i"][:], from_f[:]))
                st.did(dve.tensor_scalar(to_f[:], kept[:], -1.0, -float(NE1 * CAP), ALU.add, ALU.mult))
                st.did(dve.tensor_tensor(T["gate"][:], lsum[:], kept[:], ALU.mult))
                st.wait()
                st.link(dve.tensor_tensor(to_f[:], to_f[:], from_f[:], ALU.add))
                dve.tensor_copy(to_i[:], to_f[:]).then_inc(placed, 1)

            @block.scalar
            def _(act):
                with act.Fori(0, NG) as g:
                    act.wait_ge(tproduct, g * 2 + 1)
                    act.activation(x5T0[:], bank[:, 0, :], ACT.Copy).then_inc(took, 1)
                    act.activation(x5[:, ds(g * GB, GB), :], x5s[:], ACT.Copy).then_inc(ltook, 1)
                    act.wait_ge(lproduct, g + 1)
                    act.activation(lg[:, ds(g * GB, GB), :],
                                   bank[:, 2, 0:GB * NE1].rearrange("p (j e) -> p j e", e=NE1),
                                   ACT.Copy).then_inc(ltook, 1)
                act.wait_ge(chosen, 2)
                act.activation(lx[:], lx[:], ACT.Exp).then_inc(exped, 1)

            @block.tensor
            def _(pe):
                pe.wait_ge(loaded, 48)
                with pe.Fori(0, NG) as g:
                    pe.wait_ge(ready, g + 1)
                    for k, rows in ((0, P), (1, DR)):
                        for j in range(GB):
                            last = pe.transpose(bank[0:rows, k, j * P:(j + 1) * P],
                                                x5s[:, j, k * P:k * P + rows], ident[:])
                        last.then_inc(tproduct, 1)
                    pe.wait_ge(took, g + 1)
                    pe.wait_ge(ttook, g + 1)
                    for j in range(GB):
                        js = slice(j * P, (j + 1) * P)
                        last = matmuls(pe, bank[:, 2, j * NE1:(j + 1) * NE1],
                                       [(x5T0[:, js], rw0[:]), (x5T1[:, js], rw1[:])])
                    last.then_inc(lproduct, 1)
                pe.wait_ge(consts, 3)
                pe.wait_ge(chosen, 1)
                flat = onehot[:].rearrange("p b e -> p (b e)")
                pe.matmul(bank[:, 0, 0:NB * NE1], upto[:], flat, start=True, stop=True)
                pe.matmul(bank[:, 1, 0:NB * NE1], ones[:], flat, start=True, stop=True).then_inc(counted, 1)


def gather_phase(nc, T, out):
    with ExitStack() as ctx:
        al = Alloc(nc, ctx)
        got = al.sb("gathered_rows", [P, NB, D])
        taken = [al.sem(f"row_gathered{half}") for half in range(2)]
        added, stored = al.sem("row_added"), al.sem("out_stored")
        h = T["h"]
        with nc.Block() as block:

            @block.gpsimd
            def _(pool):
                for b in range(NB):
                    pool.indirect_dma_start(
                        out=got[:, b, :], out_offset=None, in_=T["ym"],
                        in_offset=bass.IndirectOffsetOnAxis(ap=T["from_i"][:, b:b + 1], axis=0),
                    ).then_inc(taken[2 * b // NB], 16)

            @block.vector
            def _(dve):
                for b in range(NB):
                    dve.wait_ge(taken[2 * b // NB], 16 * NB // 2)
                    dve.scalar_tensor_tensor(h[:, b, :], got[:, b, :], T["gate"][:, b:b + 1], h[:, b, :],
                                             ALU.mult, ALU.add).then_inc(added, 1)

            @block.sync
            def _(sp):
                for g in range(NG):
                    sp.wait_ge(added, (g + 1) * GB)
                    sp.dma_start(out[g * GB:(g + 1) * GB].rearrange("b p d -> p b d"),
                                 h[:, g * GB:(g + 1) * GB, :]).then_inc(stored, 16)
                sp.wait_ge(stored, 16 * NG)


def hidden_bias(b):
    return np.ascontiguousarray(b.reshape(b.shape[0], -1, P).transpose(2, 1, 0))


def host_layout(inputs):
    a = {k: np.asarray(v) for k, v in inputs.items()}
    return {
        "ids": np.ascontiguousarray(a["x"].T), "mask": np.ascontiguousarray(a["mask_BS_i1_0"].T),
        "tok": a["L0_tok_tok_w"], "pos": a["L0_tok_pos_w"], "type": a["L0_tok_type_w"],
        "gamma": a["L0_tok_gamma"], "beta": a["L0_tok_beta"],
        "WqT": np.ascontiguousarray(a["L0_attn_Wq"].T), "WkT": np.ascontiguousarray(a["L0_attn_Wk"].T),
        "Wv": a["L0_attn_Wv"],
        "ln_g": np.ascontiguousarray(a["L0_ffn_ln_g"].T), "ln_b": np.ascontiguousarray(a["L0_ffn_ln_b"].T),
        "Wqkv": np.ascontiguousarray(a["L1_attn_w_qkv"].T), "Wproj": np.ascontiguousarray(a["L1_attn_w_proj"].T),
        "bproj": a["L1_attn_b_proj"], "router": a["L1_ffn_router_w"],
        "rank": np.arange(NE1, 0, -1, dtype=np.float32), **rope_tables(),
        "w1_0": a["L0_ffn_w1"], "w2_0": a["L0_ffn_w2"], "b2_0": a["L0_ffn_b2"],
        "b1_0": hidden_bias(a["L0_ffn_b1"]),
        "w1_1": a["L1_ffn_w1"], "w2_1": a["L1_ffn_w2"], "b2_1": a["L1_ffn_b2"],
        "b1_1": hidden_bias(a["L1_ffn_b1"]),
        "phiT": np.ascontiguousarray(a["L0_ffn_phi"].reshape(NS, D).T),
    }


def rope_tables():
    freq = 1.0 / np.float32(10000.0) ** (np.arange(0, HD, 2, dtype=np.float32) / np.float32(HD))
    angle = np.arange(P, dtype=np.float32)[:, None] * freq[None, :].astype(np.float32)
    cos = np.repeat(np.cos(angle), 2, axis=1)
    sin = np.stack([-np.sin(angle), np.sin(angle)], axis=-1).reshape(P, HD)
    q_and_k = lambda t: np.concatenate([np.tile(t, NH) * np.float32(HD ** -0.5), np.tile(t, NH)], axis=1)
    return {"cos": q_and_k(cos).astype(np.float32), "sin": q_and_k(sin).astype(np.float32)}


def kernel(**inputs):
    from concourse import bacc
    from concourse.bass_utils import run_bass_kernel_spmd

    nc = bacc.Bacc("TRN2", target_bir_lowering=False, num_devices=1)
    arrays = host_layout(inputs)
    ins = {n: nc.dram_tensor(f"in_{n}", v.shape, mybir.dt.from_np(v.dtype), kind="ExternalInput").ap()
           for n, v in arrays.items()}
    out = nc.dram_tensor("out", (NB, P, D), F32, kind="ExternalOutput").ap()
    tower_program(nc, ins, out)
    r = run_bass_kernel_spmd(nc, [{f"in_{n}": v for n, v in arrays.items()}], core_ids=[0])
    return r.results[0]["out"]
```

```python
from contextlib import ExitStack

import concourse.bass as bass
from concourse import mybir
import numpy as np

F32 = mybir.dt.float32
F32R = mybir.dt.float32r
I32 = mybir.dt.int32
ALU = mybir.AluOpType
ACT = mybir.ActivationFunctionType
AX_X = mybir.AxisListType.X
ds = bass.ds

P = 128
NB = 32
D = 192
DR = D - P
GB = 4
NG = NB // GB
NE0 = 64
SP_E = 16
NS = NE0 * SP_E
NC = NS // P
H0 = 384
NH = 12
HD = D // NH
NE1 = 8
H1 = 768
CAP = P * NB // NE1
TAG = 2
EPS = 1e-5
EPS_PHI = 1e-6
MASKED = -1e30


def group4(ap):
    return ap.rearrange("p (j n) -> p j n", j=GB)


def matmuls(pe, out, pairs, **kw):
    for n, (w, m) in enumerate(pairs):
        last = pe.matmul(out, w, m, start=n == 0, stop=n == len(pairs) - 1, **kw)
    return last


def wait_apart(eng, sem, value):
    eng.wait_ge(sem, value)
    eng.nop(nofuse=True)


class Steps:

    def __init__(self, eng, sem, turn=0, per_turn=0, start=0):
        self.eng, self.sem, self.base, self.n, self.per_turn = eng, sem, turn * per_turn + start, 0, per_turn

    def did(self, ins):
        ins.then_inc(self.sem, 1)
        self.n += 1
        return ins

    def wait(self):
        self.eng.wait_ge(self.sem, self.base + self.n)

    def wait_apart(self):
        wait_apart(self.eng, self.sem, self.base + self.n)

    def link(self, ins):
        self.did(ins)
        self.wait()

    def end(self):
        assert self.n == self.per_turn, (self.n, self.per_turn)


class Alloc:
    def __init__(self, nc, ctx):
        self.nc, self.ctx, self.sems = nc, ctx, []

    def sb(self, name, shape, dt=F32):
        return self.ctx.enter_context(self.nc.sbuf_tensor(name, shape, dt))

    def sem(self, name):
        self.sems.append(self.nc.alloc_semaphore(name))
        return self.sems[-1]

    def free_sems(self):
        self.nc.clear_and_free_semaphores(self.sems)
        self.nc.all_engine_barrier()


def tower_program(nc, ins, out):
    with ExitStack() as ctx:
        al = Alloc(nc, ctx)
        T = {}
        T["ident"] = al.sb("ident", [P, P])
        T["h"] = al.sb("h_all", [P, NB, D])
        T["half"] = al.sb("minus_half", [P, GB])
        T["minus_upper"] = al.sb("minus_upper", [P, 1])
        T["bank"] = ctx.enter_context(nc.psum_tensor("bank", [P, 8, 512], F32))
        T["xs"] = nc.dram_tensor("slot_inputs", [NS, NB, D], F32, kind="Internal").ap()
        T["ys"] = nc.dram_tensor("slot_outputs", [NS, NB, D], F32, kind="Internal").ap()
        T["xm"] = nc.dram_tensor("routed_inputs", [NE1 * CAP, TAG + D], F32, kind="Internal").ap()
        with ExitStack() as c1:
            a1 = Alloc(nc, c1)
            for n in ("x_hi", "x_lo", "x_hi_over_lo"):
                T[n] = a1.sb(n + "_all", [P, NB * P], F32R)
            for n in ("phi_hi0", "phi_lo0", "phi_hi1", "phi_lo1"):
                T[n] = a1.sb(n, [P, NS], F32R)
            with ExitStack() as c2:
                a2 = Alloc(nc, c2)
                for n, shape in (("M0", [P, D]), ("M1", [DR, D]), ("Wv0", [P, D]), ("Wv1", [DR, D]),
                                 ("causal", [P, P]), ("pos0", [P, D]), ("dtype", [P, D]),
                                 ("maskf", [P, NB]), ("gamma", [P, D]), ("beta", [P, D]),
                                 ("phiT0", [P, NS]), ("phiT1", [P, NS])):
                    T[n] = a2.sb(n, shape)
                T["tok"], T["ids"] = ins["tok"], a2.sb("ids", [P, NB], I32)
                T["gathered"] = [a2.sem(f"rows_gathered{k}") for k in range(4)]
                T["phi_norm"], T["half16"] = a2.sb("phi_norm", [P, 2, SP_E]), a2.sb("minus_half16", [P, SP_E])
                T["phi_in"], T["xm_filled"] = a2.sem("phi_in"), a2.sem("routed_rows_filled")
                T["zero"] = a2.sb("zero", [P, 4, TAG + D])
                setup_phase(nc, ins, T)
                tower_phase(nc, T)
            expert_phase(nc, T, "e0", NE0, H0, T["xs"].rearrange("s b d -> (s b) d"),
                         T["ys"].rearrange("s b d -> (s b) d"), ins["w1_0"], ins["b1_0"], ins["w2_0"],
                         ins["b2_0"], ACT.Gelu, ln=(ins["ln_g"], ins["ln_b"]))
            combine_phase(nc, ins, T)
        routing_phase(nc, ins, T, out.rearrange("b p d -> (b p) d"))
        expert_phase(nc, T, "e1", NE1, H1, T["xm"], None, ins["w1_1"], ins["b1_1"], ins["w2_1"],
                     ins["b2_1"], ACT.Gelu_apprx_tanh, routed_to=out.rearrange("b p d -> (b p) d"))


def setup_phase(nc, ins, T):
    with ExitStack() as ctx:
        al = Alloc(nc, ctx)
        ids, gathered = T["ids"], T["gathered"]
        maski = al.sb("maski", [P, NB], I32)
        type0 = al.sb("type0", [P, D])
        type1 = al.sb("type1", [P, D])
        WqT0, WqT1 = al.sb("WqT0", [P, D]), al.sb("WqT1", [DR, D])
        WkT0, WkT1 = al.sb("WkT0", [P, D]), al.sb("WkT1", [DR, D])
        half16 = T["half16"]
        loads = {n: al.sem(f"{n}_loaded") for n in ("ids", "qk", "emb", "rest")}
        qk_product = al.sem("qk_product")
        consts = al.sem("pool_constants")
        vsteps = al.sem("setup_vector_steps")
        zero = T["zero"]
        zeroed = al.sem("zeroed")
        bank = T["bank"]
        with nc.Block() as block:

            @block.sync
            def _(sp):
                sp.dma_start(ids[:], ins["ids"]).then_inc(loads["ids"], 16)
                for t, n in ((WqT0, "WqT"), (WkT0, "WkT")):
                    sp.dma_start(t[:], ins[n][0:P]).then_inc(loads["qk"], 16)
                for t, n in ((WqT1, "WqT"), (WkT1, "WkT")):
                    sp.dma_start(t[:], ins[n][P:D]).then_inc(loads["qk"], 16)
                sp.dma_start(T["phiT0"][:], ins["phiT"][0:P]).then_inc(T["phi_in"], 16)
                sp.dma_start(T["phiT1"][0:DR], ins["phiT"][P:D]).then_inc(T["phi_in"], 16)
                sp.dma_start(T["phiT1"][DR:P], ins["phiT"][P:D]).then_inc(T["phi_in"], 16)
                sp.dma_start(T["pos0"][:], ins["pos"]).then_inc(loads["emb"], 16)
                sp.dma_start(type0[:], ins["type"][0, :].partition_broadcast(P)).then_inc(loads["emb"], 16)
                sp.dma_start(type1[:], ins["type"][1, :].partition_broadcast(P)).then_inc(loads["emb"], 16)
                sp.dma_start(maski[:], ins["mask"]).then_inc(loads["emb"], 16)
                sp.dma_start(T["gamma"][:], ins["gamma"].partition_broadcast(P)).then_inc(loads["rest"], 16)
                sp.dma_start(T["beta"][:], ins["beta"].partition_broadcast(P)).then_inc(loads["rest"], 16)
                sp.dma_start(T["Wv0"][:], ins["Wv"][0:P]).then_inc(loads["rest"], 16)
                sp.dma_start(T["Wv1"][:], ins["Wv"][P:D]).then_inc(loads["rest"], 16)
                sp.wait_ge(zeroed, 1)
                xm = T["xm"].rearrange("(r p j) d -> r p j d", p=P, j=4)
                for r in range(NE1 * CAP // (4 * P)):
                    sp.dma_start(xm[r], zero[:]).then_inc(T["xm_filled"], 16)
                sp.wait_ge(loads["rest"], 16 * 4)

            @block.gpsimd
            def _(pool):
                pool.memset(T["half"][:], -0.5).then_inc(consts, 1)
                pool.memset(half16[:], -0.5).then_inc(consts, 1)
                pool.wait_ge(loads["ids"], 16)
                for b in range(2 * GB):
                    pool.indirect_dma_start(
                        out=T["h"][:, b, :], out_offset=None, in_=ins["tok"],
                        in_offset=bass.IndirectOffsetOnAxis(ap=ids[:, b:b + 1], axis=0),
                    ).then_inc(gathered[b // GB], 16)
                pool.memset(T["ident"][:], 0.0).then_inc(consts, 1)
                pool.memset(T["causal"][:], 0.0).then_inc(consts, 1)
                pool.wait_ge(consts, 4)
                pool.affine_select(out=T["ident"][:], in_=T["ident"][:], compare_op=ALU.not_equal,
                                   fill=1.0, base=0, pattern=[[-1, P]],
                                   channel_multiplier=1).then_inc(consts, 1)
                pool.affine_select(out=T["causal"][:], in_=T["causal"][:], compare_op=ALU.is_ge,
                                   fill=MASKED, base=0, pattern=[[-1, P]],
                                   channel_multiplier=1).then_inc(consts, 1)

            @block.vector
            def _(dve):
                st = Steps(dve, vsteps)
                st.link(dve.memset(zero[:], 0.0))
                dve.memset(zero[:, :, 1:2], float(NB * P)).then_inc(zeroed, 1)
                dve.memset(T["minus_upper"][0:DR, :], 0.0)
                dve.memset(T["minus_upper"][DR:P, :], -1.0)
                dve.wait_ge(loads["emb"], 64)
                dve.tensor_tensor(T["pos0"][:], T["pos0"][:], type0[:], ALU.add)
                dve.tensor_tensor(T["dtype"][:], type1[:], type0[:], ALU.subtract)
                dve.tensor_copy(T["maskf"][:], maski[:])

            @block.tensor
            def _(pe):
                pe.wait_ge(loads["qk"], 64)
                matmuls(pe, bank[:, 0, 0:D], [(WqT0[:, 0:P], WkT0[:]), (WqT1[:, 0:P], WkT1[:])])
                matmuls(pe, bank[0:DR, 1, 0:D], [(WqT0[:, P:D], WkT0[:]), (WqT1[:, P:D], WkT1[:])]
                        ).then_inc(qk_product, 1)

            @block.scalar
            def _(act):
                act.wait_ge(qk_product, 1)
                act.activation(T["M0"][:], bank[:, 0, 0:D], ACT.Copy)
                act.activation(T["M1"][:], bank[0:DR, 1, 0:D], ACT.Copy)


def tower_phase(nc, T):
    with ExitStack() as ctx:
        al = Alloc(nc, ctx)
        sb, sem = al.sb, al.sem
        bank, ident, h = T["bank"], T["ident"], T["h"]
        half = T["half"]
        typed = sb("typed", [P, GB, D])
        st6, mv = sb("ln_stats", [P, GB, 6]), sb("ln_mean_var", [P, GB, 2])
        ve, rs = sb("ln_var_eps", [P, GB]), sb("ln_rstd", [P, GB])
        xn = sb("xn", [P, GB, D])
        emb_added, h0_ready = sem("emb_added"), sem("h0_ready")
        evar, erstd = sem("emb_var_ready"), sem("emb_rstd_ready")
        pool_steps, emb_steps = sem("emb_pool_steps"), sem("emb_vector_steps")
        xn_ready = sem("xn_ready")
        xT0, xT1 = sb("xT0", [P, GB * P]), sb("xT1", [DR, GB * P])
        qT0, qT1 = sb("qT0", [P, GB * P]), sb("qT1", [DR, GB * P])
        v = sb("v", [P, GB, D])
        sm, ex = sb("masked_scores", [P, GB, P]), sb("exp_scores", [P, GB, P])
        nmx, ssum, rinv = sb("neg_max", [P, GB]), sb("exp_sum", [P, GB]), sb("inv_sum", [P, GB])
        pT = sb("probsT", [P, GB * P])
        product = sem("attn_product")
        act_took, dve_took = sem("attn_act_took"), sem("attn_vector_took")
        score_max, exp_done, attn_steps = sem("score_max_ready"), sem("exp_done"), sem("attn_vector_steps")
        PRIME = 2
        xst6, xmv = sb("x3_stats", [P, GB, 6]), sb("x3_mean_var", [P, GB, 2])
        xve, xrs = sb("x3_var_eps", [P, GB]), sb("x3_rstd", [P, GB])
        xvar, xrstd = sem("x3_var_ready"), sem("x3_rstd_ready")
        x3 = sb("x3", [P, GB, 2 + D + DR])
        ls = sb("slot_exp", [P, 2, 512])
        nmc = sb("column_neg_max", [P, 2, GB])
        disp = sb("dispatch_weights", [P, 2, 512])
        usum = sb("slot_sums", [P, 2, GB, 2])
        uss = sb("slot_square_sums", [P, 2, GB])
        usq = sb("slot_squares", [P, GB, D])
        q1, q2, uve = sb("eps_s2", [P, 2, GB]), sb("minus_mean2", [P, 2, GB]), sb("slot_var", [P, 2, GB])
        umean, urs = sb("slot_mean", [P, 2, GB]), sb("slot_rstd", [P, 2, GB])
        stage = sb("slot_stage", [P, 2, GB, D])
        x3_ready, x3T_product, x3T_act = sem("x3_ready"), sem("x3T_product"), sem("x3T_act")
        logits, col_max, exped = sem("logits"), sem("col_max"), sem("exped")
        turned, disp_ready, slots_sum = sem("weights_turned"), sem("dispatch_ready"), sem("slots_summed")
        stats_ready, stage_ready, stored = sem("slot_stats_ready"), sem("stage_ready"), [sem("stored0"), sem("stored1")]
        svar_ready, srstd_ready = sem("slot_var_ready"), sem("slot_rstd_ready")
        x3_steps, slot_steps, act_steps = sem("x3_vector_steps"), sem("slot_vector_steps"), sem("slot_act_steps")
        phi_sq = sb("phi_sq", [P, NS])
        phi_steps, phi_squares, phi_powed = sem("phi_steps"), sem("phi_squares"), sem("phi_powed")
        phi_scaled, phi_hi_ready, phi_ready = sem("phi_scaled"), sem("phi_hi_ready"), sem("phi_ready")
        xhi1 = sb("x_hi1", [P, 512], F32R)
        x_split = sem("x_split")
        U = [bank[:, 2:4, 0:2 * (D + 2)].rearrange("p k (j d) -> p k j d", j=2),
             bank[:, 4:6, 0:2 * (D + 2)].rearrange("p k (j d) -> p k j d", j=2)]

        def logits_bank(c):
            return bank[:, 6 * (c % 2), :]

        def hg(g):
            return h[:, ds(g * GB, GB), :]

        def turns(eng, turn):
            turn(0, None, None)
            turn(1, 0, None)
            turn(2, 1, 0)
            with eng.Fori(2, NG - 1) as t:
                turn(t + 1, t, t - 1)
            turn(None, NG - 1, NG - 2)
            turn(None, None, NG - 1)

        def norm_stats(dve, steps, x, st6, mv, ve, ready):
            for j in range(GB):
                steps.did(dve.bn_stats(st6[:, j, :], x[:, j, :]))
            steps.wait_apart()
            for j in range(GB):
                steps.did(dve.bn_aggr(mv[:, j, :], st6[:, j, :]))
            steps.wait()
            dve.tensor_scalar(ve[:], mv[:, :, 1], EPS, None, ALU.add).then_inc(ready, 1)

        with nc.Block() as block:

            @block.gpsimd
            def _(pool):
                tiles = lambda t: t.unsqueeze(2).broadcast_to([P, GB, D])
                columns = lambda t: t[:].unsqueeze(1).broadcast_to([P, GB, D])

                def embed(e, s):
                    if s == 0:
                        past(pool, emb_added, e)
                        st = Steps(pool, pool_steps, e, 5)
                        st.link(pool.tensor_tensor(typed[:], T["dtype"][:].unsqueeze(1).broadcast_to([P, GB, D]),
                                                   T["maskf"][:, ds(e * GB, GB)].unsqueeze(2)
                                                   .broadcast_to([P, GB, D]), ALU.mult))
                        st.did(pool.tensor_tensor(typed[:], typed[:],
                                                  T["pos0"][:].unsqueeze(1).broadcast_to([P, GB, D]), ALU.add))
                        st.wait_apart()
                        if isinstance(e, int):
                            pool.wait_ge(T["gathered"][e], 16 * GB)
                        pool.tensor_tensor(hg(e), hg(e), typed[:], ALU.add).then_inc(emb_added, 1)
                    if s == 1:
                        rsqrt(evar, e * 2 + 1, rs[:], ve[:], erstd)
                    if s == 2:
                        wait_apart(pool, erstd, e * 2 + 1)
                        st = Steps(pool, pool_steps, e, 5, start=2)
                        st.did(pool.tensor_tensor(hg(e), hg(e), tiles(mv[:, :, 0]), ALU.subtract))
                    if 3 <= s <= 5:
                        st = Steps(pool, pool_steps, e, 5, start=s)
                        st.wait_apart()
                        b, op = {3: (tiles(rs[:]), ALU.mult), 4: (columns(T["gamma"]), ALU.mult),
                                 5: (columns(T["beta"]), ALU.add)}[s]
                        last = pool.tensor_tensor(hg(e), hg(e), b, op)
                        if s < 5:
                            st.did(last)
                        else:
                            last.then_inc(h0_ready, 1)
                    if s == 6:
                        rsqrt(evar, e * 2 + 2, rs[:], ve[:], erstd)

                def rsqrt(ready, value, out, of, done):
                    pool.wait_ge(ready, value)
                    pool.tensor_tensor(out, of, half[:], ALU.pow).then_inc(done, 1)

                def turn(e, a, d):
                    for s in range(NC + 3):
                        if d is not None and s >= 3:
                            c = s - 3
                            rsqrt(svar_ready, d * NC + c + 1, urs[:, c % 2, :], uve[:, c % 2, :], srstd_ready)
                        if e is not None:
                            embed(e, s)
                        if a is not None and s == 8:
                            rsqrt(xvar, a + 1, xrs[:], xve[:], xrstd)
                        if isinstance(e, int) and e in (0, 1) and s == 5:
                            pool.wait_ge(phi_squares, e + 1)
                            pool.tensor_tensor(T["phi_norm"][:, e, :], T["phi_norm"][:, e, :], T["half16"][:],
                                               ALU.pow).then_inc(phi_powed, 1)
                        if isinstance(e, int) and e == 2 and s < 10:
                            gather(3 * GB + 2 * s, 2, T["gathered"][3])
                    if isinstance(e, int) and e == 1:
                        gather(2 * GB, GB, T["gathered"][2])
                    if isinstance(e, int) and e == 2:
                        pool.wait_ge(T["gathered"][3], 16 * (NB - 3 * GB))

                def gather(first, n, done):
                    for b in range(first, first + n):
                        pool.indirect_dma_start(
                            out=h[:, b, :], out_offset=None, in_=T["tok"],
                            in_offset=bass.IndirectOffsetOnAxis(ap=T["ids"][:, b:b + 1], axis=0),
                        ).then_inc(done, 16)

                turns(pool, turn)

            @block.vector
            def _(dve):
                dve.memset(x3[:, :, 0:1], 1.0)

                def embed(e, s):
                    if s == 1:
                        wait_apart(dve, emb_added, e + 1)
                        norm_stats(dve, Steps(dve, emb_steps, e, 4 * GB), hg(e), st6, mv, ve, evar)
                    if s == 6:
                        wait_apart(dve, h0_ready, e + 1)
                        norm_stats(dve, Steps(dve, emb_steps, e, 4 * GB, start=2 * GB), hg(e), st6, mv, ve, evar)
                    if s == 7:
                        dve.wait_ge(erstd, e * 2 + 2)
                        past(dve, product, (e - 1) * 10 + 2)
                        for j in range(GB):
                            last = dve.tensor_scalar(xn[:, j, :], h[:, ds(e * GB + j, 1), :], mv[:, j, 0:1],
                                                     rs[:, j:j + 1], ALU.subtract, ALU.mult)
                        last.then_inc(xn_ready, 1)

                def attn(a, s):
                    if s == 3:
                        dve.wait_ge(product, a * 10 + 7)
                        dve.tensor_tensor(sm[:], group4(bank[:, 7, :]),
                                          T["causal"][:].unsqueeze(1).broadcast_to([P, GB, P]),
                                          ALU.add).then_inc(dve_took, 1)
                        dve.wait_ge(dve_took, a * 3 + 1)
                        dve.tensor_reduce(nmx[:], sm[:], AX_X, ALU.max, negate=True).then_inc(score_max, 1)
                    if s in (6, 7):
                        k = s - 6
                        if k == 0:
                            dve.wait_ge(exp_done, a + 1)
                            Steps(dve, attn_steps, a, 1).link(dve.reciprocal(rinv[:], ssum[:]))
                        dve.wait_ge(product, a * 10 + 9 + k)
                        for j in (2 * k, 2 * k + 1):
                            x = h[:, ds(a * GB + j, 1), :].rearrange("p a d -> p (a d)")
                            o = bank[:, 7, (j % 2) * D:(j % 2) * D + D]
                            last = dve.scalar_tensor_tensor(x, o, rinv[:, j:j + 1], x, ALU.mult, ALU.add)
                        last.then_inc(dve_took, 1)
                    if s == 8:
                        wait_apart(dve, dve_took, a * 3 + 3)
                        norm_stats(dve, Steps(dve, x3_steps, a, 2 * GB + 1), hg(a), xst6, xmv, xve, xvar)
                    if s == 9:
                        dve.wait_ge(xrstd, a + 1)
                        past(dve, slots_sum, a * NC + PRIME if not isinstance(a, int) or a > 0 else 0)
                        for j in range(GB):
                            last = dve.tensor_scalar(x3[:, j, 2:2 + D], h[:, ds(a * GB + j, 1), :], xmv[:, j, 0:1],
                                                     xrs[:, j:j + 1], ALU.subtract, ALU.mult)
                        Steps(dve, x3_steps, a, 2 * GB + 1, start=2 * GB).link(last)
                        dve.tensor_copy(x3[:, :, 2 + D:], x3[:, :, 2 + P:2 + D]).then_inc(x3_ready, 1)
                        dve.tensor_reduce(x3[:, :, 1:2], x3[:, :, 2:2 + D], AX_X, ALU.add).then_inc(x3_ready, 1)

                def column_max(d, c):
                    dve.wait_ge(logits, d * NC + c + 1)
                    dve.tensor_reduce(nmc[:, c % 2, :], group4(logits_bank(c)), AX_X, ALU.max,
                                      negate=True).then_inc(col_max, 1)

                def slot_var(d, c, sl):
                    dve.wait_ge(stats_ready, d * NC + c + 1)
                    s, m = usum[:, c % 2, :, 0], usum[:, c % 2, :, 1]
                    sl.did(dve.scalar_tensor_tensor(q1[:, c % 2, :], s, EPS, s, ALU.mult, ALU.mult))
                    sl.did(dve.scalar_tensor_tensor(q2[:, c % 2, :], m, -1.0 / (D * D), m, ALU.mult, ALU.mult))
                    sl.did(dve.tensor_scalar(umean[:, c % 2, :], m, 1.0 / D, None, ALU.mult))
                    sl.wait()
                    sl.link(dve.tensor_tensor(q1[:, c % 2, :], q1[:, c % 2, :], q2[:, c % 2, :], ALU.add))
                    dve.tensor_tensor(uve[:, c % 2, :], q1[:, c % 2, :], uss[:, c % 2, :], ALU.add).then_inc(svar_ready, 1)

                def slot_norm(d, c):
                    u = U[c % 2]
                    dve.wait_ge(srstd_ready, d * NC + c + 1)
                    dve.wait_ge(stored[c % 2], 16 * (d * (NC // 2) + c // 2) + 1)
                    for j in range(GB):
                        last = dve.tensor_scalar(stage[:, c % 2, j, :], u[:, j // 2, j % 2, 2:2 + D],
                                                 umean[:, c % 2, j:j + 1], urs[:, c % 2, j:j + 1],
                                                 ALU.subtract, ALU.mult)
                    last.then_inc(stage_ready, 1)

                def last_norms(d):
                    slot_norm(d, NC - 2)
                    slot_norm(d, NC - 1)

                def turn(e, a, d):
                    if d is not None:
                        sl = Steps(dve, slot_steps, d, 4 * NC)
                        here = ds(d * GB * P, GB * P)
                        dve.wait_ge(x3T_act, d * 2 + 1)
                        dve.tensor_tensor(T["x_lo"][:, here], bank[:, 0, :], T["x_hi"][:, here].bitcast(F32),
                                          ALU.subtract)
                        dve.wait_ge(x3T_act, d * 2 + 2)
                        dve.scalar_tensor_tensor(T["x_hi_over_lo"][:, here], xhi1[:].bitcast(F32),
                                                 T["minus_upper"][:, 0:1], bank[:, 1, :],
                                                 ALU.mult, ALU.add).then_inc(x_split, 1)
                        if not isinstance(d, int) or d > 0:
                            last_norms(d - 1)
                    for s in range(NC + 2):
                        if d is not None and s < NC:
                            if s >= 4:
                                slot_norm(d, s - 4)
                            if s >= 3:
                                slot_var(d, s - 3, sl)
                            column_max(d, s)
                        if s == 9:
                            if d is not None:
                                slot_norm(d, s - 4)
                            if a is not None:
                                attn(a, s)
                            if d is not None:
                                slot_var(d, NC - 2, sl)
                                slot_var(d, NC - 1, sl)
                        if d is not None and s == NC:
                            slot_norm(d, s - 4)
                        if d is not None and s == NC:
                            slot_var(d, s - 3, sl)
                        if a is not None and s != 9:
                            attn(a, s)
                        if e is not None:
                            embed(e, s)
                    if d is not None:
                        sl.end()
                    if isinstance(e, int) and e in (0, 1):
                        dve.wait_ge(phi_powed, e + 1)
                        phi = T[f"phiT{e}"][:].rearrange("d (n p) -> d n p", p=SP_E)
                        dve.tensor_tensor(phi, phi, T["phi_norm"][:, e:e + 1, :].broadcast_to([P, NE0, SP_E]),
                                          ALU.mult).then_inc(phi_scaled, 1)
                        dve.wait_ge(phi_hi_ready, e + 1)
                        dve.tensor_tensor(T[f"phi_lo{e}"][:], T[f"phiT{e}"][:], T[f"phi_hi{e}"][:].bitcast(F32),
                                          ALU.subtract).then_inc(phi_ready, 1)

                st = Steps(dve, phi_steps)
                dve.wait_ge(T["phi_in"], 48)
                for k in range(2):
                    st.link(dve.tensor_tensor(phi_sq[:], T[f"phiT{k}"][:], T[f"phiT{k}"][:], ALU.mult))
                    norm = T["phi_norm"][:, k, :]
                    st.link(dve.tensor_reduce(norm, phi_sq[:].rearrange("d (n p) -> d p n", p=SP_E), AX_X, ALU.add))
                    dve.tensor_scalar(norm, norm, EPS_PHI, None, ALU.add).then_inc(phi_squares, 1)
                turns(dve, turn)
                last_norms(NG - 1)

            @block.scalar
            def _(act):
                b7 = bank[:, 7, :]

                def take(a, n, dst, src):
                    act.wait_ge(product, a * 10 + n)
                    act.activation(dst, src, ACT.Copy).then_inc(act_took, 1)

                def first_products(e, s):
                    if s == 8:
                        take(e, 1, xT0[:], b7)
                    if s == 9:
                        take(e, 2, xT1[:], b7[0:DR])

                def attn(a, s):
                    if s in (1, 2):
                        k = s - 1
                        take(a, 5 + k, v[:, 2 * k:2 * k + 2, :], b7[:, 0:2 * D].rearrange("p (j d) -> p j d", j=2))
                    if s == 4:
                        act.wait_ge(score_max, a + 1)
                        for j in range(GB):
                            last = act.activation(ex[:, j, :], sm[:, j, :], ACT.Exp, bias=nmx[:, j:j + 1],
                                                  accum_out=ssum[:, j:j + 1])
                        last.then_inc(exp_done, 1)
                    if s == 5:
                        take(a, 8, pT[:], b7)

                def exps(d, c):
                    act.wait_ge(col_max, d * NC + c + 1)
                    act.wait_ge(turned, d * NC + c - 1 + PRIME)
                    for j in range(GB):
                        js = slice(j * P, (j + 1) * P)
                        last = act.activation(ls[:, c % 2, js], logits_bank(c)[:, js], ACT.Exp, bias=nmc[:, c % 2, j:j + 1])
                    last.then_inc(exped, 1)

                def take_turned(d, c):
                    act.wait_ge(turned, d * NC + c + 1 + PRIME)
                    act.wait_ge(slots_sum, d * NC + c - 1 + PRIME)
                    act.activation(disp[:, c % 2, :], bank[:, 1, :], ACT.Copy).then_inc(disp_ready, 1)

                def stats(d, c, st):
                    u = U[c % 2]
                    act.wait_ge(slots_sum, d * NC + c + 1 + PRIME)
                    st.wait()
                    for j in range(GB):
                        st.did(act.activation(usq[:, j, :], u[:, j // 2, j % 2, 2:2 + D], ACT.Square,
                                               scale=float(D) ** -0.5,
                                               accum_out=uss[:, c % 2, j:j + 1]))
                    act.activation(usum[:, c % 2, :, :].rearrange("p (k j) s -> p k j s", k=2),
                                   u[:, :, :, 0:2], ACT.Copy).then_inc(stats_ready, 1)

                def turn(e, a, d):
                    if d is not None:
                        st = Steps(act, act_steps, d, GB * NC, start=1)
                        act.wait_ge(x3T_product, d * 2 + 1)
                        act.activation(T["x_hi"][:, ds(d * GB * P, GB * P)], bank[:, 0, :],
                                       ACT.Copy).then_inc(x3T_act, 1)
                        act.wait_ge(x3T_product, d * 2 + 2)
                        past(act, x_split, d)
                        act.activation(xhi1[:], bank[:, 1, :], ACT.Copy).then_inc(x3T_act, 1)
                    if a is not None:
                        take(a, 4, qT1[:], b7[0:DR])
                    for s in range(NC + 2):
                        if d is not None:
                            if 1 <= s <= NC:
                                take_turned(d, s - 1)
                            if s < NC:
                                exps(d, s)
                        if e is not None and s == 9:
                            first_products(e, s)
                        if d is not None and s >= 2:
                            stats(d, s - 2, st)
                        if a is not None:
                            attn(a, s)
                        if e is not None and s == 8:
                            first_products(e, s)
                    if e is not None:
                        take(e, 3, qT0[:], b7)
                    if d is not None:
                        st.end()
                    if isinstance(e, int) and e in (0, 1):
                        act.wait_ge(phi_scaled, e + 1)
                        act.activation(T[f"phi_hi{e}"][:], T[f"phiT{e}"][:], ACT.Copy).then_inc(phi_hi_ready, 1)

                act.sem_inc(act_steps, 1)
                turns(act, turn)

            @block.tensor
            def _(pe):
                pe.sem_inc(turned, PRIME)
                pe.sem_inc(slots_sum, PRIME)
                b7 = bank[:, 7, :]

                def done(ins):
                    ins.then_inc(product, 1)

                def turn_x(e, k):
                    if k == 0:
                        pe.wait_ge(xn_ready, e + 1)
                        past(pe, dve_took, e * 3)
                    else:
                        wait_apart(pe, act_took, e * 7 + 1)
                    rows = P if k == 0 else DR
                    for j in range(GB):
                        last = pe.transpose(b7[0:rows, j * P:(j + 1) * P], xn[:, j, k * P:k * P + rows], ident[:])
                    done(last)

                def queries(g, k):
                    pe.wait_ge(act_took, g * 7 + 2 + k)
                    c = slice(0, P) if k == 0 else slice(P, D)
                    done(matmuls(pe, b7[0:c.stop - c.start], [(T["M0"][:, c], xT0[:]), (T["M1"][:, c], xT1[:])]))

                def attn(a, s):
                    if s in (1, 2):
                        pe.wait_ge(act_took, a * 7 + 3 + s)
                        for j in (2 * s - 2, 2 * s - 1):
                            last = matmuls(pe, b7[:, (j % 2) * D:(j % 2) * D + D],
                                           [(xT0[:, j * P:(j + 1) * P], T["Wv0"][:]),
                                            (xT1[:, j * P:(j + 1) * P], T["Wv1"][:])])
                        done(last)
                    if s == 3:
                        pe.wait_ge(act_took, a * 7 + 6)
                        for j in range(GB):
                            c = slice(j * P, (j + 1) * P)
                            last = matmuls(pe, b7[:, c], [(qT0[:, c], xT0[:, c]), (qT1[:, c], xT1[:, c])])
                        done(last)
                    if s == 5:
                        pe.wait_ge(dve_took, a * 3 + 1)
                        pe.wait_ge(exp_done, a + 1)
                        for j in range(GB):
                            last = pe.transpose(b7[:, j * P:(j + 1) * P], ex[:, j, :], ident[:])
                        done(last)
                    if s in (6, 7):
                        if s == 6:
                            pe.wait_ge(act_took, a * 7 + 7)
                        else:
                            pe.wait_ge(dve_took, a * 3 + 2)
                        for j in (2 * s - 12, 2 * s - 11):
                            last = pe.matmul(b7[:, (j % 2) * D:(j % 2) * D + D], pT[:, j * P:(j + 1) * P], v[:, j, :],
                                             start=True, stop=True)
                        done(last)

                def turn_x3(d):
                    pe.wait_ge(x3_ready, d * 2 + 1)
                    for k in range(2):
                        for j in range(GB):
                            last = pe.transpose(bank[:, k, j * P:(j + 1) * P],
                                                x3[:, j, 2 + k * P:2 + (k + 1) * P], ident[:])
                        last.then_inc(x3T_product, 1)

                def logits_of(d, c):
                    if c == 0:
                        pe.wait_ge(x_split, d + 1)
                    else:
                        past(pe, exped, d * NC + c - 1)
                    if isinstance(d, int) and d == 0 and c == 0:
                        pe.wait_ge(phi_ready, 2)
                    cs = slice(c * P, (c + 1) * P)
                    hi, lo, both = [T[n][:, ds(d * GB * P, GB * P)] for n in ("x_hi", "x_lo", "x_hi_over_lo")]
                    matmuls(pe, logits_bank(c), [
                        (T["phi_hi0"][:, cs], hi), (T["phi_lo0"][:, cs], hi), (T["phi_hi0"][:, cs], lo),
                        (T["phi_hi1"][:, cs], both), (T["phi_lo1"][:, cs], both)]).then_inc(logits, 1)

                def turn_weights(d, c):
                    pe.wait_ge(exped, d * NC + c + 1)
                    if c >= 1:
                        pe.wait_ge(disp_ready, d * NC + c)
                    for j in range(GB):
                        last = pe.transpose(bank[:, 1, j * P:(j + 1) * P],
                                            ls[:, c % 2, j * P:(j + 1) * P], ident[:])
                    last.then_inc(turned, 1)

                def slot_sums(d, c):
                    pe.wait_ge(disp_ready, d * NC + c + 1)
                    past(pe, stage_ready, d * NC + c - 1)
                    if c == 0:
                        pe.wait_ge(x3_ready, d * 2 + 2)
                    for j in range(GB):
                        last = pe.matmul(U[c % 2][:, j // 2, j % 2, :], disp[:, c % 2, j * P:(j + 1) * P],
                                         x3[:, j, 0:2 + D], start=True, stop=True)
                    last.then_inc(slots_sum, 1)

                def turn(e, a, d):
                    if d is not None:
                        turn_x3(d)
                    if a is not None:
                        queries(a, 1)
                    for s in range(NC + 2):
                        if d is not None:
                            if s < NC:
                                logits_of(d, s)
                            if 1 <= s <= NC:
                                turn_weights(d, s - 1)
                        if e is not None and s == 9:
                            turn_x(e, 1)
                        if d is not None and s >= 2:
                            slot_sums(d, s - 2)
                        if a is not None:
                            attn(a, s)
                        if e is not None and s == 8:
                            turn_x(e, 0)
                    if e is not None:
                        queries(e, 0)

                turns(pe, turn)

            @block.sync
            def _(sp):
                for k in range(2):
                    sp.sem_inc(stored[k], 1)
                with sp.Fori(0, NG) as g:
                    for c in range(NC):
                        sp.wait_ge(stage_ready, g * NC + c + 1)
                        sp.dma_start(T["xs"][c * P:(c + 1) * P, ds(g * GB, GB), :],
                                     stage[:, c % 2, :, :]).then_inc(stored[c % 2], 16)
                for k in range(2):
                    sp.wait_ge(stored[k], 16 * NG * NC // 2 + 1)
                sp.wait_ge(T["xm_filled"], 16 * NE1 * CAP // (4 * P))
        al.free_sems()


def past(eng, sem, value, wait=None):
    if not isinstance(value, int) or value > 0:
        if wait:
            wait(eng, sem, value)
        else:
            eng.wait_ge(sem, value)


def expert_phase(nc, T, name, n_exp, hid, src, dst, w1, b1T, w2, b2, act_fn, ln=None, routed_to=None):
    MT = hid // P
    turns = n_exp // 2
    routed = routed_to is not None
    tag = TAG if routed else 0
    with ExitStack() as ctx:
        al = Alloc(nc, ctx)
        sb = lambda n, *a: al.sb(f"{name}_{n}", *a)
        sem = lambda n: al.sem(f"{name}_{n}")
        bank, ident = T["bank"], T["ident"]
        rows = [sb(f"rows{u}", [P, 4, D + DR]) for u in range(2)]
        w1raw = [sb(f"w1raw{u}", [P, 2, hid]) for u in range(2)]
        w1hi = [sb(f"w1hi{u}", [P, 2, hid], F32R) for u in range(2)]
        w1lo = [sb(f"w1lo{u}", [P, 2, hid], F32R) for u in range(2)]
        w2raw = [sb(f"w2raw{u}", [P, MT, D]) for u in range(2)]
        w2p = [sb(f"w2_hi_lo{u}", [P, MT, 2, D], F32R) for u in range(2)]
        w2hi, w2lo = [w[:, :, 0, :] for w in w2p], [w[:, :, 1, :] for w in w2p]
        b1s = sb("b1", [P, MT, n_exp])
        b2s = [sb(f"b2_{u}", [P, D]) for u in range(2)]
        stage = [sb(f"stage{u}", [P, 4, D]) for u in range(2)]
        ysum = [sb(f"ysum{u}", [P, 4, D]) for u in range(2)] if routed else stage
        xf = sb("x_full", [P, 2, 512])
        xhi = [sb(f"x_hi{u}", [P, 2, 512], F32R) for u in range(2)]
        xlo = [sb(f"x_lo{u}", [P, 512], F32R) for u in range(2)]
        xst = [sb(f"x_hi_over_lo{u}", [P, 512], F32R) for u in range(2)]
        hf = sb("h_full", [P, MT, 512])
        hhi = sb("h_hi", [P, MT, 512], F32R)
        hlo = sb("h_lo", [P, MT, 512], F32R)
        if ln is not None:
            lng, lnb = sb("ln_gain", [P, 2, n_exp]), sb("ln_shift", [P, 2, n_exp])
        rows_in, w_in = [sem(f"rows_in{u}") for u in range(2)], [sem(f"weights_in{u}") for u in range(2)]
        b2_in, stored = [sem(f"b2_in{u}") for u in range(2)], [sem(f"stored{u}") for u in range(2)]
        small_in = sem("small_in")
        w1_hi_ready, w2_hi_ready = sem("w1_hi_ready"), sem("w2_hi_ready")
        w1_split, w2_split = sem("w1_split"), sem("w2_split")
        act_steps, vec_steps = sem("act_steps"), sem("vector_steps")
        turned, w1_done, w2_done = sem("turned"), sem("w1_product"), sem("w2_product")
        x_taken, x_hi_ready, x_split = sem("x_taken"), sem("x_hi_ready"), sem("x_split")
        acted, h_split, y_added = sem("acted"), sem("h_split"), sem("y_added")
        h0_hi_ready, h0_split = sem("h0_hi_ready"), sem("h0_split")
        lo_sign = T["minus_upper"]
        if routed:
            tags = [sb(f"tags{u}", [P, 4, TAG]) for u in range(2)]
            numbers = [sb(f"token_numbers{u}", [P, 4, 1], I32) for u in range(2)]
            tags_in, gated = [sem(f"tags_in{u}") for u in range(2)], sem("gated")

        def f32(ap):
            return ap.bitcast(F32)

        def hbank(u, m):
            return bank[:, 2 + (u * MT + m) % 2, :]

        def each_pair(eng, turn):
            turn(0)
            with eng.Fori(1, turns - 1) as i:
                turn(i)
            turn(turns - 1)

        with nc.Block() as block:

            @block.sync
            def _(sp):
                def load_rows(n, u):
                    past(sp, turned, 2 * (n - 1))
                    x = src[ds(n * 512, 512), :].rearrange("(p j) d -> p j d", j=4)
                    sp.dma_start(rows[u][:, :, 0:D], x[:, :, tag:]).then_inc(rows_in[u], 16)
                    sp.dma_start(rows[u][:, :, D:], x[:, :, tag + P:tag + D]).then_inc(rows_in[u], 16)

                def load_weights(n, u):
                    past(sp, w2_split, n - 1)
                    w = w1[ds(n, 1), :, :].rearrange("a d h -> (a d) h")
                    sp.dma_start(w1raw[u][:, 0, :], w[0:P]).then_inc(w_in[u], 16)
                    sp.dma_start(w1raw[u][0:DR, 1, :], w[P:D]).then_inc(w_in[u], 16)
                    sp.dma_start(w1raw[u][DR:P, 1, :], w[P:D]).then_inc(w_in[u], 16)
                    sp.dma_start(w2raw[u][:], w2[ds(n, 1), :, :].rearrange("a (k p) d -> p (a k) d", p=P)
                                 ).then_inc(w_in[u], 16)

                def turn(i):
                    for u in range(2):
                        n = i * 2 + u
                        if not isinstance(n, int) or n > 1:
                            load_rows(n, u)
                            load_weights(n, u)

                load_rows(0, 0)
                if ln is not None:
                    for t, g in ((lng, ln[0]), (lnb, ln[1])):
                        sp.dma_start(t[:, 0, :], g[0:P]).then_inc(small_in, 16)
                        sp.dma_start(t[0:DR, 1, :], g[P:D]).then_inc(small_in, 16)
                        sp.dma_start(t[DR:P, 1, :], g[P:D]).then_inc(small_in, 16)
                load_weights(0, 0)
                sp.dma_start(b1s[:], b1T).then_inc(small_in, 16)
                load_rows(1, 1)
                load_weights(1, 1)
                each_pair(sp, turn)

            @block.gpsimd
            def _(pool):
                def weights_lo(n, u):
                    pool.wait_ge(w1_hi_ready, n + 1)
                    pool.tensor_tensor(w1lo[u][:], w1raw[u][:], f32(w1hi[u][:]),
                                       ALU.subtract).then_inc(w1_split, 1)
                    pool.wait_ge(w2_hi_ready, n + 1)
                    pool.tensor_tensor(w2lo[u], w2raw[u][:], f32(w2hi[u]), ALU.subtract).then_inc(w2_split, 1)

                def turn(i):
                    for u in range(2):
                        n = i * 2 + u
                        pool.wait_ge(h0_hi_ready, n + 1)
                        pool.tensor_tensor(hlo[:, 0, :], hf[:, 0, :], f32(hhi[:, 0, :]),
                                           ALU.subtract).then_inc(h0_split, 1)
                        if not isinstance(n, int) or n + 1 < n_exp:
                            weights_lo(n + 1, 1 - u)
                        if routed and (not isinstance(n, int) or n > 0):
                            add_rows(n - 1, 1 - u)

                def add_rows(n, u):
                    wait_apart(pool, gated, n + 1)
                    for j in range(4):
                        pool.indirect_dma_start(
                            out=routed_to, out_offset=bass.IndirectOffsetOnAxis(ap=numbers[u][:, j, :], axis=0),
                            in_=ysum[u][:, j, :], in_offset=None, bounds_check=NB * P - 1, oob_is_err=False,
                            compute_op=ALU.add).then_inc(stored[u], 16)

                weights_lo(0, 0)
                each_pair(pool, turn)
                if routed:
                    add_rows(n_exp - 1, 1)
                    for u in range(2):
                        pool.wait_ge(stored[u], 64 * turns)

            @block.tensor
            def _(pe):
                def turn_rows(n, u):
                    pe.wait_ge(rows_in[u], 32 * (n // 2 + 1) if isinstance(n, int) else (n - u) * 16 + 32)
                    past(pe, x_taken, 2 * n)
                    for k in range(2):
                        for j in range(4):
                            last = pe.transpose(bank[:, k, j * P:(j + 1) * P],
                                                rows[u][:, j, k * P:(k + 1) * P], ident[:])
                        last.then_inc(turned, 1)

                def turn(i):
                    for u in range(2):
                        n = i * 2 + u
                        pe.wait_ge(x_split, n + 1)
                        pe.wait_ge(w1_split, n + 1)
                        for m in range(MT):
                            past(pe, acted, n * MT + m - 1)
                            ms = slice(m * P, (m + 1) * P)
                            matmuls(pe, hbank(u, m), [
                                (w1hi[u][:, 0, ms], xhi[u][:, 0, :]), (w1lo[u][:, 0, ms], xhi[u][:, 0, :]),
                                (w1hi[u][:, 0, ms], xlo[u][:]), (w1hi[u][:, 1, ms], xst[u][:]),
                                (w1lo[u][:, 1, ms], xst[u][:])]).then_inc(w1_done, 1)
                        if not isinstance(n, int) or n + 2 < n_exp:
                            turn_rows(n + 2, u)
                        pe.wait_ge(w2_split, n + 1)
                        past(pe, y_added, n)
                        for k in range(MT):
                            if k == 0:
                                pe.wait_ge(h0_split, n + 1)
                            else:
                                pe.wait_ge(h_split, n * (MT - 1) + k)
                            for j in range(4):
                                js = slice(j * P, (j + 1) * P)
                                both = w2p[u][:, k, :, :].rearrange("p q d -> p (q d)")
                                if k == 0:
                                    pe.matmul(bank[:, 4 + j, 0:2 * D], hhi[:, k, js], both, start=True, stop=False)
                                last = pe.matmul(bank[:, 4 + j, 0:D], hlo[:, k, js], w2hi[u][:, k, :],
                                                 start=False, stop=False)
                                if k > 0:
                                    last = pe.matmul(bank[:, 4 + j, 0:2 * D], hhi[:, k, js], both,
                                                     start=False, stop=k == MT - 1)
                        last.then_inc(w2_done, 1)

                turn_rows(0, 0)
                turn_rows(1, 1)
                each_pair(pe, turn)

            @block.scalar
            def _(act):
                def load_b2(n, u):
                    act.dma_start(b2s[u][:], b2[ds(n, 1), :].rearrange("a d -> (a d)").partition_broadcast(P)
                                  ).then_inc(b2_in[u], 16)

                def load_tags(n, u):
                    past(act, gated, n - 1)
                    act.dma_start(tags[u][:], src[ds(n * 512, 512), 0:TAG].rearrange("(p j) d -> p j d", j=4)
                                  ).then_inc(tags_in[u], 16)

                def weights_hi(n, u, i):
                    act.wait_ge(w_in[u], 64 * (i + 1))
                    past(act, w1_done, (n - 1) * MT)
                    act.activation(w1hi[u][:], w1raw[u][:], ACT.Copy).then_inc(w1_hi_ready, 1)
                    past(act, w2_done, n - 1)
                    act.activation(w2hi[u], w2raw[u][:], ACT.Copy).then_inc(w2_hi_ready, 1)

                def take_x(n, u):
                    for k in range(2):
                        act.wait_ge(turned, 2 * n + k + 1)
                        past(act, x_split, n)
                        if ln is None:
                            last = act.activation(xf[:, k, :], bank[:, k, :], ACT.Copy)
                        else:
                            last = act.activation(xf[:, k, :], bank[:, k, :], ACT.Identity,
                                                  bias=lnb[:, k, ds(n, 1)], scale=lng[:, k, ds(n, 1)])
                        last.then_inc(x_taken, 1)
                    act.wait_ge(x_taken, 2 * n + 2)
                    past(act, w1_done, (n - 1) * MT)
                    act.activation(xhi[u][:], xf[:], ACT.Copy).then_inc(x_hi_ready, 1)

                def send(n, u):
                    act.wait_ge(y_added, n + 1)
                    if routed:
                        past(act, gated, n - 1)
                        act.activation(stage[u][:], ysum[u][:], act_fn).then_inc(act_steps, 1)
                    else:
                        act.dma_start(dst[ds(n * 512, 512), :].rearrange("(p j) d -> p j d", j=4),
                                      stage[u][:]).then_inc(stored[u], 16)

                def turn(i):
                    for u in range(2):
                        n = i * 2 + u
                        if not isinstance(n, int) or n + 1 < n_exp:
                            weights_hi(n + 1, 1 - u, i + u)
                        for m in range(MT):
                            act.wait_ge(w1_done, n * MT + m + 1)
                            if m == 0:
                                past(act, h0_split, n)
                            else:
                                past(act, h_split, (n - 1) * (MT - 1) + m)
                            act.activation(hf[:, m, :], hbank(u, m), act_fn,
                                           bias=b1s[:, m, ds(n, 1)]).then_inc(acted, 1)
                        if not isinstance(n, int) or n > 0:
                            send(n - 1, 1 - u)
                        if routed:
                            load_tags(n, u)
                        if not isinstance(n, int) or n + 1 < n_exp:
                            load_b2(n + 1, 1 - u)
                        if not isinstance(n, int) or n + 2 < n_exp:
                            take_x(n + 2, u)

                load_b2(0, 0)
                act.wait_ge(small_in, 16 * (1 if ln is None else 7))
                take_x(0, 0)
                weights_hi(0, 0, 0)
                take_x(1, 1)
                each_pair(act, turn)
                send(n_exp - 1, 1)
                if not routed:
                    for u in range(2):
                        act.wait_ge(stored[u], 16 * turns)

            @block.vector
            def _(dve):
                def split_x(n, u):
                    dve.wait_ge(x_hi_ready, n + 1)
                    dve.tensor_tensor(xlo[u][:], xf[:, 0, :], f32(xhi[u][:, 0, :]), ALU.subtract)
                    dve.scalar_tensor_tensor(xst[u][:], f32(xhi[u][:, 1, :]), lo_sign[:, 0:1], xf[:, 1, :],
                                             ALU.mult, ALU.add).then_inc(x_split, 1)

                def turn(i):
                    st = Steps(dve, vec_steps, i, 2 * MT)
                    for u in range(2):
                        n = i * 2 + u
                        for m in range(MT):
                            dve.wait_ge(acted, n * MT + m + 1)
                            if m == 0:
                                past(dve, w2_done, n)
                            if m == 0:
                                dve.tensor_copy(hhi[:, m, :], hf[:, m, :]).then_inc(h0_hi_ready, 1)
                                if not isinstance(n, int) or n + 1 < n_exp:
                                    split_x(n + 1, 1 - u)
                            else:
                                st.link(dve.tensor_copy(hhi[:, m, :], hf[:, m, :]))
                                dve.tensor_tensor(hlo[:, m, :], hf[:, m, :], f32(hhi[:, m, :]),
                                                  ALU.subtract).then_inc(h_split, 1)
                        if routed and (not isinstance(n, int) or n > 0):
                            gate(n - 1, 1 - u, i - 1 + u)
                        dve.wait_ge(w2_done, n + 1)
                        dve.wait_ge(b2_in[u], 16 * (i + 1))
                        past(dve, stored[u], (64 if routed else 16) * i)
                        st.link(dve.tensor_tensor(ysum[u][:], bank[:, 4:8, 0:D],
                                                  b2s[u][:].unsqueeze(1).broadcast_to([P, 4, D]), ALU.add))
                        dve.tensor_tensor(ysum[u][:], ysum[u][:], bank[:, 4:8, D:2 * D],
                                          ALU.add).then_inc(y_added, 1)
                    st.end()

                def gate(n, u, i):
                    dve.wait_ge(tags_in[u], 16 * (i + 1))
                    dve.tensor_copy(numbers[u][:], tags[u][:, :, 1:2])
                    dve.wait_ge(act_steps, n + 1)
                    dve.tensor_tensor(ysum[u][:], stage[u][:], tags[u][:, :, 0:1].broadcast_to([P, 4, D]),
                                      ALU.mult).then_inc(gated, 1)

                split_x(0, 0)
                each_pair(dve, turn)
                if routed:
                    gate(n_exp - 1, 1, turns - 1)


def combine_phase(nc, ins, T):
    with ExitStack() as ctx:
        al = Alloc(nc, ctx)
        sb, sem = al.sb, al.sem
        bank, ident, h, half = T["bank"], T["ident"], T["h"], T["half"]
        xc_hi, xc_lo, xc_both = (sb(n, [P, P], F32R) for n in ("xc_hi", "xc_lo", "xc_hi_over_lo"))
        ysb = [sb(f"slot_out{u}", [P, NC, D]) for u in range(2)]
        nm2 = sb("half_row_max", [P, 2])
        nm, csum, cinv = sb("row_neg_max", [P, 1]), sb("row_sum", [P, 1]), sb("row_inv", [P, 1])
        comb = sb("combine_exp", [P, NS])
        chi, clo = sb("combineT_hi", [P, NC, P], F32R), sb("combineT_lo", [P, NC, P], F32R)
        yp = sb("slot_out_hi_lo", [P, NC, 2, D], F32R)
        st6, mv = sb("ln4_stats", [P, 6]), sb("ln4_mean_var", [P, 2])
        ve, rs = sb("ln4_var_eps", [P, 1]), sb("ln4_rstd", [P, 1])
        x4 = sb("x4", [P, D + DR])
        x4hi, x4lo, x4both = sb("x4T_hi", [P, 2 * P], F32R), sb("x4T_lo", [P, P], F32R), sb("x4T_hi_over_lo", [P, P], F32R)
        Wraw = sb("Wqkv", [P, 2, 3 * D])
        Whi, Wlo = sb("Wqkv_hi", [P, 2, 3 * D], F32R), sb("Wqkv_lo", [P, 2, 3 * D], F32R)
        Wp0, Wp1 = sb("Wproj0", [P, D]), sb("Wproj1", [DR, D])
        bproj = sb("bproj", [P, D])
        cos, sin = sb("rope_cos", [P, 2 * D]), sb("rope_sin", [P, 2 * D])
        straight, crossed = sb("rope_straight", [P, 2 * D]), sb("rope_crossed", [P, 2 * D])
        qk = sb("qk_padded", [P, 2 * NH, 2 * HD])
        vs = sb("v_and_one", [P, NH, HD + 1])
        qT, kT = sb("headsT_q", [P, 3 * P]), sb("headsT_k", [P, 3 * P])
        nmx = sb("head_neg_max", [P, 4, 3])
        pr = sb("probs", [P, 4, 3, P])
        pT = sb("probsT1", [P, 4, 3, P])
        oinv, o = sb("head_inv", [P, NH]), sb("attn_out", [P, D])
        oT0, oT1 = sb("oT0", [P, P]), sb("oT1", [DR, P])
        hb = sb("h_and_bias", [P, D])
        loaded = sem("attn1_weights_in")
        ys_in = [sem(f"slot_out_in{u}") for u in range(2)]
        S = {n: sem(n) for n in (
            "xc_ready", "L_done", "L_max", "L_exp", "T_done", "T_act", "T_dve", "Y_done", "h2_ready",
            "ln_var", "ln_rstd", "x4_ready", "a_done", "x4_hi_ready", "x4_split", "W_hi_ready", "W_split", "y_hi_ready", "y_split", "qk_done", "v_done", "head_max", "rope_ready",
            "v_took", "c_done", "q_took", "k_took", "S_done", "S_exp", "f_done", "f_act", "f_dve",
            "g_done", "o_ready", "h1_done", "oT_took", "p_done", "h3_ready", "hb_ready", "dve_c", "dve_a",
            "dve_o", "dve_y", "padded", "ones_set")}

        def at(b, n=1, k=0):
            return b * n + (k or n)

        def stages(t):
            if not isinstance(t, int):
                return t, t - 1, t - 2
            return tuple(b if 0 <= b < NB else None for b in (t, t - 1, t - 2))

        def each_turn(eng, turn):
            for t in range(4):
                turn(t, t % 2)
            with eng.Fori(2, NB // 2) as i:
                for u in range(2):
                    turn(i * 2 + u, u)
            for t in range(NB, NB + 2):
                turn(t, t % 2)

        def pT_flat(n):
            return pT[:].rearrange("p s g n -> p (s g n)")[:, n * 512:(n + 1) * 512]

        hb_of = lambda b: h[:, ds(b, 1), :].rearrange("p a d -> p (a d)")

        with nc.Block() as block:

            @block.sync
            def _(sp):
                for t, s in ((Wraw[:, 0, :], ins["Wqkv"][0:P]), (Wraw[0:DR, 1, :], ins["Wqkv"][P:D]),
                             (Wraw[DR:P, 1, :], ins["Wqkv"][P:D])):
                    sp.dma_start(t, s).then_inc(loaded, 16)
                for t, s in ((Wp0, ins["Wproj"][0:P]),
                             (Wp1, ins["Wproj"][P:D]), (bproj, ins["bproj"].partition_broadcast(P)),
                             (cos, ins["cos"]), (sin, ins["sin"])):
                    sp.dma_start(t[:], s).then_inc(loaded, 16)

                def turn(t, u):
                    b1, _, _ = stages(t)
                    if b1 is None:
                        return
                    past(sp, S["y_split"], b1 - 1)
                    sp.dma_start(ysb[u][:], T["ys"][:, ds(b1, 1), :].rearrange("(c p) a d -> p c (a d)", p=P)
                                 ).then_inc(ys_in[u], 16)

                each_turn(sp, turn)

            @block.gpsimd
            def _(pool):
                pool.memset(qk[:], 0.0).then_inc(S["padded"], 1)
                pool.memset(vs[:], 1.0).then_inc(S["ones_set"], 1)
                pool.wait_ge(loaded, 8 * 16)
                pool.wait_ge(S["W_hi_ready"], 1)
                pool.tensor_tensor(Wlo[:], Wraw[:], Whi[:].bitcast(F32), ALU.subtract).then_inc(S["W_split"], 1)

                def turn(t, u):
                    b1, b2, b3 = stages(t)
                    if b1 is not None:
                        past(pool, S["L_done"], 2 * b1)
                        for xc, n in ((xc_hi, "x_hi"), (xc_lo, "x_lo"), (xc_both, "x_hi_over_lo")):
                            pool.tensor_copy(xc[:], T[n][:, ds(b1 * P, P)]).then_inc(S["xc_ready"], 1)
                    if b2 is not None:
                        pool.wait_ge(S["ln_var"], at(b2))
                        pool.tensor_tensor(rs[:], ve[:], half[:, 0:1], ALU.pow).then_inc(S["ln_rstd"], 1)
                    if b1 is not None:
                        pool.wait_ge(S["y_hi_ready"], at(b1))
                        pool.tensor_tensor(yp[:, :, 1, :], ysb[u][:], yp[:, :, 0, :].bitcast(F32),
                                           ALU.subtract).then_inc(S["y_split"], 1)
                    if b3 is not None:
                        past(pool, S["h3_ready"], b3)
                        pool.tensor_tensor(hb[:], hb_of(b3), bproj[:], ALU.add).then_inc(S["hb_ready"], 1)

                each_turn(pool, turn)

            @block.tensor
            def _(pe):
                pe.wait_ge(loaded, 8 * 16)

                def turn(t, u):
                    b1, b2, b3 = stages(t)

                    def logits_half(k):
                        if k == 0:
                            pe.wait_ge(S["xc_ready"], at(b1, 3))
                            past(pe, S["h2_ready"], b1)
                        ks = slice(k * 512, (k + 1) * 512)
                        matmuls(pe, bank[:, k, :], [
                            (xc_hi[:], T["phi_hi0"][:, ks]), (xc_hi[:], T["phi_lo0"][:, ks]),
                            (xc_lo[:], T["phi_hi0"][:, ks]), (xc_both[:], T["phi_hi1"][:, ks]),
                            (xc_both[:], T["phi_lo1"][:, ks])]).then_inc(S["L_done"], 1)

                    def turn_probs():
                        pe.wait_ge(S["S_exp"], at(b3, 4))
                        for n in range(3):
                            for m in range(4):
                                s, g = divmod(n * 4 + m, 3)
                                last = pe.transpose(bank[:, 4 + n, m * P:(m + 1) * P], pr[:, s, g, :], ident[:])
                            last.then_inc(S["f_done"], 1)

                    def heads_out():
                        for n, (took, value) in enumerate(((S["f_act"], at(b3, 2, 1)), (S["f_dve"], at(b3)),
                                                           (S["f_act"], at(b3, 2)))):
                            pe.wait_ge(took, value)
                            for m in range(4):
                                s, g = divmod(n * 4 + m, 3)
                                hd = 4 * g + s
                                last = pe.matmul(bank[:, 7, hd * (HD + 1):(hd + 1) * (HD + 1)], pT[:, s, g, :],
                                                 vs[:, hd, :], start=True, stop=True)
                        last.then_inc(S["g_done"], 1)

                    def two_pieces(src, n, done):
                        pe.transpose(bank[:, n, 0:P], src[:, 0:P], ident[:])
                        pe.transpose(bank[0:DR, n, P:2 * P], src[:, P:D], ident[:]).then_inc(done, 1)

                    if b1 is not None:
                        logits_half(0)
                        logits_half(1)
                    if b3 is not None:
                        turn_probs()
                    if b2 is not None:
                        if b3 is not None:
                            pe.wait_ge(S["f_act"], at(b3, 2, 1))
                        pe.wait_ge(S["x4_ready"], at(b2))
                        for k in range(2):
                            last = pe.transpose(bank[:, 4, k * P:(k + 1) * P], x4[:, k * P:(k + 1) * P], ident[:])
                        last.then_inc(S["a_done"], 1)
                    if b3 is not None:
                        heads_out()
                    if b2 is not None:
                        pe.wait_ge(S["x4_split"], at(b2))
                        for out, c, done in ((bank[:, 6, 0:2 * D], slice(0, 2 * D), "qk_done"),
                                             (bank[:, 4, 2 * P:2 * P + D], slice(2 * D, 3 * D), "v_done")):
                            matmuls(pe, out, [
                                (x4hi[:, 0:P], Whi[:, 0, c]), (x4hi[:, 0:P], Wlo[:, 0, c]), (x4lo[:], Whi[:, 0, c]),
                                (x4both[:], Whi[:, 1, c]), (x4both[:], Wlo[:, 1, c])]).then_inc(S[done], 1)
                    if b3 is not None:
                        pe.wait_ge(S["o_ready"], at(b3))
                        two_pieces(o, 5, S["h1_done"])
                    if b1 is not None:
                        pe.wait_ge(S["L_exp"], at(b1))
                        for k in range(2):
                            for m in range(4):
                                c = 4 * k + m
                                last = pe.transpose(bank[:, 2 + k, m * P:(m + 1) * P],
                                                    comb[:, c * P:(c + 1) * P], ident[:])
                            last.then_inc(S["T_done"], 1)
                    if b3 is not None:
                        pe.wait_ge(S["oT_took"], at(b3, 2))
                        matmuls(pe, bank[:, 4, 0:D], [(oT0[:], Wp0[:]), (oT1[:], Wp1[:])]
                                ).then_inc(S["p_done"], 1)
                    if b2 is not None:
                        pe.wait_ge(S["rope_ready"], at(b2))
                        for k in range(2):
                            for g in range(3):
                                last = pe.transpose(
                                    bank[:, 5 + k, g * P:(g + 1) * P],
                                    qk[:, k * NH + 4 * g:k * NH + 4 * g + 4, :].rearrange("p a d -> p (a d)"),
                                    ident[:])
                            last.then_inc(S["c_done"], 1)
                    if b1 is not None:
                        pe.wait_ge(S["y_split"], at(b1))
                        for c in range(NC):
                            if c % 4 == 0:
                                pe.wait_ge(S["T_dve"], at(b1, 2, c // 4 + 1))
                            pe.matmul(bank[:, 0, 0:2 * D], chi[:, c, :], yp[:, c, :, :].rearrange("p q d -> p (q d)"),
                                      start=c == 0, stop=False)
                            last = pe.matmul(bank[:, 0, 0:D], clo[:, c, :], yp[:, c, 0, :],
                                             start=False, stop=c == NC - 1)
                        last.then_inc(S["Y_done"], 1)
                    if b2 is not None:
                        pe.wait_ge(S["q_took"], at(b2))
                        pe.wait_ge(S["k_took"], at(b2))
                        pe.wait_ge(S["v_took"], at(b2))
                        past(pe, S["h3_ready"], b2)
                        for s in range(4):
                            rows = slice(32 * s, 32 * s + HD)
                            for g in range(3):
                                gs = slice(g * P, (g + 1) * P)
                                last = pe.matmul(bank[:, 4 + s, gs], qT[rows, gs], kT[rows, gs],
                                                 start=True, stop=True)
                            last.then_inc(S["S_done"], 1)

                pe.wait_ge(S["W_split"], 1)
                each_turn(pe, turn)

            @block.scalar
            def _(act):
                act.wait_ge(S["ones_set"], 1)
                act.wait_ge(loaded, 8 * 16)
                act.activation(Whi[:], Wraw[:], ACT.Copy).then_inc(S["W_hi_ready"], 1)

                def ys_value(t, u):
                    return 16 * (t // 2 + 1) if isinstance(t, int) else (t - u) * 8 + 16

                def turn(t, u):
                    b1, b2, b3 = stages(t)

                    def pieces(n, d0, d1, done, took):
                        act.wait_ge(done, at(b_of))
                        act.activation(d0[:], bank[:, n, 0:P], ACT.Copy).then_inc(took, 1)
                        act.activation(d1[:], bank[0:DR, n, P:2 * P], ACT.Copy).then_inc(took, 1)

                    if b1 is not None:
                        act.wait_ge(ys_in[u], ys_value(t, u))
                        past(act, S["Y_done"], b1)
                        act.activation(yp[:, :, 0, :], ysb[u][:], ACT.Copy).then_inc(S["y_hi_ready"], 1)
                    if b3 is not None:
                        for k, n in enumerate((0, 2)):
                            act.wait_ge(S["f_done"], at(b3, 3, n + 1))
                            past(act, S["g_done"], b3)
                            act.activation(pT_flat(n), bank[:, 4 + n, :], ACT.Copy).then_inc(S["f_act"], 1)
                    if b2 is not None:
                        act.wait_ge(S["a_done"], at(b2))
                        past(act, S["v_done"], b2)
                        act.activation(x4hi[:], bank[:, 4, 0:2 * P], ACT.Copy).then_inc(S["x4_hi_ready"], 1)
                    if b1 is not None:
                        act.wait_ge(S["L_max"], at(b1))
                        past(act, S["T_done"], 2 * b1)
                        act.activation(comb[:].rearrange("p (k n) -> p k n", k=2), bank[:, 0:2, :], ACT.Exp,
                                       bias=nm[:], accum_out=csum[:]).then_inc(S["L_exp"], 1)
                    if b2 is not None:
                        act.wait_ge(S["v_done"], at(b2))
                        past(act, S["g_done"], b2)
                        act.activation(vs[:, :, 0:HD], bank[:, 4, 2 * P:2 * P + D].rearrange("p (a d) -> p a d", d=HD),
                                       ACT.Copy).then_inc(S["v_took"], 1)
                    if b3 is not None:
                        b_of = b3
                        pieces(5, oT0, oT1, S["h1_done"], S["oT_took"])
                    if b1 is not None:
                        for k in range(2):
                            act.wait_ge(S["T_done"], at(b1, 2, k + 1))
                            act.activation(chi[:, 4 * k:4 * k + 4, :], group4(bank[:, 2 + k, :]),
                                           ACT.Copy).then_inc(S["T_act"], 1)
                    if b2 is not None:
                        act.wait_ge(S["c_done"], at(b2, 2, 1))
                        past(act, S["S_done"], 4 * b2)
                        act.activation(qT[:], bank[:, 5, 0:3 * P], ACT.Copy).then_inc(S["q_took"], 1)
                        for s in range(4):
                            act.wait_ge(S["head_max"], at(b2, 4, s + 1))
                            past(act, S["f_done"], 3 * b2)
                            for g in range(3):
                                last = act.activation(pr[:, s, g, :], bank[:, 4 + s, g * P:(g + 1) * P], ACT.Exp,
                                                      bias=nmx[:, s, g:g + 1])
                            last.then_inc(S["S_exp"], 1)

                each_turn(act, turn)

            @block.vector
            def _(dve):
                dve.wait_ge(loaded, 8 * 16)
                dve.wait_ge(S["padded"], 1)

                def half_max(b, k):
                    dve.wait_ge(S["L_done"], at(b, 2, k + 1))
                    dve.tensor_reduce(nm2[:, k:k + 1], bank[:, k, :], AX_X, ALU.max).then_inc(S["dve_c"], 1)

                def turn(t, u):
                    b1, b2, b3 = stages(t)
                    if b2 is not None:
                        x = hb_of(b2)
                        wait_apart(dve, S["h2_ready"], at(b2))
                        dve.bn_stats(st6[:], x).then_inc(S["dve_a"], 1)
                        wait_apart(dve, S["dve_a"], at(b2, 5, 1))
                        dve.bn_aggr(mv[:], st6[:]).then_inc(S["dve_a"], 1)
                        dve.wait_ge(S["dve_a"], at(b2, 5, 2))
                        dve.tensor_scalar(ve[:], mv[:, 1:2], EPS, None, ALU.add).then_inc(S["ln_var"], 1)
                    if b2 is not None:
                        dve.wait_ge(S["ln_rstd"], at(b2))
                        past(dve, S["a_done"], b2)
                        dve.tensor_scalar(x4[:, 0:D], x, mv[:, 0:1], rs[:], ALU.subtract, ALU.mult)
                        dve.tensor_scalar(x4[:, D:], x[:, P:D], mv[:, 0:1], rs[:], ALU.subtract, ALU.mult
                                          ).then_inc(S["x4_ready"], 1)
                    if b1 is not None:
                        past(dve, S["L_exp"], b1)
                        half_max(b1, 0)
                    if b3 is not None:
                        dve.wait_ge(S["f_done"], at(b3, 3, 2))
                        past(dve, S["g_done"], b3)
                        dve.tensor_copy(pT_flat(1), bank[:, 5, :]).then_inc(S["f_dve"], 1)
                    if b1 is not None:
                        half_max(b1, 1)
                        dve.wait_ge(S["dve_c"], at(b1, 3, 2))
                        dve.tensor_reduce(nm[:], nm2[:], AX_X, ALU.max, negate=True).then_inc(S["L_max"], 1)
                    if b2 is not None:
                        dve.wait_ge(S["x4_hi_ready"], at(b2))
                        past(dve, S["v_done"], b2)
                        dve.tensor_tensor(x4lo[:], bank[:, 4, 0:P], x4hi[:, 0:P].bitcast(F32), ALU.subtract)
                        dve.scalar_tensor_tensor(x4both[:], x4hi[:, P:2 * P].bitcast(F32), T["minus_upper"][:, 0:1],
                                                 bank[:, 4, P:2 * P], ALU.mult, ALU.add).then_inc(S["x4_split"], 1)
                    if b3 is not None:
                        heads = bank[:, 7, 0:NH * (HD + 1)].rearrange("p (a d) -> p a d", d=HD + 1)
                        dve.wait_ge(S["g_done"], at(b3))
                        dve.reciprocal(oinv[:], heads[:, :, HD]).then_inc(S["dve_o"], 1)
                        dve.wait_ge(S["dve_o"], at(b3))
                        past(dve, S["h1_done"], b3)
                        dve.tensor_tensor(o[:].rearrange("p (a d) -> p a d", d=HD), heads[:, :, 0:HD],
                                          oinv[:].unsqueeze(2).broadcast_to([P, NH, HD]), ALU.mult
                                          ).then_inc(S["o_ready"], 1)
                    if b2 is not None:
                        src = bank[:, 6, 0:2 * D]
                        pairs = src.rearrange("p (m two) -> p m two", two=2)
                        cp = crossed[:].rearrange("p (m two) -> p m two", two=2)
                        sp_ = sin[:].rearrange("p (m two) -> p m two", two=2)
                        dve.wait_ge(S["qk_done"], at(b2))
                        dve.tensor_tensor(straight[:], src, cos[:], ALU.mult).then_inc(S["dve_a"], 1)
                        dve.tensor_tensor(cp[:, :, 0:1], pairs[:, :, 1:2], sp_[:, :, 0:1], ALU.mult
                                          ).then_inc(S["dve_a"], 1)
                        dve.tensor_tensor(cp[:, :, 1:2], pairs[:, :, 0:1], sp_[:, :, 1:2], ALU.mult
                                          ).then_inc(S["dve_a"], 1)
                        dve.wait_ge(S["dve_a"], at(b2, 5, 5))
                        past(dve, S["c_done"], 2 * b2)
                        dve.tensor_tensor(qk[:, :, 0:HD], straight[:].rearrange("p (a d) -> p a d", d=HD),
                                          crossed[:].rearrange("p (a d) -> p a d", d=HD), ALU.add
                                          ).then_inc(S["rope_ready"], 1)
                    if b1 is not None:
                        for k in range(2):
                            dve.wait_ge(S["T_act"], at(b1, 2, k + 1))
                            past(dve, S["Y_done"], b1)
                            dve.tensor_tensor(clo[:, 4 * k:4 * k + 4, :], group4(bank[:, 2 + k, :]),
                                              chi[:, 4 * k:4 * k + 4, :].bitcast(F32), ALU.subtract
                                              ).then_inc(S["T_dve"], 1)
                    if b3 is not None:
                        dve.wait_ge(S["p_done"], at(b3))
                        dve.wait_ge(S["hb_ready"], at(b3))
                        dve.tensor_tensor(hb_of(b3), bank[:, 4, 0:D], hb[:], ALU.add).then_inc(S["h3_ready"], 1)
                    if b2 is not None:
                        dve.wait_ge(S["c_done"], at(b2, 2, 2))
                        past(dve, S["S_done"], 4 * b2)
                        dve.tensor_copy(kT[:], bank[:, 6, 0:3 * P]).then_inc(S["k_took"], 1)
                    if b1 is not None:
                        dve.wait_ge(S["L_exp"], at(b1))
                        dve.reciprocal(cinv[:], csum[:]).then_inc(S["dve_c"], 1)
                        dve.wait_ge(S["dve_c"], at(b1, 3))
                        dve.wait_ge(S["Y_done"], at(b1))
                        dve.scalar_tensor_tensor(hb_of(b1), bank[:, 0, 0:D], cinv[:, 0:1], hb_of(b1),
                                                 ALU.mult, ALU.add).then_inc(S["dve_y"], 1)
                        dve.wait_ge(S["dve_y"], at(b1))
                        dve.scalar_tensor_tensor(hb_of(b1), bank[:, 0, D:2 * D], cinv[:, 0:1], hb_of(b1),
                                                 ALU.mult, ALU.add).then_inc(S["h2_ready"], 1)
                    if b2 is not None:
                        past(dve, S["S_exp"], 4 * b2)
                        for s in range(4):
                            dve.wait_ge(S["S_done"], at(b2, 4, s + 1))
                            dve.tensor_reduce(nmx[:, s, :], group4(bank[:, 4 + s, :])[:, 0:3], AX_X, ALU.max,
                                              negate=True).then_inc(S["head_max"], 1)

                each_turn(dve, turn)


def routing_phase(nc, ins, T, out):
    with ExitStack() as ctx:
        al = Alloc(nc, ctx)
        sb, sem = al.sb, al.sem
        bank, ident, h, half = T["bank"], T["ident"], T["h"], T["half"]
        two = lambda name, shape: [sb(f"{name}{u}", shape) for u in range(2)]
        st6, mv = two("ln5_stats", [P, GB, 6]), two("ln5_mean_var", [P, GB, 2])
        ve, rs = two("ln5_var_eps", [P, GB]), two("ln5_rstd", [P, GB])
        x5 = sb("x5_rows", [P, NB, TAG + D])
        numbers = sb("token_numbers", [P, NB])
        x5s = two("x5_group", [P, GB, D])
        x5T0, x5T1 = two("x5T0_", [P, GB * P]), two("x5T1_", [DR, GB * P])
        rw0, rw1 = sb("router0", [P, NE1]), sb("router1", [DR, NE1])
        lg = sb("router_logits", [P, NB, NE1])
        rank, w, onehot = sb("rank", [P, NE1]), sb("ranked", [P, NB, NE1]), sb("onehot", [P, NB, NE1])
        lmax, first = sb("router_max", [P, NB]), sb("first", [P, NB])
        upto, ones = sb("upto", [P, P]), sb("ones", [P, P])
        pre = [sb(f"before{k}", [P, NB, NE1]) for k in range(2)]
        pos, kept = sb("position", [P, NB]), sb("kept", [P, NB])
        base, to_f, row_f = sb("expert_base", [P, NB]), sb("to_f", [P, NB]), sb("row_of_token", [P, NB])
        to_i = sb("to_i", [P, NB], I32)
        tables, out_stored = sem("tables_in"), sem("out_stored")
        loaded, consts = sem("router_in"), sem("router_constants")
        steps, var, rstd = sem("router_steps"), sem("ln5_var"), sem("ln5_rstd_ready")
        ready, tproduct, took, ttook = sem("x5_ready"), sem("x5T_product"), sem("x5T_act"), sem("x5T_vector")
        lproduct, ltook, kept_rows = sem("router_product"), sem("router_took"), sem("x5_rows_kept")
        chosen, counted, placed, scattered = sem("chosen"), sem("counted"), sem("placed"), sem("scattered")
        exped = sem("router_exp")
        lx, lsum = sb("router_exp_of", [P, NB, NE1]), sb("router_sum", [P, NB])
        bc = lambda t: t[:].unsqueeze(2).broadcast_to([P, NB, NE1])

        def each_group(eng, turn):
            turn(0, 0)
            turn(1, 1)
            with eng.Fori(1, NG // 2) as i:
                for u in range(2):
                    turn(i * 2 + u, u)

        with nc.Block() as block:

            @block.sync
            def _(sp):
                sp.dma_start(rw0[:], ins["router"][0:P]).then_inc(loaded, 16)
                sp.dma_start(rw1[:], ins["router"][P:D]).then_inc(loaded, 16)
                sp.dma_start(rank[:], ins["rank"].partition_broadcast(P)).then_inc(tables, 16)
                sp.dma_start(numbers[:], ins["numbers"]).then_inc(tables, 16)
                sp.dma_start(out.rearrange("(b p) d -> p b d", p=P), h[:]).then_inc(out_stored, 16)
                sp.wait_ge(out_stored, 16)

            @block.gpsimd
            def _(pool):
                pool.memset(upto[:], 1.0).then_inc(consts, 1)
                pool.memset(ones[:], 1.0).then_inc(consts, 1)
                pool.wait_ge(consts, 2)
                pool.affine_select(out=upto[:], in_=upto[:], compare_op=ALU.is_ge, fill=0.0, base=0,
                                   pattern=[[1, P]], channel_multiplier=-1).then_inc(consts, 1)

                def turn(g, u):
                    pool.wait_ge(var, g + 1)
                    pool.tensor_tensor(rs[u][:], ve[u][:], half[:], ALU.pow).then_inc(rstd, 1)

                each_group(pool, turn)
                pool.wait_ge(placed, 1)
                for b in range(NB):
                    pool.indirect_dma_start(
                        out=T["xm"], out_offset=bass.IndirectOffsetOnAxis(ap=to_i[:, b:b + 1], axis=0),
                        in_=x5[:, b, :], in_offset=None, bounds_check=NE1 * CAP - 1, oob_is_err=False,
                    ).then_inc(scattered, 16)
                pool.wait_ge(scattered, 16 * NB)

            @block.vector
            def _(dve):
                def take_x5T1(g, u):
                    dve.wait_ge(tproduct, g * 2 + 2)
                    past(dve, lproduct, g - 1)
                    dve.tensor_copy(x5T1[u][:], bank[0:DR, 2 * u + 1, :]).then_inc(ttook, 1)

                def turn(g, u):
                    st = Steps(dve, steps, g, 2 * GB)
                    for j in range(GB):
                        st.did(dve.bn_stats(st6[u][:, j, :], h[:, ds(g * GB + j, 1), :]))
                    st.wait_apart()
                    for j in range(GB):
                        st.did(dve.bn_aggr(mv[u][:, j, :], st6[u][:, j, :]))
                    st.wait()
                    dve.tensor_scalar(ve[u][:], mv[u][:, :, 1], EPS, None, ALU.add).then_inc(var, 1)
                    if not isinstance(g, int) or g > 0:
                        take_x5T1(g - 1, 1 - u)
                    dve.wait_ge(rstd, g + 1)
                    past(dve, kept_rows, g - 1)
                    for j in range(GB):
                        last = dve.tensor_scalar(x5s[u][:, j, :], h[:, ds(g * GB + j, 1), :], mv[u][:, j, 0:1],
                                                 rs[u][:, j:j + 1], ALU.subtract, ALU.mult)
                    last.then_inc(ready, 1)

                each_group(dve, turn)
                take_x5T1(NG - 1, 1)
                st = Steps(dve, steps, start=2 * GB * NG)
                dve.wait_ge(ltook, NG)
                dve.wait_ge(tables, 32)
                st.link(dve.tensor_reduce(lmax[:], lg[:], AX_X, ALU.max))
                st.link(dve.tensor_tensor(w[:], lg[:], bc(lmax), ALU.is_equal))
                st.link(dve.tensor_tensor(w[:], w[:], rank[:].unsqueeze(1).broadcast_to([P, NB, NE1]), ALU.mult))
                st.link(dve.tensor_reduce(first[:], w[:], AX_X, ALU.max))
                dve.tensor_tensor(onehot[:], w[:], bc(first), ALU.is_equal).then_inc(chosen, 1)
                dve.tensor_tensor(lx[:], lg[:], bc(lmax), ALU.subtract).then_inc(chosen, 1)
                dve.wait_ge(exped, 1)
                st.link(dve.tensor_reduce(lsum[:], lx[:], AX_X, ALU.add))
                st.link(dve.reciprocal(lsum[:], lsum[:]))
                dve.wait_ge(counted, 1)
                tot = bank[:, 1, 0:NB * NE1].rearrange("p (b e) -> p b e", e=NE1)
                cum = bank[:, 0, 0:NB * NE1].rearrange("p (b e) -> p b e", e=NE1)
                st.did(dve.memset(pre[0][:, 0, :], 0.0))
                st.did(dve.tensor_copy(pre[0][:, 1:NB, :], tot[:, 0:NB - 1, :]))
                st.wait()
                a, k = 0, 1
                while k < NB:
                    st.did(dve.tensor_copy(pre[1 - a][:, 0:k, :], pre[a][:, 0:k, :]))
                    st.did(dve.tensor_tensor(pre[1 - a][:, k:NB, :], pre[a][:, k:NB, :], pre[a][:, 0:NB - k, :],
                                             ALU.add))
                    st.wait()
                    a, k = 1 - a, 2 * k
                st.link(dve.tensor_tensor(pre[a][:], pre[a][:], cum, ALU.add))
                st.link(dve.tensor_tensor(pre[a][:], pre[a][:], onehot[:], ALU.mult))
                st.link(dve.tensor_reduce(pos[:], pre[a][:], AX_X, ALU.add))
                st.did(dve.tensor_scalar(kept[:], pos[:], float(CAP), None, ALU.is_lt))
                st.did(dve.tensor_scalar(base[:], first[:], float(NE1), -float(CAP), ALU.subtract, ALU.mult))
                st.wait()
                st.link(dve.tensor_tensor(row_f[:], pos[:], kept[:], ALU.mult))
                st.link(dve.tensor_tensor(row_f[:], row_f[:], base[:], ALU.add))
                dve.tensor_copy(x5[:, :, 0:1], lsum[:].unsqueeze(2))
                dve.tensor_copy(x5[:, :, 1:2], numbers[:].unsqueeze(2))
                st.did(dve.tensor_scalar(to_f[:], kept[:], -1.0, -float(NE1 * CAP), ALU.add, ALU.mult))
                st.wait()
                st.link(dve.tensor_tensor(to_f[:], to_f[:], row_f[:], ALU.add))
                dve.tensor_copy(to_i[:], to_f[:]).then_inc(placed, 1)

            @block.scalar
            def _(act):
                def take_logits(g, u):
                    act.wait_ge(lproduct, g + 1)
                    act.activation(lg[:, ds(g * GB, GB), :],
                                   bank[:, 4 + u, 0:GB * NE1].rearrange("p (j e) -> p j e", e=NE1),
                                   ACT.Copy).then_inc(ltook, 1)

                def turn(g, u):
                    act.wait_ge(tproduct, g * 2 + 1)
                    past(act, lproduct, g - 1)
                    act.activation(x5T0[u][:], bank[:, 2 * u, :], ACT.Copy).then_inc(took, 1)
                    act.wait_ge(tproduct, g * 2 + 2)
                    act.activation(x5[:, ds(g * GB, GB), TAG:], x5s[u][:], ACT.Copy).then_inc(kept_rows, 1)
                    if not isinstance(g, int) or g > 0:
                        take_logits(g - 1, 1 - u)

                each_group(act, turn)
                take_logits(NG - 1, 1)
                act.wait_ge(chosen, 2)
                act.activation(lx[:], lx[:], ACT.Exp).then_inc(exped, 1)

            @block.tensor
            def _(pe):
                pe.wait_ge(loaded, 32)

                def router_logits(g, u):
                    pe.wait_ge(took, g + 1)
                    pe.wait_ge(ttook, g + 1)
                    past(pe, ltook, g - 1)
                    for j in range(GB):
                        js = slice(j * P, (j + 1) * P)
                        last = matmuls(pe, bank[:, 4 + u, j * NE1:(j + 1) * NE1],
                                       [(x5T0[u][:, js], rw0[:]), (x5T1[u][:, js], rw1[:])])
                    last.then_inc(lproduct, 1)

                def turn(g, u):
                    pe.wait_ge(ready, g + 1)
                    for k, rows in ((0, P), (1, DR)):
                        for j in range(GB):
                            last = pe.transpose(bank[0:rows, 2 * u + k, j * P:(j + 1) * P],
                                                x5s[u][:, j, k * P:k * P + rows], ident[:])
                        last.then_inc(tproduct, 1)
                    if not isinstance(g, int) or g > 0:
                        router_logits(g - 1, 1 - u)

                each_group(pe, turn)
                router_logits(NG - 1, 1)
                pe.wait_ge(consts, 3)
                pe.wait_ge(chosen, 1)
                flat = onehot[:].rearrange("p b e -> p (b e)")
                pe.matmul(bank[:, 0, 0:NB * NE1], upto[:], flat, start=True, stop=True)
                pe.matmul(bank[:, 1, 0:NB * NE1], ones[:], flat, start=True, stop=True).then_inc(counted, 1)


def hidden_bias(b):
    return np.ascontiguousarray(b.reshape(b.shape[0], -1, P).transpose(2, 1, 0))


def host_layout(inputs):
    a = {k: np.asarray(v) for k, v in inputs.items()}
    return {
        "ids": np.ascontiguousarray(a["x"].T), "mask": np.ascontiguousarray(a["mask_BS_i1_0"].T),
        "tok": a["L0_tok_tok_w"], "pos": a["L0_tok_pos_w"], "type": a["L0_tok_type_w"],
        "gamma": a["L0_tok_gamma"], "beta": a["L0_tok_beta"],
        "WqT": np.ascontiguousarray(a["L0_attn_Wq"].T), "WkT": np.ascontiguousarray(a["L0_attn_Wk"].T),
        "Wv": a["L0_attn_Wv"],
        "ln_g": np.ascontiguousarray(a["L0_ffn_ln_g"].T), "ln_b": np.ascontiguousarray(a["L0_ffn_ln_b"].T),
        "Wqkv": np.ascontiguousarray(a["L1_attn_w_qkv"].T), "Wproj": np.ascontiguousarray(a["L1_attn_w_proj"].T),
        "bproj": a["L1_attn_b_proj"], "router": a["L1_ffn_router_w"],
        "numbers": np.ascontiguousarray(np.arange(NB * P, dtype=np.float32).reshape(NB, P).T),
        "rank": np.arange(NE1, 0, -1, dtype=np.float32), **rope_tables(),
        "w1_0": a["L0_ffn_w1"], "w2_0": a["L0_ffn_w2"], "b2_0": a["L0_ffn_b2"],
        "b1_0": hidden_bias(a["L0_ffn_b1"]),
        "w1_1": a["L1_ffn_w1"], "w2_1": a["L1_ffn_w2"], "b2_1": a["L1_ffn_b2"],
        "b1_1": hidden_bias(a["L1_ffn_b1"]),
        "phiT": np.ascontiguousarray(a["L0_ffn_phi"].reshape(NS, D).T),
    }


def rope_tables():
    freq = 1.0 / np.float32(10000.0) ** (np.arange(0, HD, 2, dtype=np.float32) / np.float32(HD))
    angle = np.arange(P, dtype=np.float32)[:, None] * freq[None, :].astype(np.float32)
    cos = np.repeat(np.cos(angle), 2, axis=1)
    sin = np.stack([-np.sin(angle), np.sin(angle)], axis=-1).reshape(P, HD)
    q_and_k = lambda t: np.concatenate([np.tile(t, NH) * np.float32(HD ** -0.5), np.tile(t, NH)], axis=1)
    return {"cos": q_and_k(cos).astype(np.float32), "sin": q_and_k(sin).astype(np.float32)}


def kernel(**inputs):
    from concourse import bacc
    from concourse.bass_utils import run_bass_kernel_spmd

    nc = bacc.Bacc("TRN2", target_bir_lowering=False, num_devices=1)
    arrays = host_layout(inputs)
    ins = {n: nc.dram_tensor(f"in_{n}", v.shape, mybir.dt.from_np(v.dtype), kind="ExternalInput").ap()
           for n, v in arrays.items()}
    out = nc.dram_tensor("out", (NB, P, D), F32, kind="ExternalOutput").ap()
    tower_program(nc, ins, out)
    r = run_bass_kernel_spmd(nc, [{f"in_{n}": v for n, v in arrays.items()}], core_ids=[0])
    return r.results[0]["out"]
```
